# Optimizing a Trainium2 kernel written in Bass

```python
import numpy as np
import jax
import jax.numpy as jnp

def _softmax(x, axis=-1):
    return jax.nn.softmax(x, axis=axis)

def _gelu(x):
    return jax.nn.gelu(x, approximate=True)

def _silu(x):
    return jax.nn.silu(x)

def _sigmoid(x):
    return jax.nn.sigmoid(x)

def _layernorm(x, axis=-1, eps=1e-05):
    m = jnp.mean(x, axis=axis, keepdims=True)
    v = jnp.var(x, axis=axis, keepdims=True)
    return (x - m) / jnp.sqrt(v + eps)

def _scatter_add(tgt, idx, src, axis=0):
    return tgt.at[idx].add(src)

def _segment_sum(src, seg, n):
    return jax.ops.segment_sum(src, seg, n)
kernel_name = 'mk_decoder_postln_d1_seqx_r4_af7456'

def setup_inputs(seed: int=0):
    np.random.seed(seed)
    _w = jnp.asarray

    def _rec_inputs():
        import jax
        import jax.numpy as jnp
        _rk = jax.random.key(seed)
        x = 2.818e-05 + 1 * jax.random.normal(jax.random.fold_in(_rk, 1), (4, 512, 512), jnp.float32)
        _lenS = 512 - jax.random.randint(jax.random.fold_in(_rk, 7), (4,), 0, max(1, 512 // 4) + 1, jnp.int32)
        _lenS2 = 512 - jax.random.randint(jax.random.fold_in(_rk, 8), (4,), 0, max(1, 512 // 4) + 1, jnp.int32)
        _ctx_1024P = jax.random.normal(jax.random.fold_in(_rk, 11), (4, 16, 256), jnp.float32)
        _ctx_1024c = jax.random.dirichlet(jax.random.fold_in(_rk, 511), 0.3 * jnp.ones((16,), jnp.float32), (4, 512))
        _ctx_1024t = jnp.einsum('bsk,bkd->bsd', _ctx_1024c, _ctx_1024P)
        _ctx_1024t = _ctx_1024t * jax.lax.rsqrt(jnp.mean(jnp.square(_ctx_1024t)) + 1e-12) * 0.953939
        ctx_1024 = 7.22013e-05 + 1.00017 * (_ctx_1024t + 0.3 * jax.random.normal(jax.random.fold_in(_rk, 611), (4, 512, 256), jnp.float32))
        return (x, ctx_1024)
    x, ctx_1024 = _rec_inputs()

    def _L0_attn_setup():
        import jax, jax.numpy as jnp
        import numpy as np
        import math
        H = 16
        KV = 8
        D = 128
        HID = 512
        LAYER_IDX = 1
        LAMBDA_INIT = 0.8 - 0.6 * math.exp(-0.3 * LAYER_IDX)
        EPS = 1e-05
        key = jax.random.key(seed)
        ks = jax.random.split(key, 8)
        B, S = (2, 512)
        op_size = H * D + 2 * KV * D
        return {'hidden_states': jax.random.normal(ks[0], (B, S, HID), jnp.float32), 'Wqkv_w': jax.random.normal(ks[1], (op_size, HID), jnp.float32) * 0.02, 'Wqkv_b': jnp.zeros((op_size,), jnp.float32), 'lambda_q1': jax.random.normal(ks[2], (D,), jnp.float32) * 0.1, 'lambda_k1': jax.random.normal(ks[3], (D,), jnp.float32) * 0.1, 'lambda_q2': jax.random.normal(ks[4], (D,), jnp.float32) * 0.1, 'lambda_k2': jax.random.normal(ks[5], (D,), jnp.float32) * 0.1, 'subln_w': jnp.ones((2 * D,), jnp.float32), 'out_w': jax.random.normal(ks[6], (HID, H * D), jnp.float32) * 0.02, 'out_b': jnp.zeros((HID,), jnp.float32)}
    _L0_attn_all = _L0_attn_setup()
    _L0_attn_in = {k: v for k, v in _L0_attn_all.items() if k in ('Wqkv_w', 'Wqkv_b', 'lambda_q1', 'lambda_k1', 'lambda_q2', 'lambda_k2', 'subln_w', 'out_w', 'out_b')}
    del _L0_attn_all

    def _L0_xattn_setup():
        import jax, jax.numpy as jnp
        import numpy as np
        B_, L_, D_MODEL = (4, 512, 256)
        D_STATE, D_CONV, EXPAND = (16, 4, 2)
        D_INNER = EXPAND * D_MODEL
        DT_RANK = (D_MODEL + 15) // 16

        def silu(x):
            return x * jax.nn.sigmoid(x)
        key = jax.random.key(seed)
        ks = jax.random.split(key, 10)
        f32 = jnp.float32
        hidden_states = jax.random.normal(ks[0], (B_, L_, D_MODEL), dtype=f32)
        z = jax.random.normal(ks[1], (B_, D_INNER, L_), dtype=f32)
        in_proj_w = jax.random.normal(ks[2], (D_INNER, D_MODEL), dtype=f32) * 0.02
        conv_w = jax.random.normal(ks[3], (D_INNER, 1, D_CONV), dtype=f32) * 0.1
        conv_b = jax.random.normal(ks[4], (D_INNER,), dtype=f32) * 0.02
        x_proj_w = jax.random.normal(ks[5], (DT_RANK + 2 * D_STATE, D_INNER), dtype=f32) * 0.02
        dt_proj_w = jax.random.uniform(ks[6], (D_INNER, DT_RANK), dtype=f32, minval=-DT_RANK ** (-0.5), maxval=DT_RANK ** (-0.5))
        dt = jnp.exp(jax.random.uniform(ks[7], (D_INNER,), dtype=f32, minval=np.log(0.001), maxval=np.log(0.1)))
        dt_proj_b = jnp.log(jnp.expm1(dt))
        A_log = jnp.log(jnp.broadcast_to(jnp.arange(1, D_STATE + 1, dtype=f32), (D_INNER, D_STATE)))
        D = jnp.ones((D_INNER,), f32)
        return {'hidden_states': hidden_states, 'z': z, 'in_proj_w': in_proj_w, 'conv_w': conv_w, 'conv_b': conv_b, 'x_proj_w': x_proj_w, 'dt_proj_w': dt_proj_w, 'dt_proj_b': dt_proj_b, 'A_log': A_log, 'D': D}
    _L0_xattn_all = _L0_xattn_setup()
    _L0_xattn_in = {k: v for k, v in _L0_xattn_all.items() if k in ('in_proj_w', 'conv_w', 'conv_b', 'x_proj_w', 'dt_proj_w', 'dt_proj_b', 'A_log', 'D')}
    del _L0_xattn_all

    def _L0_ffn_setup():
        import jax, jax.numpy as jnp
        import numpy as np
        B, S, EMB = (4, 512, 512)
        LAT, HID = (128, 256)
        E, K = (16, 8)
        SCALE = 2.5

        def _w(key, shape, fan_in):
            return jax.random.normal(key, shape, jnp.float32) * fan_in ** (-0.5)

        def _sqrelu(x):
            return jnp.square(jax.nn.relu(x))
        key = jax.random.key(seed)
        ks = jax.random.split(key, 11)
        return {'x': jax.random.normal(ks[0], (B, S, EMB), jnp.float32), 'sw1': _w(ks[1], (HID, EMB), EMB), 'swg': _w(ks[2], (HID, EMB), EMB), 'sw2': _w(ks[3], (EMB, HID), HID), 'rw1': _w(ks[4], (E, HID, LAT), LAT), 'rwg': _w(ks[5], (E, HID, LAT), LAT), 'rw2': _w(ks[6], (E, LAT, HID), HID), 'Wg': _w(ks[7], (E, EMB), EMB), 'Wdown': _w(ks[8], (LAT, EMB), EMB), 'Wup': _w(ks[9], (EMB, LAT), LAT), 'biases': jnp.zeros((E,), jnp.float32)}
    _L0_ffn_all = _L0_ffn_setup()
    _L0_ffn_in = {k: v for k, v in _L0_ffn_all.items() if k in ('sw1', 'swg', 'sw2', 'rw1', 'rwg', 'rw2', 'Wg', 'Wdown', 'Wup', 'biases')}
    del _L0_ffn_all
    return {'x': x, 'ctx_1024': ctx_1024, 'L0_attn_Wqkv_w': _L0_attn_in['Wqkv_w'], 'L0_attn_Wqkv_b': _L0_attn_in['Wqkv_b'], 'L0_attn_lambda_q1': _L0_attn_in['lambda_q1'], 'L0_attn_lambda_k1': _L0_attn_in['lambda_k1'], 'L0_attn_lambda_q2': _L0_attn_in['lambda_q2'], 'L0_attn_lambda_k2': _L0_attn_in['lambda_k2'], 'L0_attn_subln_w': _L0_attn_in['subln_w'], 'L0_attn_out_w': _L0_attn_in['out_w'], 'L0_attn_out_b': _L0_attn_in['out_b'], 'L0_xattn_in_proj_w': _L0_xattn_in['in_proj_w'], 'L0_xattn_conv_w': _L0_xattn_in['conv_w'], 'L0_xattn_conv_b': _L0_xattn_in['conv_b'], 'L0_xattn_x_proj_w': _L0_xattn_in['x_proj_w'], 'L0_xattn_dt_proj_w': _L0_xattn_in['dt_proj_w'], 'L0_xattn_dt_proj_b': _L0_xattn_in['dt_proj_b'], 'L0_xattn_A_log': _L0_xattn_in['A_log'], 'L0_xattn_D': _L0_xattn_in['D'], 'L0_ffn_sw1': _L0_ffn_in['sw1'], 'L0_ffn_swg': _L0_ffn_in['swg'], 'L0_ffn_sw2': _L0_ffn_in['sw2'], 'L0_ffn_rw1': _L0_ffn_in['rw1'], 'L0_ffn_rwg': _L0_ffn_in['rwg'], 'L0_ffn_rw2': _L0_ffn_in['rw2'], 'L0_ffn_Wg': _L0_ffn_in['Wg'], 'L0_ffn_Wdown': _L0_ffn_in['Wdown'], 'L0_ffn_Wup': _L0_ffn_in['Wup'], 'L0_ffn_biases': _L0_ffn_in['biases']}

def reference(x, ctx_1024, L0_attn_Wqkv_w, L0_attn_Wqkv_b, L0_attn_lambda_q1, L0_attn_lambda_k1, L0_attn_lambda_q2, L0_attn_lambda_k2, L0_attn_subln_w, L0_attn_out_w, L0_attn_out_b, L0_xattn_in_proj_w, L0_xattn_conv_w, L0_xattn_conv_b, L0_xattn_x_proj_w, L0_xattn_dt_proj_w, L0_xattn_dt_proj_b, L0_xattn_A_log, L0_xattn_D, L0_ffn_sw1, L0_ffn_swg, L0_ffn_sw2, L0_ffn_rw1, L0_ffn_rwg, L0_ffn_rw2, L0_ffn_Wg, L0_ffn_Wdown, L0_ffn_Wup, L0_ffn_biases):
    import jax
    import jax.numpy as jnp

    def _L0_attn_ref(hidden_states, Wqkv_w, Wqkv_b, lambda_q1, lambda_k1, lambda_q2, lambda_k2, subln_w, out_w, out_b):
        import jax, jax.numpy as jnp
        import numpy as np
        import math
        H = 16
        KV = 8
        D = 128
        HID = 512
        LAYER_IDX = 1
        LAMBDA_INIT = 0.8 - 0.6 * math.exp(-0.3 * LAYER_IDX)
        EPS = 1e-05
        B, S, _ = hidden_states.shape
        qkv = hidden_states @ Wqkv_w.T + Wqkv_b
        q, k, v = jnp.split(qkv, [H * D, H * D + KV * D], axis=-1)
        q = q.reshape(B, S, H // 2, 2, D)
        k = k.reshape(B, S, KV // 2, 2, D)
        v = v.reshape(B, S, KV // 2, 2 * D)
        rep = H // KV
        k = jnp.repeat(k, rep, axis=2)
        v = jnp.repeat(v, rep, axis=2)
        scale = D ** (-0.5)
        causal = jnp.tril(jnp.ones((S, S), bool))
        neg = jnp.finfo(jnp.float32).min

        def attn_map(qi, ki):
            s = jnp.einsum('bqhd,bkhd->bhqk', qi, ki) * scale
            s = jnp.where(causal, s, neg)
            return jax.nn.softmax(s, axis=-1)
        p1 = attn_map(q[:, :, :, 0], k[:, :, :, 0])
        p2 = attn_map(q[:, :, :, 1], k[:, :, :, 1])
        lam1 = jnp.exp(jnp.sum(lambda_q1 * lambda_k1))
        lam2 = jnp.exp(jnp.sum(lambda_q2 * lambda_k2))
        lam = lam1 - lam2 + LAMBDA_INIT
        p = p1 - lam * p2
        o = jnp.einsum('bhqk,bkhe->bqhe', p, v)
        rms = jax.lax.rsqrt(jnp.mean(o * o, axis=-1, keepdims=True) + EPS)
        o = o * rms * subln_w
        o = o * (1.0 - LAMBDA_INIT)
        o = o.reshape(B, S, H * D)
        return o @ out_w.T + out_b

    def _L0_xattn_ref(hidden_states, z, in_proj_w, conv_w, conv_b, x_proj_w, dt_proj_w, dt_proj_b, A_log, D):
        import jax, jax.numpy as jnp
        import numpy as np
        B_, L_, D_MODEL = (4, 512, 256)
        D_STATE, D_CONV, EXPAND = (16, 4, 2)
        D_INNER = EXPAND * D_MODEL
        DT_RANK = (D_MODEL + 15) // 16

        def silu(x):
            return x * jax.nn.sigmoid(x)
        Bsz, L, _ = hidden_states.shape
        d_inner, _, d_conv = conv_w.shape
        dt_rank = dt_proj_w.shape[1]
        d_state = A_log.shape[1]
        x = jnp.einsum('bld,ed->bel', hidden_states, in_proj_w)
        xc = jax.lax.conv_general_dilated(x, conv_w, window_strides=(1,), padding=[(d_conv - 1, 0)], feature_group_count=d_inner, dimension_numbers=('NCH', 'OIH', 'NCH'))
        x = silu(xc + conv_b[None, :, None])
        x_dbl = jnp.einsum('bdl,ed->bel', x, x_proj_w)
        dt_low, Bm, Cm = jnp.split(x_dbl, [dt_rank, dt_rank + d_state], axis=1)
        dt = jnp.einsum('brl,dr->bdl', dt_low, dt_proj_w)
        dt = jax.nn.softplus(dt + dt_proj_b[None, :, None])
        A = -jnp.exp(A_log)
        dt_t = jnp.moveaxis(dt, -1, 0)
        B_t = jnp.moveaxis(Bm, -1, 0)
        C_t = jnp.moveaxis(Cm, -1, 0)
        u_t = jnp.moveaxis(x, -1, 0)

        def step(state, inp):
            d, b, c, u = inp
            dA = jnp.exp(d[..., None] * A)
            state = state * dA + (d * u)[..., None] * b[:, None, :]
            y = jnp.einsum('bdn,bn->bd', state, c)
            return (state, y)
        state0 = jnp.zeros((Bsz, d_inner, d_state), x.dtype)
        _, ys = jax.lax.scan(step, state0, (dt_t, B_t, C_t, u_t))
        y = jnp.moveaxis(ys, 0, 2)
        y = y + D[None, :, None] * x
        y = y * silu(z)
        return jnp.swapaxes(y, 1, 2)

    def _L0_ffn_ref(x, sw1, swg, sw2, rw1, rwg, rw2, Wg, Wdown, Wup, biases):
        import jax, jax.numpy as jnp
        import numpy as np
        B, S, EMB = (4, 512, 512)
        LAT, HID = (128, 256)
        E, K = (16, 8)
        SCALE = 2.5

        def _w(key, shape, fan_in):
            return jax.random.normal(key, shape, jnp.float32) * fan_in ** (-0.5)

        def _sqrelu(x):
            return jnp.square(jax.nn.relu(x))
        b, s, d = x.shape
        x2 = x.reshape(-1, d)
        shared = x2 @ sw1.T * _sqrelu(x2 @ swg.T) @ sw2.T
        xl = x2 @ Wdown.T
        probas = jax.nn.sigmoid(x2 @ Wg.T)
        _, idx = jax.lax.top_k(probas + biases, K)
        p = jnp.take_along_axis(probas, idx, axis=-1)
        p = p / p.sum(-1, keepdims=True) * SCALE
        T = x2.shape[0]
        w_dense = jnp.zeros((T, E), x2.dtype).at[jnp.arange(T)[:, None], idx].add(p)
        acc = jnp.zeros_like(xl)
        for e in range(E):
            ye = xl @ rw1[e].T * _sqrelu(xl @ rwg[e].T) @ rw2[e].T
            acc = acc + w_dense[:, e:e + 1] * ye
        out = shared + acc @ Wup.T
        return out.reshape(b, s, d)
    x = _layernorm(x + _L0_attn_ref(x, L0_attn_Wqkv_w, L0_attn_Wqkv_b, L0_attn_lambda_q1, L0_attn_lambda_k1, L0_attn_lambda_q2, L0_attn_lambda_k2, L0_attn_subln_w, L0_attn_out_w, L0_attn_out_b), axis=-1)
    x = _layernorm(x + _L0_xattn_ref(ctx_1024, x, L0_xattn_in_proj_w, L0_xattn_conv_w, L0_xattn_conv_b, L0_xattn_x_proj_w, L0_xattn_dt_proj_w, L0_xattn_dt_proj_b, L0_xattn_A_log, L0_xattn_D), axis=-1)
    x = _layernorm(x + _L0_ffn_ref(x, L0_ffn_sw1, L0_ffn_swg, L0_ffn_sw2, L0_ffn_rw1, L0_ffn_rwg, L0_ffn_rw2, L0_ffn_Wg, L0_ffn_Wdown, L0_ffn_Wup, L0_ffn_biases), axis=-1)
    return x

_drawn_inputs = setup_inputs


def setup_inputs(seed=0):
    import zlib

    import numpy as np

    out = dict(_drawn_inputs(seed))
    spreads = {'L0_attn_Wqkv_b': (0.0, 0.1),
     'L0_attn_subln_w': (1.0, 0.2),
     'L0_attn_out_b': (0.0, 0.1),
     'L0_xattn_D': (1.0, 0.6),
     'L0_ffn_biases': (0.0, 0.1)}
    factors = {'L0_attn_lambda_q2': 3.225,
     'L0_xattn_x_proj_w': 8.0,
     'L0_xattn_dt_proj_w': 8.0,
     'L0_xattn_dt_proj_b': 8.0,
     'L0_xattn_A_log': 8.0}
    for name, (base, spread) in spreads.items():
        noise = np.random.default_rng([zlib.crc32(name.encode()), seed]).standard_normal(out[name].shape)
        drawn = base * np.exp(spread * noise) if base else spread * noise
        out[name] = jnp.asarray(drawn.astype(out[name].dtype))
    for name, factor in factors.items():
        out[name] = (out[name] * factor).astype(out[name].dtype)
    return out
```

```python
import math
from contextlib import ExitStack

import concourse.bass as bass
from concourse import mybir

F32 = mybir.dt.float32
F32R = mybir.dt.float32r
BF16 = mybir.dt.bfloat16
ALU = mybir.AluOpType
ACT = mybir.ActivationFunctionType
AX = mybir.AxisListType

P = 128
B, T, HID = 4, 512, 512
KT = HID // P
TT = T // P
G = 4
HD = 128
E2 = 2 * HD
QC, KC, VC = 4 * HD, 2 * HD, E2
GC = QC + KC + VC
LAMBDA_INIT = 0.8 - 0.6 * math.exp(-0.3)
SCALE = HD ** -0.5
EPS = 1e-5
NEG = -1e30
CT = 4
NS = 16
RANK = 16
TAPS = 4
CTX = 256
NE = 16
LAT = 128
TOPK = 8
ROUTE_SCALE = 2.5
ATANH = (2.0000000078777487, 0.6666631593508026, 0.40024853723499904,
         0.27961418834331303, 0.2817465726538725)

SW1 = 0
SWG = SW1 + KT * 256
SW2 = SWG + KT * 256
WDN = SW2 + 2 * HID
WUP = WDN + KT * LAT
WGT = WUP + HID
RW1 = WGT + KT * NE
RWG = RW1 + NE * 256
RW2 = RWG + NE * 256
WCOLS = RW2 + NE * 2 * LAT


def rsqrt_newton(dve, step, y, v, tmp):
    step(dve.scalar_tensor_tensor(tmp, y, -0.5, y, ALU.mult, ALU.mult))
    step(dve.tensor_tensor(tmp, tmp, v, ALU.mult))
    step(dve.scalar_tensor_tensor(y, tmp, 1.5, y, ALU.add, ALU.mult))


def chained(engine, sem):
    count = [0]

    def step(ins):
        count[0] += 1
        ins.then_inc(sem, 1)
        engine.wait_ge(sem, count[0])

    return step


def clear(nc, sems):
    nums = [s.num for s in sems]
    assert nums == list(range(nums[0], nums[0] + len(nums)))
    nc.vector.sem_clear(range(nums[0], nums[-1] + 1))
    nc.all_engine_barrier(sem_only=True)


def setup(nc, d, s):
    with ExitStack() as ctx:
        def sb(name, shape, dt=F32):
            return ctx.enter_context(nc.sbuf_tensor(name, shape, dt))

        lams = sb("lams", [P, 4, P])
        prod = sb("lam_prod", [P, 2, P])
        lsum = sb("lam_sum", [P, 2])
        lexp = sb("lam_exp", [P, 2])
        alog = sb("alog", [P, CT * NS])
        sems = [ctx.enter_context(nc.semaphore(n)) for n in
                ("loaded", "cleared", "const_done", "lam_step", "act_step", "copied")]
        loaded, cleared, const_done, lam_step, act_step, copied = sems
        with nc.Block() as block:
            @block.sync
            def _(sp):
                for n in range(4):
                    sp.dma_start(lams[:, n, :], d["lam"][n:n + 1, :].broadcast_to([P, P])).then_inc(loaded, 16)
                sp.dma_start(alog[:, :], d["alog"]).then_inc(loaded, 16)
                sp.dma_start(d["acc"], d["x"]).then_inc(copied, 16)
                sp.wait_ge(copied, 16)

            @block.gpsimd
            def _(pool):
                nc.gpsimd.memset(s["ident"][:, :], 0.0).then_inc(cleared, 1)
                nc.gpsimd.memset(s["identb"][:, :], 0.0).then_inc(cleared, 1)
                nc.gpsimd.memset(s["maskb"][:, :], 0.0).then_inc(cleared, 1)
                pool.wait_ge(cleared, 3)
                for m in ("ident", "identb"):
                    nc.gpsimd.affine_select(out=s[m][:, :], in_=s[m][:, :], compare_op=ALU.not_equal, fill=1.0,
                                            base=0, pattern=[[-1, P]], channel_multiplier=1).then_inc(const_done, 1)
                nc.gpsimd.affine_select(out=s["maskb"][:, :], in_=s["maskb"][:, :], compare_op=ALU.is_ge, fill=NEG,
                                        base=0, pattern=[[-1, P]], channel_multiplier=1).then_inc(const_done, 1)
                nc.gpsimd.memset(s["ones"][:, :], 1.0).then_inc(const_done, 1)
                nc.gpsimd.memset(s["two"][:, :], 2.0).then_inc(const_done, 1)
                pool.wait_ge(const_done, 5)

            @block.vector
            def _(dve):
                step = chained(dve, lam_step)
                dve.wait_ge(loaded, 80)
                for n in range(2):
                    step(nc.vector.tensor_tensor(prod[:, n, :], lams[:, 2 * n, :], lams[:, 2 * n + 1, :], ALU.mult))
                step(nc.vector.reduce_sum(lsum[:, :], prod[:, :, :], AX.X))
                dve.wait_ge(act_step, 2)
                step(nc.vector.tensor_tensor(s["neglam"][:, :], lexp[:, 1:2], lexp[:, 0:1], ALU.subtract))
                step(nc.vector.tensor_scalar(s["neglam"][:, :], s["neglam"][:, :], -LAMBDA_INIT, None, ALU.add))
                step(nc.vector.tensor_scalar(s["negA"][:, :], s["negA"][:, :], -1.0, None, ALU.mult))

            @block.scalar
            def _(act):
                act.wait_ge(loaded, 80)
                nc.scalar.activation(s["negA"][:, :], alog[:, :], ACT.Exp).then_inc(act_step, 1)
                act.wait_ge(lam_step, 3)
                nc.scalar.activation(lexp[:, :], lsum[:, :], ACT.Exp).then_inc(act_step, 1)


def scan_inputs(nc, d, s):
    with ExitStack() as ctx:
        def sb(name, shape, dt=F32):
            return ctx.enter_context(nc.sbuf_tensor(name, shape, dt))

        win = sb("win", [P, 2, CT * P])
        wxp = sb("wxp", [P, CT, RANK + 2 * NS])
        wdt = sb("wdt", [RANK, CT * P])
        cols = sb("scan_cols", [P, CT, TAPS + 2])
        ctxT = sb("ctxT", [P, 2, T])
        xpad = sb("xpad", [P, CT, TAPS - 1 + T])
        conv = sb("conv", [P, CT, T])
        e = sb("fe", [P, CT, T])
        u = sb("u", [P, CT, T])
        z = sb("fz", [P, CT, T])
        z2 = sb("fz2", [P, CT, T])
        q = sb("fq", [P, CT, T])
        v = sb("fv", [P, CT, T])
        xdbl = sb("xdbl", [RANK + 2 * NS, T])
        psX = ctx.enter_context(nc.psum_tensor("psX", [P, CT, T], F32))
        psD = ctx.enter_context(nc.psum_tensor("psD", [RANK + 2 * NS, T], F32))
        w_loaded = ctx.enter_context(nc.semaphore("w_loaded"))
        pad_zero = ctx.enter_context(nc.semaphore("pad_zero"))
        halved = ctx.enter_context(nc.semaphore("halved"))
        sems = [ctx.enter_context(nc.semaphore(n)) for n in
                ("ctx_loaded", "inproj_done", "pad_done", "conv_done", "exp_done", "u_done", "xdbl_ps",
                 "xdbl_sb", "dt_ps", "v_done", "abs_done", "exp2_done", "step", "dt_done", "stored")]
        (ctx_loaded, inproj_done, pad_done, conv_done, exp_done, u_done, xdbl_ps, xdbl_sb, dt_ps, v_done, abs_done,
         exp2_done, step_sem, dt_done, stored) = sems
        with nc.Block() as block:
            @block.sync
            def _(sp):
                sp.dma_start(win[:, :, :], d["inT"].rearrange("(k p) n -> p k n", p=P)).then_inc(w_loaded, 16)
                sp.dma_start(wxp[:, :, :], d["xpT"].rearrange("(k p) n -> p k n", p=P)).then_inc(w_loaded, 16)
                sp.dma_start(wdt[:, :], d["dtT"]).then_inc(w_loaded, 16)
                sp.dma_start(cols[:, :, :], d["scan_cols"]).then_inc(w_loaded, 16)
                sp.wait_ge(w_loaded, 64)

            @block.gpsimd
            def _(pool):
                nc.gpsimd.memset(xpad[:, :, 0:TAPS - 1], 0.0).then_inc(pad_zero, 1)
                pool.wait_ge(pad_zero, 1)

            @block.vector
            def _(dve):
                dve.wait_ge(w_loaded, 64)
                nc.vector.tensor_scalar(cols[:, :, 0:TAPS + 1], cols[:, :, 0:TAPS + 1], 0.5, None, ALU.mult) \
                    .then_inc(halved, 1)
        with nc.Fori(0, B) as b:
            with nc.Block(no_gpsimd_drain=True) as block:
                @block.sync
                def _(sp):
                    sp.dma_start(ctxT[:, :, :],
                                 d["ctxT"][bass.ds(b, 1), :, :, :].rearrange("b k p t -> p (b k) t")).then_inc(ctx_loaded, 16)
                    sp.wait_ge(u_done, 1)
                    sp.dma_start(d["u"][bass.ds(b, 1), :, :].rearrange("b p n -> p (b n)"),
                                 u[:, :, :].rearrange("p c t -> p (c t)")).then_inc(stored, 16)
                    sp.wait_ge(xdbl_sb, 1)
                    sp.dma_start(d["bc"][bass.ds(b, 1), :, :].rearrange("b p n -> p (b n)"),
                                 xdbl[RANK:, :]).then_inc(stored, 16)
                    sp.wait_ge(dt_done, 1)
                    sp.dma_start(d["dt"][bass.ds(b, 1), :, :].rearrange("b p n -> p (b n)"),
                                 q[:, :, :].rearrange("p c t -> p (c t)")).then_inc(stored, 16)
                    sp.wait_ge(dt_done, 2)
                    sp.dma_start(d["dtu"][bass.ds(b, 1), :, :].rearrange("b p n -> p (b n)"),
                                 z[:, :, :].rearrange("p c t -> p (c t)")).then_inc(stored, 16)
                    sp.wait_ge(stored, 64)

                @block.tensor
                def _(pe):
                    pe.wait_ge(ctx_loaded, 16)
                    for c in range(CT):
                        for k in range(2):
                            mm = nc.tensor.matmul(psX[:, c, :], win[:, k, c * P:(c + 1) * P], ctxT[:, k, :],
                                                  start=k == 0, stop=k == 1)
                        mm.then_inc(inproj_done, 1)
                    pe.wait_ge(u_done, 1)
                    for c in range(CT):
                        mm = nc.tensor.matmul(psD[:, :], wxp[:, c, :], u[:, c, :], start=c == 0, stop=c == CT - 1)
                    mm.then_inc(xdbl_ps, 1)
                    pe.wait_ge(xdbl_sb, 1)
                    for c in range(CT):
                        mm = nc.tensor.matmul(psX[:, c, :], wdt[:, c * P:(c + 1) * P], xdbl[0:RANK, :],
                                              start=True, stop=True)
                        mm.then_inc(dt_ps, 1)

                @block.scalar
                def _(act):
                    for c in range(CT):
                        act.wait_ge(inproj_done, c + 1)
                        nc.scalar.copy(xpad[:, c, TAPS - 1:], psX[:, c, :]).then_inc(pad_done, 1)
                    for c in range(CT):
                        act.wait_ge(conv_done, c + 1)
                        nc.scalar.activation(e[:, c, :], conv[:, c, :], ACT.Tanh).then_inc(exp_done, 1)
                    act.wait_ge(xdbl_ps, 1)
                    nc.scalar.copy(xdbl[:, :], psD[:, :]).then_inc(xdbl_sb, 1)
                    for c in range(CT):
                        act.wait_ge(dt_ps, c + 1)
                        nc.scalar.activation(v[:, c, :], psX[:, c, :], ACT.Identity,
                                             bias=cols[:, c, TAPS + 1:TAPS + 2]).then_inc(v_done, 1)
                    act.wait_ge(v_done, CT)
                    nc.scalar.activation(z[:, :, :], v[:, :, :], ACT.Abs).then_inc(abs_done, 1)
                    act.wait_ge(abs_done, 1)
                    act.wait_ge(u_done, 1)
                    nc.scalar.activation(e[:, :, :], z[:, :, :], ACT.Exp, scale=-1.0).then_inc(exp2_done, 1)
                    act.wait_ge(exp2_done, 1)
                    nc.scalar.activation(z2[:, :, :], e[:, :, :], ACT.Ln, bias=s["two"][:, :]).then_inc(exp2_done, 1)
                    act.wait_ge(exp2_done, 2)
                    nc.scalar.activation(q[:, :, :], z2[:, :, :], ACT.Exp, scale=-1.0).then_inc(exp2_done, 1)

                @block.vector
                def _(dve):
                    step = chained(dve, step_sem)
                    for c in range(CT):
                        dve.wait_ge(pad_done, c + 1)
                        step(nc.vector.tensor_scalar(conv[:, c, :], xpad[:, c, 0:T], cols[:, c, 0:1],
                                                     cols[:, c, TAPS:TAPS + 1], ALU.mult, ALU.add))
                        for j in range(1, TAPS):
                            ins = nc.vector.scalar_tensor_tensor(conv[:, c, :], xpad[:, c, j:j + T],
                                                                 cols[:, c, j:j + 1], conv[:, c, :], ALU.mult, ALU.add)
                            if j < TAPS - 1:
                                step(ins)
                        ins.then_inc(conv_done, 1)
                    dve.wait_ge(exp_done, CT)
                    dve.wait_ge(conv_done, CT)
                    nc.vector.scalar_tensor_tensor(u[:, :, :], e[:, :, :], 1.0, conv[:, :, :], ALU.add, ALU.mult) \
                        .then_inc(u_done, 1)
                    dve.wait_ge(exp2_done, 3)
                    step(nc.vector.scalar_tensor_tensor(z2[:, :, :], e[:, :, :], 2.0, q[:, :, :], ALU.add, ALU.mult))
                    step(nc.vector.scalar_tensor_tensor(z2[:, :, :], z2[:, :, :], 2.0, q[:, :, :],
                                                        ALU.subtract, ALU.mult))
                    step(nc.vector.scalar_tensor_tensor(z[:, :, :], z2[:, :, :], -1.0, e[:, :, :], ALU.mult, ALU.mult))
                    step(nc.vector.tensor_tensor(z2[:, :, :], z[:, :, :], z[:, :, :], ALU.mult))
                    step(nc.vector.tensor_scalar(q[:, :, :], z2[:, :, :], ATANH[4], None, ALU.mult))
                    for n in (3, 2, 1):
                        step(nc.vector.scalar_tensor_tensor(q[:, :, :], q[:, :, :], ATANH[n], z2[:, :, :],
                                                            ALU.add, ALU.mult))
                    step(nc.vector.scalar_tensor_tensor(q[:, :, :], q[:, :, :], ATANH[0], z[:, :, :],
                                                        ALU.add, ALU.mult))
                    nc.vector.scalar_tensor_tensor(q[:, :, :], v[:, :, :], 0.0, q[:, :, :], ALU.max, ALU.add) \
                        .then_inc(dt_done, 1)
                    dve.wait_ge(dt_done, 1)
                    nc.vector.tensor_tensor(z[:, :, :], q[:, :, :], u[:, :, :], ALU.mult).then_inc(dt_done, 1)
            clear(nc, sems)



def attention_order():
    order = []
    for j in range(B + 1):
        last = j == B
        slots = [[("K", j, 0)], [("Q", j, 0)], [("Q", j, 1)], [("V", j, 0)]] + [[("S", j, u)] for u in range(8)]
        if last:
            slots = [[] for _ in range(5)]
        if j > 0:
            slots[0] += [("R", j - 1, 2), ("T", j - 1, 7), ("OUT", j - 1, 1)]
            slots[1] += [("OT", j - 1, 2), ("PV", j - 1, 3)]
            slots[2] += [("R", j - 1, 3), ("OUT", j - 1, 2)]
            slots[3] += [("OT", j - 1, 3)]
            slots[4] += [("OUT", j - 1, 3)]
        if not last:
            for u in range(1, 8):
                slots[4 + u] += [("T", j, u - 1)]
            for qt in range(3):
                slots[4 + 2 * qt + 3] += [("PV", j, qt)]
            for qt in range(2):
                slots[4 + 2 * qt + 4].insert(1, ("R", j, qt))
                slots[4 + 2 * qt + 5].insert(2, ("OT", j, qt))
            slots[4 + 6] += [("OUT", j, 0)]
            for u in range(8):
                slots[4 + u] += [("C", j, u)]
            if j < B - 1:
                slots[4 + 3] += [("X", j + 1, 0)]
                slots[4 + 5] += [("X", j + 1, 1)]
            for n, slot in enumerate((0, 1, 2, 3, 5, 7, 8, 10)):
                slots[slot] += [("M", j, n)]
        for slot in slots:
            order += slot
    return order


def attend_and_scan(nc, d, s):
    order = attention_order()
    with ExitStack() as ctx:
        def sb(name, shape, dt=F32):
            return ctx.enter_context(nc.sbuf_tensor(name, shape, dt))

        def pair(name, shape):
            return sb(name + "_hi", shape, F32R), sb(name + "_lo", shape, F32R)

        def ps(name, shape):
            return ctx.enter_context(nc.psum_tensor(name, shape, F32))

        wraw = sb("wraw", [P, KT, GC])
        w = pair("w", [P, KT, GC])
        ow = pair("ow", [P, 4, HID])
        bias = sb("qk_bias", [P, 6])
        vbias = sb("v_bias", [1, VC])
        subln = sb("subln", [P, 2])
        xraw = sb("xraw", [P, KT, T])
        x = pair("x", [P, KT, T])
        qT = pair("qT", [P, 4, T])
        kT = pair("kT", [P, 2, T])
        v = pair("v", [P, TT, E2])
        prob = sb("prob", [P, 2, 2, T])
        pT = pair("pT", [P, 2, TT, P])
        junk = sb("junk", [P, E2])
        head = sb("head", [P, 2, E2])
        hT = pair("hT", [P, 4, P])
        acc = sb("acc_sb", [P, 2, HID])
        mx = sb("mx", [P, 2, 2])
        nb = sb("nb", [P, 2, 2])
        rowsum = sb("rowsum", [P, 2, 2])
        rinv = sb("rinv", [P, 2, 2])
        coef = sb("coef", [P, 2])
        r1 = sb("r1", [P, 2, 2])
        msq = sb("msq", [P, 2, 2])
        var = sb("var", [P, 2, 2])
        rms = sb("rms", [P, 2, 2])
        tmp = sb("rms_tmp", [P, 2])
        dt = sb("dt_sb", [P, CT, T])
        dtu = sb("dtu_sb", [P, CT, T])
        y = sb("y_sb", [P, CT, T])
        Bn = sb("Bn", [P, 2, T])
        Cn = sb("Cn", [P, 2, T])
        dA = sb("dA", [P, 2, 2, T])
        st = sb("state", [P, 3, 2, T])

        psBig = ps("psBig", [P, 2, 2, T])
        psT = ps("psT", [P, TT, P])
        psPV = ps("psPV", [P, 2, E2])
        psOT = ps("psOT", [P, 4, P])
        psOUT = ps("psOUT", [P, HID])

        zeroed = ctx.enter_context(nc.semaphore("dA_zeroed"))
        names = ("w_loaded", "b_loaded", "ow_loaded", "x_loaded", "acc_loaded0", "acc_loaded1", "acc_stored0", "acc_stored1", "w_hi", "w_lo", "ow_hi",
                 "ow_lo", "ow_col", "x_hi", "x_lo", "proj_done", "proj_hi", "proj_lo", "scores_done", "max_done",
                 "max_step", "exp_done", "probs_done", "comb_step", "pt_done", "pt_hi", "pt_lo", "pv_done", "sq_done",
                 "var_done", "var_step", "ln_done", "guess_done", "rms_step", "head_done", "ot_done", "ot_hi",
                 "ot_lo", "out_done", "acc_done", "scan_loaded", "bc_loaded0", "bc_loaded1", "dA_done", "dbu_done", "scan_done",
                 "gated", "piece_done", "y_init", "y_stored")
        sems = [ctx.enter_context(nc.semaphore(n)) for n in names]
        S = dict(zip(names, sems))

        with nc.Block() as block:
            @block.gpsimd
            def _(pool):
                nc.gpsimd.memset(dA[:, :, :, 0:1], 0.0).then_inc(zeroed, 1)
                pool.wait_ge(zeroed, 1)

        with nc.Fori(0, G) as g:
            with nc.Block(no_gpsimd_drain=True) as block:

                def wait_big_free(eng, w_):
                    if w_ >= 2:
                        j, r = divmod(w_ - 2, 12)
                        if r < 4:
                            eng.wait_ge(S["proj_hi"], 4 * j + r + 1)
                            eng.wait_ge(S["proj_lo"], 4 * j + r + 1)
                        else:
                            eng.wait_ge(S["exp_done"], 8 * j + r - 4 + 1)

                def use_of(kind, n):
                    return {"K": 0, "Q": 1 + n, "V": 3, "S": 4 + n}[kind]

                @block.sync
                def _(sp):
                    sp.dma_start(wraw[:, :, :], d["w"][bass.ds(g, 1), :, :].rearrange("g p n -> p (g n)")
                                 .rearrange("p (k n) -> p k n", k=KT)).then_inc(S["w_loaded"], 16)
                    sp.dma_start(xraw[:, :, :], d["xT"][0].rearrange("k p t -> p k t")).then_inc(S["x_loaded"], 16)
                    sp.dma_start(bias[:, :], d["qk_bias"][bass.ds(g, 1), :, :].rearrange("g p n -> p (g n)")) \
                        .then_inc(S["b_loaded"], 16)
                    sp.dma_start(vbias[:, :], d["v_bias"][bass.ds(g, 1), :]).then_inc(S["b_loaded"], 16)
                    sp.dma_start(subln[:, :], d["subln"]).then_inc(S["b_loaded"], 16)
                    for buf, src in ((dt, "dt"), (dtu, "dtu"), (y, "u")):
                        sp.dma_start(buf[:, :, :].rearrange("p c t -> p (c t)"),
                                     d[src][bass.ds(g, 1), :, :].rearrange("b p n -> p (b n)")).then_inc(S["scan_loaded"], 16)

                    def load_bc(n):
                        if n >= 2:
                            sp.wait_ge(S["piece_done"], 2 * (n - 2) + 2)
                        for buf, row in ((Bn, n), (Cn, NS + n)):
                            sp.dma_start(buf[:, n % 2, :], d["bc"][bass.ds(g, 1), row:row + 1, :]
                                         .rearrange("b n t -> (b n) t").broadcast_to([P, T])).then_inc(S[f"bc_loaded{n % 2}"], 16)

                    def load_acc(n):
                        if n >= 2:
                            sp.wait_ge(S[f"acc_stored{n % 2}"], 16 * (n // 2))
                        sp.dma_start(acc[:, n % 2, :], d["acc"][n * P:(n + 1) * P, :]).then_inc(S[f"acc_loaded{n % 2}"], 16)

                    load_bc(0)
                    load_bc(1)
                    load_acc(0)
                    load_acc(1)
                    sp.wait_ge(S["w_hi"], KT)
                    sp.wait_ge(S["w_lo"], KT)
                    sp.dma_start(wraw[:, :, 0:HID], d["ow"][bass.ds(g, 1), :, :].rearrange("g p n -> p (g n)")
                                 .rearrange("p (k n) -> p k n", k=4)).then_inc(S["ow_loaded"], 16)
                    for kind, j, n in order:
                        if kind == "M":
                            k = 8 * j + n
                            if k % 2 == 0 and k >= 4 and k // 2 < NS:
                                load_bc(k // 2)
                        elif kind == "X" and n == 0:
                            pass
                        elif kind == "V" and j < B - 1:
                            sp.wait_ge(S["x_hi"], 2 * (j + 1))
                            sp.wait_ge(S["x_lo"], 2 * (j + 1))
                            sp.dma_start(xraw[:, :, :], d["xT"][j + 1].rearrange("k p t -> p k t")) \
                                .then_inc(S["x_loaded"], 16)
                        elif kind == "OUT":
                            m = 4 * j + n
                            sp.wait_ge(S["acc_done"], m + 1)
                            sp.dma_start(d["acc"][m * P:(m + 1) * P, :], acc[:, m % 2, :]).then_inc(S[f"acc_stored{m % 2}"], 16)
                            if m + 2 < 4 * B:
                                load_acc(m + 2)
                    sp.wait_ge(S["piece_done"], 2 * NS)
                    sp.dma_start(d["y"][bass.ds(g, 1), :, :].rearrange("b p n -> p (b n)"),
                                 y[:, :, :].rearrange("p c t -> p (c t)")).then_inc(S["y_stored"], 16)
                    sp.wait_ge(S["acc_stored0"], 16 * 2 * B)
                    sp.wait_ge(S["acc_stored1"], 16 * 2 * B)
                    sp.wait_ge(S["y_stored"], 16)

                @block.tensor
                def _(pe):
                    def three(out, lhs, rhs, at_l, at_r, start, stop):
                        nc.tensor.matmul(out, at_l(lhs[0]), at_r(rhs[0]), start=start, stop=False)
                        nc.tensor.matmul(out, at_l(lhs[0]), at_r(rhs[1]), start=False, stop=False)
                        return nc.tensor.matmul(out, at_l(lhs[1]), at_r(rhs[0]), start=False, stop=stop)

                    for kind, j, n in order:
                        if kind in ("K", "Q", "V"):
                            r = use_of(kind, n)
                            wait_big_free(pe, 12 * j + r)
                            if kind == "K":
                                pe.wait_ge(S["x_hi"], 2 * (j + 1))
                                pe.wait_ge(S["x_lo"], 2 * (j + 1))
                            if kind == "K" and j == 0:
                                pe.wait_ge(S["w_hi"], KT)
                                pe.wait_ge(S["w_lo"], KT)
                                pe.wait_ge(S["b_loaded"], 48)
                            big = psBig[:, r % 2]
                            if kind == "V":
                                vps = big.rearrange("p a (b n) -> p (a b) n", b=2)
                                for t in range(TT):
                                    for k in range(KT):
                                        three(vps[:, t, :], x, w, lambda a: a[:, k, t * P:(t + 1) * P],
                                              lambda a: a[:, k, QC + KC:GC], k == 0, False)
                                    mm = nc.tensor.matmul(vps[:, t, :], s["ones"][0:1, :], vbias[:, :],
                                                          start=False, stop=True)
                            else:
                                c0 = QC if kind == "K" else 2 * n * HD
                                for m in range(2):
                                    for k in range(KT):
                                        mm = three(big[:, m, :], w, x,
                                                   lambda a: a[:, k, c0 + m * HD:c0 + (m + 1) * HD],
                                                   lambda a: a[:, k, :], k == 0, k == KT - 1)
                            mm.then_inc(S["proj_done"], 1)
                        elif kind == "S":
                            qt, h = divmod(n, 2)
                            wait_big_free(pe, 12 * j + 4 + n)
                            if n == 0:
                                pe.wait_ge(S["proj_hi"], 4 * j + 4)
                                pe.wait_ge(S["proj_lo"], 4 * j + 4)
                            wd = (qt + 1) * P
                            for m in range(2):
                                out = psBig[:, n % 2, m, 0:wd]
                                three(out, qT, kT, lambda a: a[:, 2 * h + m, qt * P:wd], lambda a: a[:, m, 0:wd],
                                      True, False)
                                mm = nc.tensor.matmul(psBig[:, n % 2, m, qt * P:wd], s["identb"][:, :], s["maskb"][:, :],
                                                      start=False, stop=True)
                            mm.then_inc(S["scores_done"], 1)
                        elif kind == "T":
                            qt = n // 2
                            pe.wait_ge(S["probs_done"], 8 * j + n + 1)
                            if 8 * j + n > 0:
                                pe.wait_ge(S["pt_hi"], 8 * j + n)
                                pe.wait_ge(S["pt_lo"], 8 * j + n)
                            for kt in range(qt + 1):
                                mm = nc.tensor.transpose(psT[:, kt, :], prob[:, n % 2, 0, kt * P:(kt + 1) * P],
                                                         s["ident"][:, :])
                            mm.then_inc(S["pt_done"], 1)
                        elif kind == "PV":
                            m = 4 * j + n
                            pe.wait_ge(S["pt_hi"], 2 * m + 2)
                            pe.wait_ge(S["pt_lo"], 2 * m + 2)
                            if m > 0:
                                pe.wait_ge(S["head_done"], m)
                            for h in range(2):
                                for kt in range(n + 1):
                                    mm = three(psPV[:, h, :], pT, v, lambda a: a[:, h, kt, :], lambda a: a[:, kt, :],
                                               kt == 0, kt == n)
                            mm.then_inc(S["pv_done"], 1)
                        elif kind == "OT":
                            m = 4 * j + n
                            pe.wait_ge(S["head_done"], m + 1)
                            if m > 0:
                                pe.wait_ge(S["ot_hi"], m)
                                pe.wait_ge(S["ot_lo"], m)
                            for r in range(4):
                                mm = nc.tensor.transpose(psOT[:, r, :], head[:, r // 2, (r % 2) * P:(r % 2 + 1) * P],
                                                         s["ident"][:, :])
                            mm.then_inc(S["ot_done"], 1)
                        elif kind == "OUT":
                            m = 4 * j + n
                            if m == 0:
                                pe.wait_ge(S["ow_hi"], 4)
                                pe.wait_ge(S["ow_lo"], 4)
                            pe.wait_ge(S["ot_hi"], m + 1)
                            pe.wait_ge(S["ot_lo"], m + 1)
                            if m > 0:
                                pe.wait_ge(S["acc_done"], m)
                            for r in range(4):
                                mm = three(psOUT[:, :], hT, ow, lambda a: a[:, r, :], lambda a: a[:, r, :],
                                           r == 0, r == 3)
                            mm.then_inc(S["out_done"], 1)

                def split_x(eng, j, n):
                    if n == 0:
                        eng.wait_ge(S["x_loaded"], 16 * (j + 1))
                        if j > 0:
                            eng.wait_ge(S["proj_done"], 4 * j)

                @block.scalar
                def _(act):
                    def x_high(j, n):
                        split_x(act, j, n)
                        nc.scalar.copy(x[0][:, 2 * n:2 * n + 2, :], xraw[:, 2 * n:2 * n + 2, :]).then_inc(S["x_hi"], 1)

                    act.wait_ge(S["w_loaded"], 16)
                    for k in range(KT):
                        nc.scalar.copy(w[0][:, k, :], wraw[:, k, :]).then_inc(S["w_hi"], 1)
                    x_high(0, 0)
                    x_high(0, 1)
                    act.wait_ge(S["b_loaded"], 48)
                    act.wait_ge(S["scan_loaded"], 48)
                    for kind, j, n in order:
                        if kind in ("K", "Q", "V"):
                            r = use_of(kind, n)
                            if kind == "V" and j == 0:
                                act.wait_ge(S["ow_loaded"], 16)
                                act.wait_ge(S["ow_col"], 1)
                                for t in range(4):
                                    nc.scalar.activation(ow[0][:, t, :], wraw[:, t, 0:HID], ACT.Copy,
                                                         scale=subln[:, t % 2:t % 2 + 1]).then_inc(S["ow_hi"], 1)
                            act.wait_ge(S["proj_done"], 4 * j + r + 1)
                            big = psBig[:, r % 2]
                            if kind == "V":
                                ins = nc.scalar.copy(v[0][:, :, :].rearrange("p a b -> p (a b)"),
                                                     big.rearrange("p a b -> p (a b)"))
                            else:
                                dst, col = (kT, 4) if kind == "K" else (qT, 2 * n)
                                base = 0 if kind == "K" else 2 * n
                                for m in range(2):
                                    ins = nc.scalar.activation(dst[0][:, base + m, :], big[:, m, :], ACT.Identity,
                                                               bias=bias[:, col + m:col + m + 1])
                            ins.then_inc(S["proj_hi"], 1)
                        elif kind == "X":
                            x_high(j, n)
                        elif kind == "S":
                            u = 8 * j + n
                            wd = (n // 2 + 1) * P
                            act.wait_ge(S["max_done"], u + 1)
                            if u >= 2:
                                act.wait_ge(S["pt_done"], u - 1)
                            for m in range(2):
                                ins = nc.scalar.activation(prob[:, n % 2, m, 0:wd], psBig[:, n % 2, m, 0:wd], ACT.Exp,
                                                           bias=nb[:, n % 2, m:m + 1], scale=SCALE,
                                                           accum_out=rowsum[:, n % 2, m:m + 1])
                            ins.then_inc(S["exp_done"], 1)
                        elif kind == "T":
                            u = 8 * j + n
                            act.wait_ge(S["pt_done"], u + 1)
                            if u >= 2:
                                act.wait_ge(S["pv_done"], u // 2)
                            nc.scalar.copy(pT[0][:, n % 2, 0:n // 2 + 1, :], psT[:, 0:n // 2 + 1, :]) \
                                .then_inc(S["pt_hi"], 1)
                        elif kind == "PV":
                            m = 4 * j + n
                            act.wait_ge(S["pv_done"], m + 1)
                            for h in range(2):
                                if h or m:
                                    act.wait_ge(S["sq_done"], 2 * m + h)
                                nc.scalar.activation(junk[:, :], psPV[:, h, :], ACT.Square,
                                                     accum_out=msq[:, n % 2, h:h + 1]).then_inc(S["sq_done"], 1)
                        elif kind == "R":
                            m = 4 * j + n
                            act.wait_ge(S["var_done"], m + 1)
                            nc.scalar.activation(rms[:, n % 2, :], var[:, n % 2, :], ACT.Ln).then_inc(S["ln_done"], 1)
                            act.wait_ge(S["ln_done"], m + 1)
                            nc.scalar.activation(rms[:, n % 2, :], rms[:, n % 2, :], ACT.Exp, scale=-0.5) \
                                .then_inc(S["guess_done"], 1)
                        elif kind == "OT":
                            m = 4 * j + n
                            act.wait_ge(S["ot_done"], m + 1)
                            if m > 0:
                                act.wait_ge(S["out_done"], m)
                            nc.scalar.copy(hT[0][:, :, :], psOT[:, :, :]).then_inc(S["ot_hi"], 1)
                        elif kind == "M":
                            k = 8 * j + n
                            state, half = divmod(k, 2)
                            if k >= 2:
                                act.wait_ge(S["scan_done"], k - 1)
                            for c in range(2):
                                ct = 2 * half + c
                                ins = nc.scalar.activation(dA[:, k % 2, c, 1:T], dt[:, ct, 1:T], ACT.Exp,
                                                           scale=s["negA"][:, ct * NS + state:ct * NS + state + 1])
                            ins.then_inc(S["dA_done"], 1)

                def scan_piece(dve, k):
                    dve.wait_ge(S["dA_done"], k + 1)
                    dve.wait_ge(S["dbu_done"], k + 1)
                    flat = st[:, k % 3].rearrange("p c t -> p (c t)")
                    nc.vector.tensor_tensor_scan(flat, dA[:, k % 2].rearrange("p c t -> p (c t)"), flat, 0.0,
                                                 ALU.mult, ALU.add).then_inc(S["scan_done"], 1)

                @block.vector
                def _(dve):
                    mstep = chained(dve, S["max_step"])
                    cstep = chained(dve, S["comb_step"])
                    vstep = chained(dve, S["var_step"])
                    rstep = chained(dve, S["rms_step"])

                    def f32(ap):
                        return ap.bitcast(F32)

                    def x_low(j, n):
                        split_x(dve, j, n)
                        dve.wait_ge(S["x_hi"], 2 * j + n + 1)
                        nc.vector.tensor_tensor(x[1][:, 2 * n:2 * n + 2, :], xraw[:, 2 * n:2 * n + 2, :],
                                                f32(x[0][:, 2 * n:2 * n + 2, :]), ALU.subtract).then_inc(S["x_lo"], 1)

                    for k in range(KT):
                        dve.wait_ge(S["w_hi"], k + 1)
                        nc.vector.tensor_tensor(w[1][:, k, :], wraw[:, k, :], f32(w[0][:, k, :]),
                                                ALU.subtract).then_inc(S["w_lo"], 1)
                    x_low(0, 0)
                    x_low(0, 1)
                    dve.wait_ge(S["b_loaded"], 48)
                    nc.vector.tensor_scalar(subln[:, :], subln[:, :], 1.0 - LAMBDA_INIT, None, ALU.mult) \
                        .then_inc(S["ow_col"], 1)
                    dve.wait_ge(S["scan_loaded"], 48)
                    for c in range(CT):
                        nc.vector.tensor_scalar(y[:, c, :], y[:, c, :], s["Dcol"][:, c:c + 1], None, ALU.mult) \
                            .then_inc(S["y_init"], 1)
                    pieces = []
                    for kind, j, n in order:
                        if kind in ("K", "Q", "V"):
                            r = use_of(kind, n)
                            if kind == "V" and j == 0:
                                for t in range(4):
                                    dve.wait_ge(S["ow_hi"], t + 1)
                                    nc.vector.scalar_tensor_tensor(ow[1][:, t, :], wraw[:, t, 0:HID],
                                                                   subln[:, t % 2:t % 2 + 1], f32(ow[0][:, t, :]),
                                                                   ALU.mult, ALU.subtract).then_inc(S["ow_lo"], 1)
                            dve.wait_ge(S["proj_hi"], 4 * j + r + 1)
                            big = psBig[:, r % 2]
                            if kind == "V":
                                ins = nc.vector.tensor_tensor(v[1][:, :, :].rearrange("p a b -> p (a b)"),
                                                              big.rearrange("p a b -> p (a b)"),
                                                              f32(v[0][:, :, :].rearrange("p a b -> p (a b)")),
                                                              ALU.subtract)
                            else:
                                dst, col = (kT, 4) if kind == "K" else (qT, 2 * n)
                                base = 0 if kind == "K" else 2 * n
                                for m in range(2):
                                    ins = nc.vector.scalar_tensor_tensor(
                                        dst[1][:, base + m, :], big[:, m, :], bias[:, col + m:col + m + 1],
                                        f32(dst[0][:, base + m, :]), ALU.add, ALU.subtract)
                            ins.then_inc(S["proj_lo"], 1)
                        elif kind == "X":
                            x_low(j, n)
                        elif kind == "S":
                            u = 8 * j + n
                            wd = (n // 2 + 1) * P
                            dve.wait_ge(S["scores_done"], u + 1)
                            mstep(nc.vector.reduce_max(mx[:, n % 2, :], psBig[:, n % 2, :, 0:wd], AX.X))
                            nc.vector.tensor_scalar(nb[:, n % 2, :], mx[:, n % 2, :], -SCALE, None, ALU.mult) \
                                .then_inc(S["max_done"], 1)
                        elif kind == "C":
                            u = 8 * j + n
                            qt, h = divmod(n, 2)
                            wd = (qt + 1) * P
                            dve.wait_ge(S["exp_done"], u + 1)
                            cstep(nc.vector.reciprocal(rinv[:, n % 2, :], rowsum[:, n % 2, :]))
                            cstep(nc.vector.scalar_tensor_tensor(coef[:, n % 2:n % 2 + 1], rinv[:, n % 2, 1:2],
                                                                 s["neglam"][:, :], rowsum[:, n % 2, 0:1],
                                                                 ALU.mult, ALU.mult))
                            cstep(nc.vector.tensor_copy(r1[:, qt % 2, h:h + 1], rinv[:, n % 2, 0:1]))
                            nc.vector.scalar_tensor_tensor(prob[:, n % 2, 0, 0:wd], prob[:, n % 2, 1, 0:wd],
                                                           coef[:, n % 2:n % 2 + 1], prob[:, n % 2, 0, 0:wd],
                                                           ALU.mult, ALU.add).then_inc(S["probs_done"], 1)
                        elif kind == "T":
                            u = 8 * j + n
                            dve.wait_ge(S["pt_hi"], u + 1)
                            nc.vector.tensor_tensor(pT[1][:, n % 2, 0:n // 2 + 1, :], psT[:, 0:n // 2 + 1, :],
                                                    f32(pT[0][:, n % 2, 0:n // 2 + 1, :]), ALU.subtract) \
                                .then_inc(S["pt_lo"], 1)
                        elif kind == "PV":
                            m = 4 * j + n
                            dve.wait_ge(S["sq_done"], 2 * m + 2)
                            vstep(nc.vector.scalar_tensor_tensor(var[:, n % 2, :], msq[:, n % 2, :], 1.0 / E2,
                                                                 r1[:, n % 2, :], ALU.mult, ALU.mult))
                            vstep(nc.vector.tensor_tensor(var[:, n % 2, :], var[:, n % 2, :], r1[:, n % 2, :], ALU.mult))
                            nc.vector.tensor_scalar(var[:, n % 2, :], var[:, n % 2, :], EPS, None, ALU.add) \
                                .then_inc(S["var_done"], 1)
                        elif kind == "R":
                            m = 4 * j + n
                            dve.wait_ge(S["guess_done"], m + 1)
                            rsqrt_newton(nc.vector, rstep, rms[:, n % 2, :], var[:, n % 2, :], tmp[:, :])
                            rstep(nc.vector.tensor_tensor(rms[:, n % 2, :], rms[:, n % 2, :], r1[:, n % 2, :], ALU.mult))
                            if m > 0:
                                dve.wait_ge(S["ot_done"], m)
                            for h in range(2):
                                ins = nc.vector.tensor_scalar(head[:, h, :], psPV[:, h, :], rms[:, n % 2, h:h + 1],
                                                              None, ALU.mult)
                            ins.then_inc(S["head_done"], 1)
                        elif kind == "OT":
                            m = 4 * j + n
                            dve.wait_ge(S["ot_hi"], m + 1)
                            nc.vector.tensor_tensor(hT[1][:, :, :], psOT[:, :, :], f32(hT[0][:, :, :]),
                                                    ALU.subtract).then_inc(S["ot_lo"], 1)
                        elif kind == "OUT":
                            m = 4 * j + n
                            dve.wait_ge(S["out_done"], m + 1)
                            dve.wait_ge(S[f"acc_loaded{m % 2}"], 16 * (m // 2 + 1))
                            nc.vector.tensor_tensor(acc[:, m % 2, :], psOUT[:, :], acc[:, m % 2, :], ALU.add) \
                                .then_inc(S["acc_done"], 1)
                        elif kind == "M":
                            pieces.append(8 * j + n)
                            if len(pieces) > 1:
                                scan_piece(dve, pieces.pop(0))
                    scan_piece(dve, pieces.pop(0))

                @block.gpsimd
                def _(pool):
                    def drive(k):
                        state, half = divmod(k, 2)
                        pool.wait_ge(S[f"bc_loaded{state % 2}"], 32 * (state // 2 + 1))
                        if k >= 3:
                            pool.wait_ge(S["piece_done"], k - 2)
                        nc.gpsimd.tensor_tensor(st[:, k % 3], dtu[:, 2 * half:2 * half + 2, :],
                                                Bn[:, state % 2, :].unsqueeze(1).broadcast_to([P, 2, T]),
                                                ALU.mult).then_inc(S["dbu_done"], 1)

                    pool.wait_ge(S["scan_loaded"], 48)
                    drive(0)
                    drive(1)
                    pool.wait_ge(S["y_init"], CT)
                    for k in range(2 * NS):
                        state, half = divmod(k, 2)
                        pool.wait_ge(S["scan_done"], k + 1)
                        nc.gpsimd.tensor_tensor(st[:, k % 3], st[:, k % 3],
                                                Cn[:, state % 2, :].unsqueeze(1).broadcast_to([P, 2, T]),
                                                ALU.mult).then_inc(S["gated"], 1)
                        pool.wait_ge(S["gated"], k + 1)
                        nc.gpsimd.tensor_tensor(y[:, 2 * half:2 * half + 2, :], y[:, 2 * half:2 * half + 2, :],
                                                st[:, k % 3], ALU.add).then_inc(S["piece_done"], 1)
                        if k + 2 < 2 * NS:
                            drive(k + 2)
            clear(nc, sems)



def expert_phase(nc, d, s):
    with ExitStack() as ctx:
        def sb(name, shape, dt=F32):
            return ctx.enter_context(nc.sbuf_tensor(name, shape, dt))

        def pair(name, shape):
            return sb(name + "_hi", shape, F32R), sb(name + "_lo", shape, F32R)

        def ps(name, shape):
            return ctx.enter_context(nc.psum_tensor(name, shape, F32))

        cw = pair("cw", [P, WCOLS])
        x1 = sb("x1", [P, TT, HID])
        yg = sb("yg", [P, CT, T])
        gate = sb("gate", [P, 2, HID])
        outb = sb("outb", [P, HID])
        rbias = sb("rbias", [P, NE])
        x2T = pair("x2T", [P, KT, T])
        xl = pair("xl", [P, T])
        wb = sb("wb", [P, 3, T])
        act_ = sb("act_buf", [P, 3, T])
        hid = pair("hid", [P, 2, T])
        hs = pair("hs", [P, 2, T])
        lat = pair("lat", [P, T])
        stats = sb("stats", [P, TT, 6])
        mv = sb("mv", [P, TT, 2])
        var = sb("mvar", [P, TT])
        rstd = sb("rstd", [P, TT])
        tmp = sb("mtmp", [P, TT])
        ex = sb("ex", [P, TT, NE])
        prb = sb("prb", [P, TT, NE])
        sel = sb("sel", [P, TT, NE])
        top = sb("top", [P, TT, 8])
        wsum = sb("wsum", [P, TT])
        wT = sb("wT", [NE, T])
        psGU = ps("psGU", [P, 3, 2, T])
        psA = ps("psA", [P, T])
        psM = ps("psM", [P, T])

        c_load = ctx.enter_context(nc.semaphore("rows_loaded"))
        w_load = [ctx.enter_context(nc.semaphore(f"cw_loaded{n}")) for n in range(2)]
        w_hi = ctx.enter_context(nc.semaphore("cw_hi"))
        w_lo = ctx.enter_context(nc.semaphore("cw_lo"))
        stage = (x1, yg)
        CH = TT * HID
        chunks = [(c, min(c + CH, WCOLS)) for c in range(0, WCOLS, CH)]
        with nc.Block() as block:
            @block.sync
            def _(sp):
                sp.dma_start(outb[:, :], d["out_b"].broadcast_to([P, HID])).then_inc(c_load, 16)
                sp.dma_start(rbias[:, :], d["route_b"].broadcast_to([P, NE])).then_inc(c_load, 16)
                for n, (a, z) in enumerate(chunks):
                    if n >= 2:
                        sp.wait_ge(w_lo, n - 1)
                    sp.dma_start(stage[n % 2][:, :, :].rearrange("p a b -> p (a b)")[:, 0:z - a],
                                 d["cw"][:, a:z]).then_inc(w_load[n % 2], 16)
                sp.wait_ge(c_load, 32)

            @block.scalar
            def _(act):
                for n, (a, z) in enumerate(chunks):
                    act.wait_ge(w_load[n % 2], 16 * (n // 2 + 1))
                    nc.scalar.copy(cw[0][:, a:z], stage[n % 2][:, :, :].rearrange("p a b -> p (a b)")[:, 0:z - a]) \
                        .then_inc(w_hi, 1)

            @block.vector
            def _(dve):
                for n, (a, z) in enumerate(chunks):
                    dve.wait_ge(w_hi, n + 1)
                    nc.vector.tensor_tensor(cw[1][:, a:z],
                                            stage[n % 2][:, :, :].rearrange("p a b -> p (a b)")[:, 0:z - a],
                                            cw[0][:, a:z].bitcast(F32), ALU.subtract).then_inc(w_lo, 1)

        names = ("acc_loaded", "y_loaded", "x0_done", "stat_step", "var_done", "ln_done", "guess_done", "norm_done",
                 "gate_exp", "gate_step", "yg_done", "ygT_done", "x2_added", "x2_done", "x2T_done", "x2T_hi", "x2T_lo",
                 "logits_done", "rexp_done", "route_step", "route_done", "wT_ps", "wT_sb", "wT_stored", "wb_loaded0", "wb_loaded1", "wb_loaded2",
                 "xl_done", "xl_hi", "xl_lo", "up_done", "relu_done", "weighted", "sq_step", "prod_done", "hid_hi",
                 "hid_lo", "down_done", "lat_done", "lat_hi", "lat_lo", "out_ps", "x3_done", "out_done", "stored")
        sems = [ctx.enter_context(nc.semaphore(n)) for n in names]
        S = dict(zip(names, sems))

        UNITS = [("s", 0, t) for t in range(2)] + [("e", e, t) for e in range(NE) for t in range(2)]
        NU = len(UNITS)

        with nc.Fori(0, B) as b:
            with nc.Block(no_gpsimd_drain=True) as block:
                @block.sync
                def _(sp):
                    sp.dma_start(x1[:, :, :], d["acc"].rearrange("(b t p) n -> b p t n", b=B, p=P)[bass.ds(b, 1)]
                                 .rearrange("b p t n -> p (b t) n")).then_inc(S["acc_loaded"], 16)
                    sp.dma_start(yg[:, :, :].rearrange("p c t -> p (c t)"),
                                 d["y"][bass.ds(b, 1), :, :].rearrange("b p n -> p (b n)")).then_inc(S["y_loaded"], 16)
                    sp.wait_ge(S["wT_sb"], 1)
                    sp.dma_start(d["wT"], wT[:, :]).then_inc(S["wT_stored"], 16)
                    sp.wait_ge(S["wT_stored"], 16)
                    for e in range(NE):
                        if e >= 3:
                            sp.wait_ge(S["weighted"], 2 * (e - 2))
                        sp.dma_start(wb[:, e % 3, :], d["wT"][e:e + 1, :].broadcast_to([P, T])) \
                            .then_inc(S[f"wb_loaded{e % 3}"], 16)
                    for t in range(TT):
                        sp.wait_ge(S["out_done"], t + 1)
                        sp.dma_start(d["out"].rearrange("(b t p) n -> b t p n", b=B, p=P)[bass.ds(b, 1), t]
                                     .rearrange("b p n -> (b p) n"), x1[:, t, :]).then_inc(S["stored"], 16)
                    sp.wait_ge(S["stored"], 16 * TT)

                @block.tensor
                def _(pe):
                    def three(out, lhs, rhs, at_l, at_r, start, stop):
                        nc.tensor.matmul(out, at_l(lhs[0]), at_r(rhs[0]), start=start, stop=False)
                        nc.tensor.matmul(out, at_l(lhs[0]), at_r(rhs[1]), start=False, stop=False)
                        return nc.tensor.matmul(out, at_l(lhs[1]), at_r(rhs[0]), start=False, stop=stop)

                    pe.wait_ge(S["yg_done"], CT)
                    for t in range(TT):
                        for c in range(CT):
                            mm = nc.tensor.transpose(psGU[:, t // 2, t % 2, c * P:(c + 1) * P],
                                                     yg[:, c, t * P:(t + 1) * P], s["ident"][:, :])
                        mm.then_inc(S["ygT_done"], 1)
                    pe.wait_ge(S["x2_done"], TT)
                    for k in range(KT):
                        for t in range(TT):
                            mm = nc.tensor.transpose(psGU[:, k // 2, k % 2, t * P:(t + 1) * P],
                                                     x1[:, t, k * P:(k + 1) * P], s["ident"][:, :])
                        mm.then_inc(S["x2T_done"], 1)
                    pe.wait_ge(S["x2T_hi"], KT)
                    pe.wait_ge(S["x2T_lo"], KT)
                    for t in range(TT):
                        for k in range(KT):
                            mm = three(psM[:, t * NE:(t + 1) * NE], x2T, cw, lambda a: a[:, k, t * P:(t + 1) * P],
                                       lambda a: a[:, WGT + k * NE:WGT + (k + 1) * NE], k == 0, k == KT - 1)
                    mm.then_inc(S["logits_done"], 1)
                    for k in range(KT):
                        mm = three(psA[:, :], cw, x2T, lambda a: a[:, WDN + k * LAT:WDN + (k + 1) * LAT],
                                   lambda a: a[:, k, :], k == 0, k == KT - 1)
                    mm.then_inc(S["xl_done"], 1)

                    def up(n):
                        kind, e, t = UNITS[n]
                        if n >= 3:
                            pe.wait_ge(S["prod_done"], n - 2)
                        if kind == "s":
                            for gu, w0 in ((0, SWG), (1, SW1)):
                                for k in range(KT):
                                    mm = three(psGU[:, n % 3, gu, :], cw, x2T,
                                               lambda a: a[:, w0 + k * 256 + t * P:w0 + k * 256 + (t + 1) * P],
                                               lambda a: a[:, k, :], k == 0, k == KT - 1)
                        else:
                            if n == 2:
                                pe.wait_ge(S["xl_hi"], 1)
                                pe.wait_ge(S["xl_lo"], 1)
                            for gu, w0 in ((0, RWG), (1, RW1)):
                                mm = three(psGU[:, n % 3, gu, :], cw, xl,
                                           lambda a: a[:, w0 + e * 256 + t * P:w0 + e * 256 + (t + 1) * P],
                                           lambda a: a[:, :], True, True)
                        mm.then_inc(S["up_done"], 1)

                    def down(n):
                        _, e, t = UNITS[n]
                        pe.wait_ge(S["hid_hi"], n + 1)
                        pe.wait_ge(S["hid_lo"], n + 1)
                        mm = three(psA[:, :], cw, hid,
                                   lambda a: a[:, RW2 + (2 * e + t) * LAT:RW2 + (2 * e + t + 1) * LAT],
                                   lambda a: a[:, n % 2, :], n == 2, n == NU - 1)
                        mm.then_inc(S["down_done"], 1)

                    for n in range(NU):
                        up(n)
                        if n == 1:
                            pe.wait_ge(S["route_done"], 1)
                            for t in range(TT):
                                mm = nc.tensor.transpose(psM[0:NE, t * P:(t + 1) * P], sel[:, t, :], s["ident"][:, :])
                            mm.then_inc(S["wT_ps"], 1)
                        if n >= 4:
                            down(n - 2)
                    down(NU - 2)
                    down(NU - 1)
                    pe.wait_ge(S["lat_hi"], 1)
                    pe.wait_ge(S["lat_lo"], 1)
                    for t in range(TT):
                        out = psGU[:, t // 2, t % 2, :]
                        for h in range(2):
                            three(out, hs, cw, lambda a: a[:, h, t * P:(t + 1) * P],
                                  lambda a: a[:, SW2 + h * HID:SW2 + (h + 1) * HID], h == 0, False)
                        mm = three(out, lat, cw, lambda a: a[:, t * P:(t + 1) * P],
                                   lambda a: a[:, WUP:WUP + HID], False, True)
                        mm.then_inc(S["out_ps"], 1)

                @block.scalar
                def _(act):
                    def guess(n):
                        act.wait_ge(S["var_done"], n)
                        nc.scalar.activation(rstd[:, :], var[:, :], ACT.Ln).then_inc(S["ln_done"], 1)
                        act.wait_ge(S["ln_done"], n)
                        nc.scalar.activation(rstd[:, :], rstd[:, :], ACT.Exp, scale=-0.5).then_inc(S["guess_done"], 1)

                    guess(1)
                    for c in range(CT):
                        act.wait_ge(S["norm_done"], c + 1)
                        if c >= 2:
                            act.wait_ge(S["yg_done"], c - 1)
                        nc.scalar.activation(gate[:, c % 2, :], x1[:, c, :], ACT.Tanh, scale=0.5) \
                            .then_inc(S["gate_exp"], 1)
                    guess(2)
                    for k in range(KT):
                        act.wait_ge(S["x2T_done"], k + 1)
                        nc.scalar.copy(x2T[0][:, k, :], psGU[:, k // 2, k % 2, :]).then_inc(S["x2T_hi"], 1)
                    act.wait_ge(S["logits_done"], 1)
                    nc.scalar.activation(ex[:, :, :].rearrange("p a b -> p (a b)"), psM[:, 0:TT * NE], ACT.Exp,
                                         scale=-1.0).then_inc(S["rexp_done"], 1)
                    act.wait_ge(S["xl_done"], 1)
                    nc.scalar.copy(xl[0][:, :], psA[:, :]).then_inc(S["xl_hi"], 1)

                    def relu(n):
                        act.wait_ge(S["up_done"], n + 1)
                        if n >= 3:
                            act.wait_ge(S["hid_lo"], n - 2)
                        nc.scalar.activation(act_[:, n % 3, :], psGU[:, n % 3, 0, :], ACT.Relu) \
                            .then_inc(S["relu_done"], 1)

                    def high(n):
                        act.wait_ge(S["prod_done"], n + 1)
                        if UNITS[n][0] == "s":
                            dst = hs[0][:, n, :]
                        else:
                            dst = hid[0][:, n % 2, :]
                            if n >= 4:
                                act.wait_ge(S["down_done"], n - 3)
                        nc.scalar.copy(dst, act_[:, n % 3, :]).then_inc(S["hid_hi"], 1)

                    for n in range(NU):
                        relu(n)
                        if n == 1:
                            act.wait_ge(S["wT_ps"], 1)
                            nc.scalar.copy(wT[:, :], psM[0:NE, :]).then_inc(S["wT_sb"], 1)
                        if n >= 1:
                            high(n - 1)
                    high(NU - 1)
                    act.wait_ge(S["down_done"], NU - 2)
                    nc.scalar.copy(lat[0][:, :], psA[:, :]).then_inc(S["lat_hi"], 1)
                    guess(3)

                @block.gpsimd
                def _(pool):
                    pool.wait_ge(S["acc_loaded"], 16)
                    for t in range(TT):
                        nc.gpsimd.tensor_tensor(x1[:, t, :], x1[:, t, :], outb[:, :], ALU.add).then_inc(S["x0_done"], 1)
                    for n in range(2, NU):
                        _, e, t = UNITS[n]
                        pool.wait_ge(S["relu_done"], n + 1)
                        pool.wait_ge(S[f"wb_loaded{e % 3}"], 16 * (e // 3 + 1))
                        nc.gpsimd.tensor_tensor(act_[:, n % 3, :], act_[:, n % 3, :], wb[:, e % 3, :], ALU.mult) \
                            .then_inc(S["weighted"], 1)

                @block.vector
                def _(dve):
                    sstep = chained(dve, S["stat_step"])
                    gstep = chained(dve, S["gate_step"])
                    rstep = chained(dve, S["route_step"])
                    qstep = chained(dve, S["sq_step"])

                    def f32(ap):
                        return ap.bitcast(F32)

                    def norm(n, ready, done):
                        for t in range(TT):
                            dve.wait_ge(ready, t + 1)
                            sstep(nc.vector.bn_stats(stats[:, t, :], x1[:, t, :]))
                            sstep(nc.vector.bn_aggr(mv[:, t, :], stats[:, t, :]))
                        nc.vector.tensor_scalar(var[:, :], mv[:, :, 1], EPS, None, ALU.add).then_inc(S["var_done"], 1)
                        dve.wait_ge(S["guess_done"], n)
                        rsqrt_newton(nc.vector, sstep, rstd[:, :], var[:, :], tmp[:, :])
                        for t in range(TT):
                            nc.vector.tensor_scalar(x1[:, t, :], x1[:, t, :], mv[:, t, 0:1], rstd[:, t:t + 1],
                                                    ALU.subtract, ALU.mult).then_inc(done, 1)

                    norm(1, S["x0_done"], S["norm_done"])
                    dve.wait_ge(S["y_loaded"], 16)
                    for c in range(CT):
                        dve.wait_ge(S["gate_exp"], c + 1)
                        gt = gate[:, c % 2, :]
                        gstep(nc.vector.scalar_tensor_tensor(gt, gt, 1.0, x1[:, c, :], ALU.add, ALU.mult))
                        nc.vector.scalar_tensor_tensor(yg[:, c, :], yg[:, c, :], 0.5, gt, ALU.mult, ALU.mult) \
                            .then_inc(S["yg_done"], 1)
                    for t in range(TT):
                        dve.wait_ge(S["ygT_done"], t + 1)
                        nc.vector.tensor_tensor(x1[:, t, :], psGU[:, t // 2, t % 2, :], x1[:, t, :], ALU.add) \
                            .then_inc(S["x2_added"], 1)
                    norm(2, S["x2_added"], S["x2_done"])
                    for k in range(KT):
                        dve.wait_ge(S["x2T_hi"], k + 1)
                        nc.vector.tensor_tensor(x2T[1][:, k, :], psGU[:, k // 2, k % 2, :], f32(x2T[0][:, k, :]),
                                                ALU.subtract).then_inc(S["x2T_lo"], 1)
                    dve.wait_ge(S["xl_hi"], 1)
                    nc.vector.tensor_tensor(xl[1][:, :], psA[:, :], f32(xl[0][:, :]), ALU.subtract) \
                        .then_inc(S["xl_lo"], 1)
                    dve.wait_ge(S["rexp_done"], 1)
                    rstep(nc.vector.tensor_scalar(ex[:, :, :], ex[:, :, :], 1.0, None, ALU.add))
                    rstep(nc.vector.reciprocal(prb[:, :, :], ex[:, :, :]))
                    rstep(nc.vector.tensor_tensor(ex[:, :, :], prb[:, :, :],
                                                  rbias[:, :].unsqueeze(1).broadcast_to([P, TT, NE]), ALU.add))
                    for t in range(TT):
                        rstep(nc.vector.max(top[:, t, :], ex[:, t, :]))
                        rstep(nc.vector.match_replace(out=sel[:, t, :], in_to_replace=top[:, t, :],
                                                      in_values=ex[:, t, :], imm_value=-3e38))
                    rstep(nc.vector.scalar_tensor_tensor(sel[:, :, :], sel[:, :, :], -3e38, prb[:, :, :],
                                                         ALU.is_equal, ALU.mult))
                    rstep(nc.vector.reduce_sum(wsum[:, :], sel[:, :, :], AX.X))
                    rstep(nc.vector.reciprocal(wsum[:, :], wsum[:, :]))
                    rstep(nc.vector.tensor_scalar(wsum[:, :], wsum[:, :], ROUTE_SCALE, None, ALU.mult))
                    nc.vector.tensor_tensor(sel[:, :, :], sel[:, :, :],
                                            wsum[:, :].unsqueeze(2).broadcast_to([P, TT, NE]), ALU.mult) \
                        .then_inc(S["route_done"], 1)

                    def low(n):
                        dve.wait_ge(S["hid_hi"], n + 1)
                        if UNITS[n][0] == "s":
                            hi, lo = hs[0][:, n, :], hs[1][:, n, :]
                        else:
                            hi, lo = hid[0][:, n % 2, :], hid[1][:, n % 2, :]
                        nc.vector.tensor_tensor(lo, act_[:, n % 3, :], f32(hi), ALU.subtract) \
                            .then_inc(S["hid_lo"], 1)

                    for n in range(NU):
                        if n < 2:
                            dve.wait_ge(S["relu_done"], n + 1)
                        else:
                            dve.wait_ge(S["weighted"], n - 1)
                        a = act_[:, n % 3, :]
                        qstep(nc.vector.scalar_tensor_tensor(a, psGU[:, n % 3, 0, :], 0.0, a, ALU.max, ALU.mult))
                        nc.vector.tensor_tensor(a, psGU[:, n % 3, 1, :], a, ALU.mult).then_inc(S["prod_done"], 1)
                        if n >= 1:
                            low(n - 1)
                    low(NU - 1)
                    dve.wait_ge(S["lat_hi"], 1)
                    nc.vector.tensor_tensor(lat[1][:, :], psA[:, :], f32(lat[0][:, :]), ALU.subtract) \
                        .then_inc(S["lat_lo"], 1)
                    for t in range(TT):
                        dve.wait_ge(S["out_ps"], t + 1)
                        nc.vector.tensor_tensor(x1[:, t, :], psGU[:, t // 2, t % 2, :], x1[:, t, :], ALU.add) \
                            .then_inc(S["x3_done"], 1)
                    norm(3, S["x3_done"], S["out_done"])
            clear(nc, sems)


def layer(nc, d):
    with ExitStack() as ctx:
        def sb(name, shape, dt=F32):
            return ctx.enter_context(nc.sbuf_tensor(name, shape, dt))

        s = {
            "ident": sb("ident", [P, P]), "identb": sb("identb", [P, P], BF16), "maskb": sb("maskb", [P, P], BF16),
            "ones": sb("ones", [1, P]), "neglam": sb("neglam", [P, 1]), "negA": sb("negA", [P, CT * NS]),
            "Dcol": sb("Dcol", [P, CT]), "two": sb("two", [P, 1]),
        }
        d_loaded = ctx.enter_context(nc.semaphore("d_loaded"))
        with nc.Block() as block:
            @block.sync
            def _(sp):
                sp.dma_start(s["Dcol"][:, :], d["Dcol"]).then_inc(d_loaded, 16)
                sp.wait_ge(d_loaded, 16)
        setup(nc, d, s)
        scan_inputs(nc, d, s)
        attend_and_scan(nc, d, s)
        expert_phase(nc, d, s)


def lay_out(inputs):
    import numpy as np

    def rows(a, n):
        return a.reshape(n, P, -1).transpose(1, 0, 2)

    x = np.asarray(inputs["x"])
    wqkv = np.asarray(inputs["L0_attn_Wqkv_w"])
    bqkv = np.asarray(inputs["L0_attn_Wqkv_b"])
    NQ, NK = G * QC, G * KC
    ws, qkb, vb = [], [], []
    for g in range(G):
        idx = np.r_[g * QC:(g + 1) * QC, NQ + g * KC:NQ + (g + 1) * KC, NQ + NK + g * VC:NQ + NK + (g + 1) * VC]
        ws.append(rows(wqkv[idx].T, KT).reshape(P, -1))
        qkb.append(bqkv[idx[:QC + KC]].reshape(6, P).T)
        vb.append(bqkv[idx[QC + KC:]])
    ow = np.asarray(inputs["L0_attn_out_w"]).T
    i = {k: np.asarray(v) for k, v in inputs.items()}
    lam = np.stack([i["L0_attn_lambda_" + n] for n in ("q1", "k1", "q2", "k2")])
    scan_cols = np.concatenate([rows(i["L0_xattn_conv_w"].reshape(CT * P, TAPS), CT),
                                rows(i["L0_xattn_conv_b"][:, None], CT), rows(i["L0_xattn_dt_proj_b"][:, None], CT)], axis=2)

    def flat(a, n):
        return rows(a, n).reshape(P, -1)

    rw1 = i["L0_ffn_rw1"].transpose(2, 0, 1).reshape(LAT, -1)
    rwg = i["L0_ffn_rwg"].transpose(2, 0, 1).reshape(LAT, -1)
    rw2 = i["L0_ffn_rw2"].transpose(0, 2, 1).reshape(NE * 2, P, LAT).transpose(1, 0, 2).reshape(P, -1)
    cw = np.concatenate([flat(i["L0_ffn_sw1"].T, KT), flat(i["L0_ffn_swg"].T, KT), flat(i["L0_ffn_sw2"].T, 2),
                         flat(i["L0_ffn_Wdown"].T, KT), i["L0_ffn_Wup"].T, flat(i["L0_ffn_Wg"].T, KT),
                         rw1, rwg, rw2], axis=1)
    return {
        "x": x.reshape(B * T, HID),
        "xT": x.transpose(0, 2, 1).reshape(B, KT, P, T),
        "w": np.stack(ws), "qk_bias": np.stack(qkb), "v_bias": np.stack(vb),
        "ow": np.stack([rows(ow[g * 512:(g + 1) * 512], 4).reshape(P, -1) for g in range(G)]),
        "subln": i["L0_attn_subln_w"].reshape(2, P).T,
        "lam": lam, "out_b": i["L0_attn_out_b"][None, :],
        "ctxT": i["ctx_1024"].transpose(0, 2, 1).reshape(B, 2, P, T),
        "inT": i["L0_xattn_in_proj_w"].T, "xpT": i["L0_xattn_x_proj_w"].T, "dtT": i["L0_xattn_dt_proj_w"].T,
        "scan_cols": scan_cols,
        "alog": flat(i["L0_xattn_A_log"], CT), "Dcol": i["L0_xattn_D"].reshape(CT, P).T,
        "cw": cw, "route_b": i["L0_ffn_biases"][None, :],
    }


SCRATCH = {"acc": (B * T, HID), "u": (B, P, CT * T), "dt": (B, P, CT * T), "dtu": (B, P, CT * T),
           "bc": (B, 2 * NS, T), "y": (B, P, CT * T), "wT": (NE, T)}


def kernel(**inputs):
    import numpy as np
    import concourse.bacc as bacc
    from concourse.bass_utils import run_bass_kernel_spmd as run

    nc = bacc.Bacc("TRN2", target_bir_lowering=False, num_devices=1)
    arrays, d = {}, {}
    for name, a in lay_out(inputs).items():
        a = np.ascontiguousarray(a)
        arrays[f"in_{name}"] = a
        d[name] = nc.dram_tensor(f"in_{name}", a.shape, mybir.dt.from_np(a.dtype), kind="ExternalInput").ap()
    for name, shape in SCRATCH.items():
        d[name] = nc.dram_tensor(f"scratch_{name}", shape, F32, kind="Internal").ap()
    d["out"] = nc.dram_tensor("out", (B * T, HID), F32, kind="ExternalOutput").ap()
    layer(nc, d)
    r = run(nc, [arrays], core_ids=[0])
    return r.results[0]["out"].reshape(B, T, HID)
```

```python
import math
from contextlib import ExitStack

import concourse.bass as bass
from concourse import mybir

F32 = mybir.dt.float32
F32R = mybir.dt.float32r
BF16 = mybir.dt.bfloat16
ALU = mybir.AluOpType
ACT = mybir.ActivationFunctionType
AX = mybir.AxisListType

P = 128
B, T, HID = 4, 512, 512
KT = HID // P
TT = T // P
G = 4
HD = 128
E2 = 2 * HD
QC, KC, VC = 4 * HD, 2 * HD, E2
GC = QC + KC + VC
LAMBDA_INIT = 0.8 - 0.6 * math.exp(-0.3)
SCALE = HD ** -0.5
EPS = 1e-5
NEG = -1e30
CT = 4
NS = 16
RANK = 16
TAPS = 4
CTX = 256
NE = 16
LAT = 128
TOPK = 8
ROUTE_SCALE = 2.5
ATANH = (2.0000000078777487, 0.6666631593508026, 0.40024853723499904,
         0.27961418834331303, 0.2817465726538725)

WGT = 0
SW1 = WGT + KT * NE
SWG = SW1 + KT * 256
SW2 = SWG + KT * 256
WDN = SW2 + 2 * HID
WUP = WDN + KT * LAT
RW1 = WUP + HID
RWG = RW1 + NE * 256
RW2 = RWG + NE * 256
WCOLS = RW2 + NE * 2 * LAT


def rsqrt_newton(dve, step, y, v, tmp):
    step(dve.scalar_tensor_tensor(tmp, y, -0.5, y, ALU.mult, ALU.mult))
    step(dve.tensor_tensor(tmp, tmp, v, ALU.mult))
    step(dve.scalar_tensor_tensor(y, tmp, 1.5, y, ALU.add, ALU.mult))


def chained(engine, sem):
    count = [0]

    def step(ins):
        count[0] += 1
        ins.then_inc(sem, 1)
        engine.wait_ge(sem, count[0])

    return step


def clear(nc, sems):
    nums = [s.num for s in sems]
    assert nums == list(range(nums[0], nums[0] + len(nums)))
    nc.vector.sem_clear(range(nums[0], nums[-1] + 1))
    nc.all_engine_barrier(sem_only=True)


def setup(nc, d, s):
    with ExitStack() as ctx:
        def sb(name, shape, dt=F32):
            return ctx.enter_context(nc.sbuf_tensor(name, shape, dt))

        lams = sb("lams", [P, 4, P])
        prod = sb("lam_prod", [P, 2, P])
        lsum = sb("lam_sum", [P, 2])
        lexp = sb("lam_exp", [P, 2])
        alog = sb("alog", [P, CT * NS])
        sems = [ctx.enter_context(nc.semaphore(n)) for n in
                ("loaded", "cleared", "const_done", "lam_step", "act_step", "copied")]
        loaded, cleared, const_done, lam_step, act_step, copied = sems
        with nc.Block() as block:
            @block.sync
            def _(sp):
                for n in range(4):
                    sp.dma_start(lams[:, n, :], d["lam"][n:n + 1, :].broadcast_to([P, P])).then_inc(loaded, 16)
                sp.dma_start(alog[:, :], d["alog"]).then_inc(loaded, 16)
                sp.dma_start(d["acc"], d["x"]).then_inc(copied, 16)
                sp.wait_ge(copied, 16)

            @block.gpsimd
            def _(pool):
                nc.gpsimd.memset(s["ident"][:, :], 0.0).then_inc(cleared, 1)
                nc.gpsimd.memset(s["identb"][:, :], 0.0).then_inc(cleared, 1)
                nc.gpsimd.memset(s["maskb"][:, :], 0.0).then_inc(cleared, 1)
                pool.wait_ge(cleared, 3)
                for m in ("ident", "identb"):
                    nc.gpsimd.affine_select(out=s[m][:, :], in_=s[m][:, :], compare_op=ALU.not_equal, fill=1.0,
                                            base=0, pattern=[[-1, P]], channel_multiplier=1).then_inc(const_done, 1)
                nc.gpsimd.affine_select(out=s["maskb"][:, :], in_=s["maskb"][:, :], compare_op=ALU.is_ge, fill=NEG,
                                        base=0, pattern=[[-1, P]], channel_multiplier=1).then_inc(const_done, 1)
                nc.gpsimd.memset(s["ones"][:, :], 1.0).then_inc(const_done, 1)
                nc.gpsimd.memset(s["two"][:, :], 2.0).then_inc(const_done, 1)
                pool.wait_ge(const_done, 5)

            @block.vector
            def _(dve):
                step = chained(dve, lam_step)
                dve.wait_ge(loaded, 80)
                for n in range(2):
                    step(nc.vector.tensor_tensor(prod[:, n, :], lams[:, 2 * n, :], lams[:, 2 * n + 1, :], ALU.mult))
                step(nc.vector.reduce_sum(lsum[:, :], prod[:, :, :], AX.X))
                dve.wait_ge(act_step, 2)
                step(nc.vector.tensor_tensor(s["neglam"][:, :], lexp[:, 1:2], lexp[:, 0:1], ALU.subtract))
                step(nc.vector.tensor_scalar(s["neglam"][:, :], s["neglam"][:, :], -LAMBDA_INIT, None, ALU.add))
                step(nc.vector.tensor_scalar(s["negA"][:, :], s["negA"][:, :], -1.0, None, ALU.mult))

            @block.scalar
            def _(act):
                act.wait_ge(loaded, 80)
                nc.scalar.activation(s["negA"][:, :], alog[:, :], ACT.Exp).then_inc(act_step, 1)
                act.wait_ge(lam_step, 3)
                nc.scalar.activation(lexp[:, :], lsum[:, :], ACT.Exp).then_inc(act_step, 1)


def scan_inputs(nc, d, s):
    with ExitStack() as ctx:
        def sb(name, shape, dt=F32):
            return ctx.enter_context(nc.sbuf_tensor(name, shape, dt))

        win = sb("win", [P, 2, CT * P])
        wxp = sb("wxp", [P, CT, RANK + 2 * NS])
        wdt = sb("wdt", [RANK, CT * P])
        cols = sb("scan_cols", [P, CT, TAPS + 2])
        ctxT = sb("ctxT", [P, 2, T])
        xpad = sb("xpad", [P, CT, TAPS - 1 + T])
        conv = sb("conv", [P, CT, T])
        e = sb("fe", [P, CT, T])
        u = sb("u", [P, CT, T])
        z = sb("fz", [P, CT, T])
        z2 = sb("fz2", [P, CT, T])
        q = sb("fq", [P, CT, T])
        v = sb("fv", [P, CT, T])
        xdbl = sb("xdbl", [RANK + 2 * NS, T])
        psX = ctx.enter_context(nc.psum_tensor("psX", [P, CT, T], F32))
        psD = ctx.enter_context(nc.psum_tensor("psD", [RANK + 2 * NS, T], F32))
        w_loaded = ctx.enter_context(nc.semaphore("w_loaded"))
        pad_zero = ctx.enter_context(nc.semaphore("pad_zero"))
        halved = ctx.enter_context(nc.semaphore("halved"))
        sems = [ctx.enter_context(nc.semaphore(n)) for n in
                ("ctx_loaded", "inproj_done", "pad_done", "conv_done", "exp_done", "u_done", "xdbl_ps",
                 "xdbl_sb", "dt_ps", "v_done", "abs_done", "exp2_done", "step", "dt_done", "stored")]
        (ctx_loaded, inproj_done, pad_done, conv_done, exp_done, u_done, xdbl_ps, xdbl_sb, dt_ps, v_done, abs_done,
         exp2_done, step_sem, dt_done, stored) = sems
        with nc.Block() as block:
            @block.sync
            def _(sp):
                sp.dma_start(win[:, :, :], d["inT"].rearrange("(k p) n -> p k n", p=P)).then_inc(w_loaded, 16)
                sp.dma_start(wxp[:, :, :], d["xpT"].rearrange("(k p) n -> p k n", p=P)).then_inc(w_loaded, 16)
                sp.dma_start(wdt[:, :], d["dtT"]).then_inc(w_loaded, 16)
                sp.dma_start(cols[:, :, :], d["scan_cols"]).then_inc(w_loaded, 16)
                sp.wait_ge(w_loaded, 64)

            @block.gpsimd
            def _(pool):
                nc.gpsimd.memset(xpad[:, :, 0:TAPS - 1], 0.0).then_inc(pad_zero, 1)
                pool.wait_ge(pad_zero, 1)

            @block.vector
            def _(dve):
                dve.wait_ge(w_loaded, 64)
                nc.vector.tensor_scalar(cols[:, :, 0:TAPS + 1], cols[:, :, 0:TAPS + 1], 0.5, None, ALU.mult) \
                    .then_inc(halved, 1)
        with nc.Fori(0, B) as b:
            with nc.Block(no_gpsimd_drain=True) as block:
                @block.sync
                def _(sp):
                    sp.dma_start(ctxT[:, :, :],
                                 d["ctxT"][bass.ds(b, 1), :, :, :].rearrange("b k p t -> p (b k) t")).then_inc(ctx_loaded, 16)
                    sp.wait_ge(u_done, 1)
                    sp.dma_start(d["u"][bass.ds(b, 1), :, :].rearrange("b p n -> p (b n)"),
                                 u[:, :, :].rearrange("p c t -> p (c t)")).then_inc(stored, 16)
                    sp.wait_ge(xdbl_sb, 1)
                    sp.dma_start(d["bc"][bass.ds(b, 1), :, :].rearrange("b p n -> p (b n)"),
                                 xdbl[RANK:, :]).then_inc(stored, 16)
                    sp.wait_ge(dt_done, 1)
                    sp.dma_start(d["dt"][bass.ds(b, 1), :, :].rearrange("b p n -> p (b n)"),
                                 q[:, :, :].rearrange("p c t -> p (c t)")).then_inc(stored, 16)
                    sp.wait_ge(dt_done, 2)
                    sp.dma_start(d["dtu"][bass.ds(b, 1), :, :].rearrange("b p n -> p (b n)"),
                                 z[:, :, :].rearrange("p c t -> p (c t)")).then_inc(stored, 16)
                    sp.wait_ge(stored, 64)

                @block.tensor
                def _(pe):
                    pe.wait_ge(ctx_loaded, 16)
                    for c in range(CT):
                        for k in range(2):
                            mm = nc.tensor.matmul(psX[:, c, :], win[:, k, c * P:(c + 1) * P], ctxT[:, k, :],
                                                  start=k == 0, stop=k == 1)
                        mm.then_inc(inproj_done, 1)
                    pe.wait_ge(u_done, 1)
                    for c in range(CT):
                        mm = nc.tensor.matmul(psD[:, :], wxp[:, c, :], u[:, c, :], start=c == 0, stop=c == CT - 1)
                    mm.then_inc(xdbl_ps, 1)
                    pe.wait_ge(xdbl_sb, 1)
                    for c in range(CT):
                        mm = nc.tensor.matmul(psX[:, c, :], wdt[:, c * P:(c + 1) * P], xdbl[0:RANK, :],
                                              start=True, stop=True)
                        mm.then_inc(dt_ps, 1)

                @block.scalar
                def _(act):
                    for c in range(CT):
                        act.wait_ge(inproj_done, c + 1)
                        nc.scalar.copy(xpad[:, c, TAPS - 1:], psX[:, c, :]).then_inc(pad_done, 1)
                    for c in range(CT):
                        act.wait_ge(conv_done, c + 1)
                        nc.scalar.activation(e[:, c, :], conv[:, c, :], ACT.Tanh).then_inc(exp_done, 1)
                    act.wait_ge(xdbl_ps, 1)
                    nc.scalar.copy(xdbl[:, :], psD[:, :]).then_inc(xdbl_sb, 1)
                    for c in range(CT):
                        act.wait_ge(dt_ps, c + 1)
                        nc.scalar.activation(v[:, c, :], psX[:, c, :], ACT.Identity,
                                             bias=cols[:, c, TAPS + 1:TAPS + 2]).then_inc(v_done, 1)
                    act.wait_ge(v_done, CT)
                    nc.scalar.activation(z[:, :, :], v[:, :, :], ACT.Abs).then_inc(abs_done, 1)
                    act.wait_ge(abs_done, 1)
                    act.wait_ge(u_done, 1)
                    nc.scalar.activation(e[:, :, :], z[:, :, :], ACT.Exp, scale=-1.0).then_inc(exp2_done, 1)
                    act.wait_ge(exp2_done, 1)
                    nc.scalar.activation(z2[:, :, :], e[:, :, :], ACT.Ln, bias=s["two"][:, :]).then_inc(exp2_done, 1)
                    act.wait_ge(exp2_done, 2)
                    nc.scalar.activation(q[:, :, :], z2[:, :, :], ACT.Exp, scale=-1.0).then_inc(exp2_done, 1)

                @block.vector
                def _(dve):
                    step = chained(dve, step_sem)
                    for c in range(CT):
                        dve.wait_ge(pad_done, c + 1)
                        step(nc.vector.tensor_scalar(conv[:, c, :], xpad[:, c, 0:T], cols[:, c, 0:1],
                                                     cols[:, c, TAPS:TAPS + 1], ALU.mult, ALU.add))
                        for j in range(1, TAPS):
                            ins = nc.vector.scalar_tensor_tensor(conv[:, c, :], xpad[:, c, j:j + T],
                                                                 cols[:, c, j:j + 1], conv[:, c, :], ALU.mult, ALU.add)
                            if j < TAPS - 1:
                                step(ins)
                        ins.then_inc(conv_done, 1)
                    dve.wait_ge(exp_done, CT)
                    dve.wait_ge(conv_done, CT)
                    nc.vector.scalar_tensor_tensor(u[:, :, :], e[:, :, :], 1.0, conv[:, :, :], ALU.add, ALU.mult) \
                        .then_inc(u_done, 1)
                    dve.wait_ge(exp2_done, 3)
                    step(nc.vector.scalar_tensor_tensor(z2[:, :, :], e[:, :, :], 2.0, q[:, :, :], ALU.add, ALU.mult))
                    step(nc.vector.scalar_tensor_tensor(z2[:, :, :], z2[:, :, :], 2.0, q[:, :, :],
                                                        ALU.subtract, ALU.mult))
                    step(nc.vector.scalar_tensor_tensor(z[:, :, :], z2[:, :, :], -1.0, e[:, :, :], ALU.mult, ALU.mult))
                    step(nc.vector.tensor_tensor(z2[:, :, :], z[:, :, :], z[:, :, :], ALU.mult))
                    step(nc.vector.tensor_scalar(q[:, :, :], z2[:, :, :], ATANH[4], None, ALU.mult))
                    for n in (3, 2, 1):
                        step(nc.vector.scalar_tensor_tensor(q[:, :, :], q[:, :, :], ATANH[n], z2[:, :, :],
                                                            ALU.add, ALU.mult))
                    step(nc.vector.scalar_tensor_tensor(q[:, :, :], q[:, :, :], ATANH[0], z[:, :, :],
                                                        ALU.add, ALU.mult))
                    nc.vector.scalar_tensor_tensor(q[:, :, :], v[:, :, :], 0.0, q[:, :, :], ALU.max, ALU.add) \
                        .then_inc(dt_done, 1)
                    dve.wait_ge(dt_done, 1)
                    nc.vector.tensor_tensor(z[:, :, :], q[:, :, :], u[:, :, :], ALU.mult).then_inc(dt_done, 1)
            clear(nc, sems)



TRAILS = (("PV", 4), ("W", 5), ("R", 5), ("OT", 6), ("H", 7), ("OUT", 7), ("A", 8))
SCAN_SLOTS = (0, 1, 3, 5, 6, 8, 9, 10)


def attention_slots():
    slots = [[] for _ in range(12 * B + 7)]
    for j in range(B):
        at = 12 * j
        for n, item in enumerate((("K", j, 0), ("Q", j, 0), ("Q", j, 1), ("V", j, 0))):
            slots[at + n].append(item)
        for u in range(8):
            slots[at + 4 + u] += [("S", j, u), ("C", j, u)]
            slots[at + 5 + u].append(("T", j, u))
            slots[at + 6 + u].append(("L", j, u))
        for qt in range(TT):
            for kind, trail in TRAILS:
                slots[at + 4 + 2 * qt + trail].append((kind, j, qt))
        if j < B - 1:
            slots[at + 8].append(("X", j + 1, 0))
            slots[at + 10].append(("X", j + 1, 1))
        for n, slot in enumerate(SCAN_SLOTS):
            slots[at + slot].append(("M", j, n))
    return slots


PE_ORDER = "K Q V S PV OT T OUT"
ACT_PROJ = "L H M R K Q V PV X"
ACT_UNIT = "H L M X S PV R"
DVE_PROJ = "L H A W M R K Q V X"
DVE_UNIT = "A L H S X W M C R"
SP_ORDER = "M V A"


def in_order(slots, proj, unit=None):
    out = []
    for n, items in enumerate(slots):
        ranks = (unit if unit and n % 12 >= 4 else proj).split()
        out += sorted((i for i in items if i[0] in ranks), key=lambda i: ranks.index(i[0]))
    return out


W_CUTS = ((QC, QC + KC, 1.0), (0, 2 * HD, SCALE), (2 * HD, QC, SCALE), (QC + KC, GC, 1.0))


def dve_drives(k):
    return k % 8 in (1, 4)


DVE_DRIVES = sum(dve_drives(k) for k in range(2 * NS))


def attend_and_scan(nc, d, s):
    slots = attention_slots()
    with ExitStack() as ctx:
        def sb(name, shape, dt=F32):
            return ctx.enter_context(nc.sbuf_tensor(name, shape, dt))

        def pair(name, shape):
            return sb(name + "_hi", shape, F32R), sb(name + "_lo", shape, F32R)

        def ps(name, shape):
            return ctx.enter_context(nc.psum_tensor(name, shape, F32))

        wraw = sb("wraw", [P, KT, GC])
        w = pair("w", [P, KT, GC])
        ow = pair("ow", [P, 4, HID])
        bias = sb("qk_bias", [P, 6])
        vbias = sb("v_bias", [1, VC])
        subln = sb("subln", [P, 2])
        xraw = sb("xraw", [P, KT, T])
        x = pair("x", [P, KT, T])
        qT = pair("qT", [P, 4, T])
        kT = pair("kT", [P, 2, T])
        v = pair("v", [P, TT, E2])
        prob = sb("prob", [P, 2, 2, T])
        pT = pair("pT", [P, 3, TT, P])
        junk = sb("junk", [P, E2])
        head = sb("head", [P, 2, E2])
        hT = pair("hT", [P, 4, P])
        acc = sb("acc_sb", [P, 2, HID])
        negmax = sb("negmax", [P, 2, 2])
        rowsum = sb("rowsum", [P, TT, 2, 2])
        rinv = sb("rinv", [P, 2])
        coef = sb("coef", [P, 2])
        msq = sb("msq", [P, 2, 2])
        var = sb("var", [P, 2, 2])
        rms = sb("rms", [P, 2, 2])
        tmp = sb("rms_tmp", [P, 2])
        nrm = sb("nrm", [P, 2])
        dt = sb("dt_sb", [P, CT, T])
        dtu = sb("dtu_sb", [P, CT, T])
        y = sb("y_sb", [P, CT, T])
        Bn = sb("Bn", [P, 2, T])
        Cn = sb("Cn", [P, 2, T])
        dA = sb("dA", [P, 2, 2, T])
        st = sb("state", [P, 3, 2, T])

        psBig = ps("psBig", [P, 2, 2, T])
        psT = ps("psT", [P, TT, P])
        psPV = ps("psPV", [P, 2, 2, E2])
        psO = ps("psO", [P, HID])

        zeroed = ctx.enter_context(nc.semaphore("dA_zeroed"))
        names = ("next_loaded", "b_loaded", "ow_loaded", "x_loaded", "acc_loaded0", "acc_loaded1", "acc_stored0", "acc_stored1", "w_hi", "w_lo", "ow_hi",
                 "ow_lo", "ow_col", "b_scaled", "x_hi", "x_lo", "proj_done", "proj_hi", "proj_lo", "scores_done", "max_done",
                 "exp_done", "probs_done", "comb_step", "pt_done", "pt_hi", "pt_lo", "pv_done", "sq_done",
                 "var_done", "var_step", "ln_done", "guess_done", "rms_step", "head_done", "ot_done", "ot_hi",
                 "ot_lo", "out_done", "acc_done", "u_loaded", "bc_loaded0", "bc_loaded1", "dA_done", "dbu_done", "dbu_dve", "scan_done",
                 "gated", "piece_done", "y_init", "y_stored")
        sems = [ctx.enter_context(nc.semaphore(n)) for n in names]
        S = dict(zip(names, sems))

        first_loaded = ctx.enter_context(nc.semaphore("first_loaded"))

        def load_group(sp, g, sem):
            sp.dma_start(wraw[:, :, :], d["w"][bass.ds(g, 1), :, :].rearrange("g p n -> p (g n)")
                         .rearrange("p (k n) -> p k n", k=KT)).then_inc(sem, 16)

        def load_scan(sp, g, sem):
            for buf, src in ((dt, "dt"), (dtu, "dtu")):
                sp.dma_start(buf[:, :, :].rearrange("p c t -> p (c t)"),
                             d[src][bass.ds(g, 1), :, :].rearrange("b p n -> p (b n)")).then_inc(sem, 16)

        def load_x0(sp, sem):
            sp.dma_start(xraw[:, :, :], d["xT"][0].rearrange("k p t -> p k t")).then_inc(sem, 16)

        with nc.Block() as block:
            @block.sync
            def _(sp):
                load_group(sp, 0, first_loaded)
                load_x0(sp, first_loaded)
                load_scan(sp, 0, first_loaded)
                sp.wait_ge(first_loaded, 64)

            @block.gpsimd
            def _(pool):
                nc.gpsimd.memset(dA[:, :, :, 0:1], 0.0).then_inc(zeroed, 1)
                pool.wait_ge(zeroed, 1)

        with nc.Fori(0, G) as g:
            with nc.Block(no_gpsimd_drain=True) as block:

                def wait_big_free(eng, w_):
                    if w_ >= 2:
                        j, r = divmod(w_ - 2, 12)
                        if r < 4:
                            eng.wait_ge(S["proj_hi"], 4 * j + r + 1)
                            eng.wait_ge(S["proj_lo"], 4 * j + r + 1)
                        else:
                            eng.wait_ge(S["exp_done"], 8 * j + r - 4 + 1)

                def use_of(kind, n):
                    return {"K": 0, "Q": 1 + n, "V": 3, "S": 4 + n}[kind]

                @block.sync
                def _(sp):
                    sp.dma_start(bias[:, :], d["qk_bias"][bass.ds(g, 1), :, :].rearrange("g p n -> p (g n)")) \
                        .then_inc(S["b_loaded"], 16)
                    sp.dma_start(vbias[:, :], d["v_bias"][bass.ds(g, 1), :]).then_inc(S["b_loaded"], 16)
                    sp.dma_start(subln[:, :], d["subln"]).then_inc(S["b_loaded"], 16)
                    sp.dma_start(y[:, :, :].rearrange("p c t -> p (c t)"),
                                 d["u"][bass.ds(g, 1), :, :].rearrange("b p n -> p (b n)")).then_inc(S["u_loaded"], 16)

                    def load_bc(n):
                        if n >= 2:
                            sp.wait_ge(S["piece_done"], 2 * (n - 2) + 2)
                        for buf, row in ((Bn, n), (Cn, NS + n)):
                            sp.dma_start(buf[:, n % 2, :], d["bc"][bass.ds(g, 1), row:row + 1, :]
                                         .rearrange("b n t -> (b n) t").broadcast_to([P, T])).then_inc(S[f"bc_loaded{n % 2}"], 16)

                    def load_acc(n):
                        if n >= 2:
                            sp.wait_ge(S[f"acc_stored{n % 2}"], 16 * (n // 2))
                        sp.dma_start(acc[:, n % 2, :], d["acc"][n * P:(n + 1) * P, :]).then_inc(S[f"acc_loaded{n % 2}"], 16)

                    load_bc(0)
                    load_bc(1)
                    load_acc(0)
                    load_acc(1)
                    sp.wait_ge(S["w_hi"], 4)
                    sp.wait_ge(S["w_lo"], 4)
                    sp.dma_start(wraw[:, :, 0:HID], d["ow"][bass.ds(g, 1), :, :].rearrange("g p n -> p (g n)")
                                 .rearrange("p (k n) -> p k n", k=4)).then_inc(S["ow_loaded"], 16)
                    for kind, j, n in in_order(slots, SP_ORDER):
                        if kind == "M":
                            k = 8 * j + n
                            if k % 2 == 1 and 2 <= (k + 1) // 2 < NS:
                                load_bc((k + 1) // 2)
                        elif kind == "V" and j == 1:
                            sp.wait_ge(S["ow_hi"], 4)
                            sp.wait_ge(S["ow_lo"], 4)
                            load_group(sp, (g + 1) & (G - 1), S["next_loaded"])
                        if kind == "V" and j < B - 1:
                            sp.wait_ge(S["x_hi"], 2 * (j + 1))
                            sp.wait_ge(S["x_lo"], 2 * (j + 1))
                            sp.dma_start(xraw[:, :, :], d["xT"][j + 1].rearrange("k p t -> p k t")) \
                                .then_inc(S["x_loaded"], 16)
                        elif kind == "A":
                            m = 4 * j + n
                            sp.wait_ge(S["acc_done"], m + 1)
                            sp.dma_start(d["acc"][m * P:(m + 1) * P, :], acc[:, m % 2, :]).then_inc(S[f"acc_stored{m % 2}"], 16)
                            if m + 2 < 4 * B:
                                load_acc(m + 2)
                    sp.wait_ge(S["x_lo"], 2 * B)
                    load_x0(sp, S["next_loaded"])
                    sp.wait_ge(S["dA_done"], 2 * NS)
                    sp.wait_ge(S["dbu_done"], 2 * NS - DVE_DRIVES)
                    sp.wait_ge(S["dbu_dve"], DVE_DRIVES)
                    load_scan(sp, (g + 1) & (G - 1), S["next_loaded"])
                    sp.wait_ge(S["piece_done"], 2 * NS)
                    sp.dma_start(d["y"][bass.ds(g, 1), :, :].rearrange("b p n -> p (b n)"),
                                 y[:, :, :].rearrange("p c t -> p (c t)")).then_inc(S["y_stored"], 16)
                    sp.wait_ge(S["acc_stored0"], 16 * 2 * B)
                    sp.wait_ge(S["acc_stored1"], 16 * 2 * B)
                    sp.wait_ge(S["y_stored"], 16)
                    sp.wait_ge(S["next_loaded"], 64)

                @block.tensor
                def _(pe):
                    def three(out, lhs, rhs, at_l, at_r, start, stop):
                        nc.tensor.matmul(out, at_l(lhs[0]), at_r(rhs[0]), start=start, stop=False)
                        nc.tensor.matmul(out, at_l(lhs[0]), at_r(rhs[1]), start=False, stop=False)
                        return nc.tensor.matmul(out, at_l(lhs[1]), at_r(rhs[0]), start=False, stop=stop)

                    for kind, j, n in in_order(slots, PE_ORDER):
                        if kind in ("K", "Q", "V"):
                            r = use_of(kind, n)
                            wait_big_free(pe, 12 * j + r)
                            if kind == "K":
                                pe.wait_ge(S["x_hi"], 2 * (j + 1))
                                pe.wait_ge(S["x_lo"], 2 * (j + 1))
                            if j == 0:
                                pe.wait_ge(S["w_hi"], r + 1)
                                pe.wait_ge(S["w_lo"], r + 1)
                            if kind == "V" and j == 0:
                                pe.wait_ge(S["b_loaded"], 48)
                            big = psBig[:, r % 2]
                            if kind == "V":
                                vps = big.rearrange("p a (b n) -> p (a b) n", b=2)
                                for t in range(TT):
                                    for k in range(KT):
                                        three(vps[:, t, :], x, w, lambda a: a[:, k, t * P:(t + 1) * P],
                                              lambda a: a[:, k, QC + KC:GC], k == 0, False)
                                    mm = nc.tensor.matmul(vps[:, t, :], s["ones"][0:1, :], vbias[:, :],
                                                          start=False, stop=True)
                            else:
                                c0 = QC if kind == "K" else 2 * n * HD
                                for m in range(2):
                                    for k in range(KT):
                                        mm = three(big[:, m, :], w, x,
                                                   lambda a: a[:, k, c0 + m * HD:c0 + (m + 1) * HD],
                                                   lambda a: a[:, k, :], k == 0, k == KT - 1)
                            mm.then_inc(S["proj_done"], 1)
                        elif kind == "S":
                            qt, h = divmod(n, 2)
                            wait_big_free(pe, 12 * j + 4 + n)
                            if n == 0:
                                pe.wait_ge(S["proj_hi"], 4 * j + 4)
                                pe.wait_ge(S["proj_lo"], 4 * j + 4)
                            wd = (qt + 1) * P
                            for m in range(2):
                                out = psBig[:, n % 2, m, 0:wd]
                                three(out, qT, kT, lambda a: a[:, 2 * h + m, qt * P:wd], lambda a: a[:, m, 0:wd],
                                      True, False)
                                mm = nc.tensor.matmul(psBig[:, n % 2, m, qt * P:wd], s["identb"][:, :], s["maskb"][:, :],
                                                      start=False, stop=True)
                            mm.then_inc(S["scores_done"], 1)
                        elif kind == "T":
                            qt = n // 2
                            pe.wait_ge(S["probs_done"], 8 * j + n + 1)
                            if 8 * j + n > 0:
                                pe.wait_ge(S["pt_hi"], 8 * j + n)
                                pe.wait_ge(S["pt_lo"], 8 * j + n)
                            for kt in range(qt + 1):
                                mm = nc.tensor.transpose(psT[:, kt, :], prob[:, n % 2, 0, kt * P:(kt + 1) * P],
                                                         s["ident"][:, :])
                            mm.then_inc(S["pt_done"], 1)
                        elif kind == "PV":
                            m = 4 * j + n
                            pe.wait_ge(S["pt_hi"], 2 * m + 2)
                            pe.wait_ge(S["pt_lo"], 2 * m + 2)
                            if m > 1:
                                pe.wait_ge(S["head_done"], m - 1)
                            for h in range(2):
                                for kt in range(n + 1):
                                    mm = three(psPV[:, n % 2, h, :], pT, v, lambda a: a[:, (2 * m + h) % 3, kt, :],
                                               lambda a: a[:, kt, :],
                                               kt == 0, kt == n)
                            mm.then_inc(S["pv_done"], 1)
                        elif kind == "OT":
                            m = 4 * j + n
                            pe.wait_ge(S["head_done"], m + 1)
                            if m > 0:
                                pe.wait_ge(S["acc_done"], m)
                            for r in range(4):
                                mm = nc.tensor.transpose(psO[:, r * P:(r + 1) * P], head[:, r // 2, (r % 2) * P:(r % 2 + 1) * P],
                                                         s["ident"][:, :])
                            mm.then_inc(S["ot_done"], 1)
                        elif kind == "OUT":
                            m = 4 * j + n
                            if m == 0:
                                pe.wait_ge(S["ow_hi"], 4)
                                pe.wait_ge(S["ow_lo"], 4)
                            pe.wait_ge(S["ot_hi"], m + 1)
                            pe.wait_ge(S["ot_lo"], m + 1)
                            for r in range(4):
                                mm = three(psO[:, :], hT, ow, lambda a: a[:, r, :], lambda a: a[:, r, :],
                                           r == 0, r == 3)
                            mm.then_inc(S["out_done"], 1)

                def split_x(eng, j, n):
                    if n == 0 and j > 0:
                        eng.wait_ge(S["x_loaded"], 16 * j)
                        eng.wait_ge(S["proj_done"], 4 * j)

                @block.scalar
                def _(act):
                    def x_high(j, n):
                        split_x(act, j, n)
                        nc.scalar.copy(x[0][:, 2 * n:2 * n + 2, :], xraw[:, 2 * n:2 * n + 2, :]).then_inc(S["x_hi"], 1)

                    nc.scalar.preload_act_table_set("natural_log_exp_and_others")
                    for n, (c0, c1, f) in enumerate(W_CUTS):
                        nc.scalar.activation(w[0][:, :, c0:c1], wraw[:, :, c0:c1], ACT.Copy, scale=f) \
                            .then_inc(S["w_hi"], 1)
                        if n == 0:
                            x_high(0, 0)
                            x_high(0, 1)
                    act.wait_ge(S["b_scaled"], 1)
                    for kind, j, n in in_order(slots, ACT_PROJ, ACT_UNIT):
                        if kind in ("K", "Q", "V"):
                            r = use_of(kind, n)
                            if kind == "V" and j == 0:
                                act.wait_ge(S["ow_loaded"], 16)
                                act.wait_ge(S["ow_col"], 1)
                                for t in range(4):
                                    nc.scalar.activation(ow[0][:, t, :], wraw[:, t, 0:HID], ACT.Copy,
                                                         scale=subln[:, t % 2:t % 2 + 1]).then_inc(S["ow_hi"], 1)
                            act.wait_ge(S["proj_done"], 4 * j + r + 1)
                            big = psBig[:, r % 2]
                            if kind == "V":
                                ins = nc.scalar.copy(v[0][:, :, :].rearrange("p a b -> p (a b)"),
                                                     big.rearrange("p a b -> p (a b)"))
                            else:
                                dst, col = (kT, 4) if kind == "K" else (qT, 2 * n)
                                base = 0 if kind == "K" else 2 * n
                                for m in range(2):
                                    ins = nc.scalar.activation(dst[0][:, base + m, :], big[:, m, :], ACT.Identity,
                                                               bias=bias[:, col + m:col + m + 1])
                            ins.then_inc(S["proj_hi"], 1)
                        elif kind == "X":
                            x_high(j, n)
                        elif kind == "S":
                            u = 8 * j + n
                            wd = (n // 2 + 1) * P
                            act.wait_ge(S["max_done"], u + 1)
                            if u >= 2:
                                act.wait_ge(S["pt_done"], u - 1)
                            for m in range(2):
                                ins = nc.scalar.activation(prob[:, n % 2, m, 0:wd], psBig[:, n % 2, m, 0:wd], ACT.Exp,
                                                           bias=negmax[:, n % 2, m:m + 1],
                                                           accum_out=rowsum[:, n // 2, n % 2, m:m + 1])
                            ins.then_inc(S["exp_done"], 1)
                        elif kind == "L":
                            u = 8 * j + n
                            act.wait_ge(S["pt_done"], u + 1)
                            if u >= 3:
                                act.wait_ge(S["pv_done"], (u - 3) // 2 + 1)
                            nc.scalar.copy(pT[0][:, u % 3, 0:n // 2 + 1, :], psT[:, 0:n // 2 + 1, :]) \
                                .then_inc(S["pt_hi"], 1)
                        elif kind == "PV":
                            m = 4 * j + n
                            act.wait_ge(S["pv_done"], m + 1)
                            for h in range(2):
                                if h or m:
                                    act.wait_ge(S["sq_done"], 2 * m + h)
                                nc.scalar.activation(junk[:, :], psPV[:, n % 2, h, :], ACT.Square,
                                                     accum_out=msq[:, n % 2, h:h + 1]).then_inc(S["sq_done"], 1)
                        elif kind == "R":
                            m = 4 * j + n
                            act.wait_ge(S["var_done"], m + 1)
                            nc.scalar.activation(rms[:, n % 2, :], var[:, n % 2, :], ACT.Ln).then_inc(S["ln_done"], 1)
                            act.wait_ge(S["ln_done"], m + 1)
                            nc.scalar.activation(rms[:, n % 2, :], rms[:, n % 2, :], ACT.Exp, scale=-0.5) \
                                .then_inc(S["guess_done"], 1)
                        elif kind == "H":
                            m = 4 * j + n
                            act.wait_ge(S["ot_done"], m + 1)
                            if m > 0:
                                act.wait_ge(S["out_done"], m)
                            nc.scalar.copy(hT[0][:, :, :].rearrange("p r t -> p (r t)"), psO[:, :]).then_inc(S["ot_hi"], 1)
                        elif kind == "M":
                            k = 8 * j + n
                            state, half = divmod(k, 2)
                            if k >= 2:
                                act.wait_ge(S["scan_done"], k - 1)
                            for c in range(2):
                                ct = 2 * half + c
                                ins = nc.scalar.activation(dA[:, k % 2, c, 1:T], dt[:, ct, 1:T], ACT.Exp,
                                                           scale=s["negA"][:, ct * NS + state:ct * NS + state + 1])
                            ins.then_inc(S["dA_done"], 1)

                def drive(eng, unit, k, done):
                    state, half = divmod(k, 2)
                    eng.wait_ge(S[f"bc_loaded{state % 2}"], 32 * (state // 2 + 1))
                    if k >= 3:
                        eng.wait_ge(S["piece_done"], k - 2)
                    unit.tensor_tensor(st[:, k % 3], dtu[:, 2 * half:2 * half + 2, :],
                                       Bn[:, state % 2, :].unsqueeze(1).broadcast_to([P, 2, T]),
                                       ALU.mult).then_inc(done, 1)

                def scan_piece(dve, k):
                    dve.wait_ge(S["dA_done"], k + 1)
                    if dve_drives(k):
                        dve.wait_ge(S["dbu_dve"], sum(dve_drives(i) for i in range(k + 1)))
                    else:
                        dve.wait_ge(S["dbu_done"], sum(not dve_drives(i) for i in range(k + 1)))
                    flat = st[:, k % 3].rearrange("p c t -> p (c t)")
                    nc.vector.tensor_tensor_scan(flat, dA[:, k % 2].rearrange("p c t -> p (c t)"), flat, 0.0,
                                                 ALU.mult, ALU.add).then_inc(S["scan_done"], 1)

                @block.vector
                def _(dve):
                    def newton(i, j, n):
                        m = 4 * j + n
                        guess, v_ = rms[:, n % 2, :], var[:, n % 2, :]
                        if i == 0:
                            dve.wait_ge(S["guess_done"], m + 1)
                            ins = nc.vector.scalar_tensor_tensor(tmp[:, :], guess, -0.5, guess, ALU.mult, ALU.mult)
                        elif i == 1:
                            dve.wait_ge(S["rms_step"], 3 * m + 1)
                            ins = nc.vector.tensor_tensor(tmp[:, :], tmp[:, :], v_, ALU.mult)
                        else:
                            dve.wait_ge(S["rms_step"], 3 * m + 2)
                            ins = nc.vector.scalar_tensor_tensor(guess, tmp[:, :], 1.5, guess, ALU.add, ALU.mult)
                        ins.then_inc(S["rms_step"], 1)

                    def scale_heads(j, n):
                        m = 4 * j + n
                        dve.wait_ge(S["rms_step"], 3 * m + 3)
                        if m > 0:
                            dve.wait_ge(S["ot_done"], m)
                        for h in range(2):
                            ins = nc.vector.tensor_scalar(head[:, h, :], psPV[:, n % 2, h, :], rms[:, n % 2, h:h + 1],
                                                          None, ALU.mult)
                        ins.then_inc(S["head_done"], 1)

                    def f32(ap):
                        return ap.bitcast(F32)

                    def x_low(j, n):
                        split_x(dve, j, n)
                        dve.wait_ge(S["x_hi"], 2 * j + n + 1)
                        nc.vector.tensor_tensor(x[1][:, 2 * n:2 * n + 2, :], xraw[:, 2 * n:2 * n + 2, :],
                                                f32(x[0][:, 2 * n:2 * n + 2, :]), ALU.subtract).then_inc(S["x_lo"], 1)

                    for n, (c0, c1, f) in enumerate(W_CUTS):
                        dve.wait_ge(S["w_hi"], n + 1)
                        nc.vector.scalar_tensor_tensor(w[1][:, :, c0:c1], wraw[:, :, c0:c1], f,
                                                       f32(w[0][:, :, c0:c1]), ALU.mult, ALU.subtract) \
                            .then_inc(S["w_lo"], 1)
                        if n == 0:
                            x_low(0, 0)
                            x_low(0, 1)
                    dve.wait_ge(S["b_loaded"], 48)
                    nc.vector.tensor_scalar(bias[:, 0:4], bias[:, 0:4], SCALE, None, ALU.mult) \
                        .then_inc(S["b_scaled"], 1)
                    dve.wait_ge(S["b_scaled"], 1)
                    nc.vector.tensor_scalar(subln[:, :], subln[:, :], 1.0 - LAMBDA_INIT, None, ALU.mult) \
                        .then_inc(S["ow_col"], 1)
                    for kind, j, n in in_order(slots, DVE_PROJ, DVE_UNIT):
                        if kind in ("K", "Q", "V"):
                            r = use_of(kind, n)
                            if kind == "V" and j == 0:
                                for t in range(4):
                                    dve.wait_ge(S["ow_hi"], t + 1)
                                    nc.vector.scalar_tensor_tensor(ow[1][:, t, :], wraw[:, t, 0:HID],
                                                                   subln[:, t % 2:t % 2 + 1], f32(ow[0][:, t, :]),
                                                                   ALU.mult, ALU.subtract).then_inc(S["ow_lo"], 1)
                            dve.wait_ge(S["proj_hi"], 4 * j + r + 1)
                            big = psBig[:, r % 2]
                            if kind == "V":
                                ins = nc.vector.tensor_tensor(v[1][:, :, :].rearrange("p a b -> p (a b)"),
                                                              big.rearrange("p a b -> p (a b)"),
                                                              f32(v[0][:, :, :].rearrange("p a b -> p (a b)")),
                                                              ALU.subtract)
                            else:
                                dst, col = (kT, 4) if kind == "K" else (qT, 2 * n)
                                base = 0 if kind == "K" else 2 * n
                                for m in range(2):
                                    ins = nc.vector.scalar_tensor_tensor(
                                        dst[1][:, base + m, :], big[:, m, :], bias[:, col + m:col + m + 1],
                                        f32(dst[0][:, base + m, :]), ALU.add, ALU.subtract)
                            ins.then_inc(S["proj_lo"], 1)
                        elif kind == "X":
                            x_low(j, n)
                        elif kind == "S":
                            u = 8 * j + n
                            wd = (n // 2 + 1) * P
                            dve.wait_ge(S["scores_done"], u + 1)
                            nc.vector.reduce_max(negmax[:, n % 2, :], psBig[:, n % 2, :, 0:wd], AX.X, negate=True) \
                                .then_inc(S["max_done"], 1)
                        elif kind == "C":
                            u = 8 * j + n
                            qt, h = divmod(n, 2)
                            wd = (qt + 1) * P
                            due = (n - 5) // 2 if n in (5, 7) else None
                            sums = rowsum[:, qt, h, :]
                            dve.wait_ge(S["exp_done"], u + 1)
                            nc.vector.reciprocal(rinv[:, n % 2:n % 2 + 1], sums[:, 1:2]).then_inc(S["comb_step"], 1)
                            if due is not None:
                                newton(0, j, due)
                            dve.wait_ge(S["comb_step"], 2 * u + 1)
                            nc.vector.scalar_tensor_tensor(coef[:, n % 2:n % 2 + 1], rinv[:, n % 2:n % 2 + 1],
                                                           s["neglam"][:, :], sums[:, 0:1],
                                                           ALU.mult, ALU.mult).then_inc(S["comb_step"], 1)
                            if due is not None:
                                newton(1, j, due)
                            dve.wait_ge(S["comb_step"], 2 * u + 2)
                            nc.vector.scalar_tensor_tensor(prob[:, n % 2, 0, 0:wd], prob[:, n % 2, 1, 0:wd],
                                                           coef[:, n % 2:n % 2 + 1], prob[:, n % 2, 0, 0:wd],
                                                           ALU.mult, ALU.add).then_inc(S["probs_done"], 1)
                            if due is not None:
                                newton(2, j, due)
                                scale_heads(j, due)
                        elif kind == "L":
                            u = 8 * j + n
                            dve.wait_ge(S["pt_hi"], u + 1)
                            nc.vector.tensor_tensor(pT[1][:, u % 3, 0:n // 2 + 1, :], psT[:, 0:n // 2 + 1, :],
                                                    f32(pT[0][:, u % 3, 0:n // 2 + 1, :]), ALU.subtract) \
                                .then_inc(S["pt_lo"], 1)
                        elif kind == "W":
                            m = 4 * j + n
                            sums = rowsum[:, n, :, 0]
                            nc.vector.scalar_tensor_tensor(nrm[:, :], sums, EPS, sums, ALU.mult, ALU.mult) \
                                .then_inc(S["var_step"], 1)
                            dve.wait_ge(S["sq_done"], 2 * m + 2)
                            dve.wait_ge(S["var_step"], m + 1)
                            nc.vector.scalar_tensor_tensor(var[:, n % 2, :], msq[:, n % 2, :], 1.0 / E2, nrm[:, :],
                                                           ALU.mult, ALU.add).then_inc(S["var_done"], 1)
                        elif kind == "R" and n >= 2:
                            for i in range(3):
                                newton(i, j, n)
                            scale_heads(j, n)
                        elif kind == "H":
                            m = 4 * j + n
                            dve.wait_ge(S["ot_hi"], m + 1)
                            nc.vector.tensor_tensor(hT[1][:, :, :].rearrange("p r t -> p (r t)"), psO[:, :],
                                                    f32(hT[0][:, :, :].rearrange("p r t -> p (r t)")),
                                                    ALU.subtract).then_inc(S["ot_lo"], 1)
                        elif kind == "A":
                            m = 4 * j + n
                            dve.wait_ge(S["out_done"], m + 1)
                            dve.wait_ge(S[f"acc_loaded{m % 2}"], 16 * (m // 2 + 1))
                            nc.vector.tensor_tensor(acc[:, m % 2, :], psO[:, :], acc[:, m % 2, :], ALU.add) \
                                .then_inc(S["acc_done"], 1)
                        elif kind == "M":
                            k = 8 * j + n
                            if k == 0:
                                dve.wait_ge(S["u_loaded"], 16)
                                for c in range(CT):
                                    nc.vector.tensor_scalar(y[:, c, :], y[:, c, :], s["Dcol"][:, c:c + 1], None,
                                                            ALU.mult).then_inc(S["y_init"], 1)
                            if dve_drives(k):
                                drive(dve, nc.vector, k, S["dbu_dve"])
                            if k > 0:
                                scan_piece(dve, k - 1)
                    scan_piece(dve, 2 * NS - 1)

                @block.gpsimd
                def _(pool):
                    drive(pool, nc.gpsimd, 0, S["dbu_done"])
                    pool.wait_ge(S["y_init"], CT)
                    for k in range(2 * NS):
                        state, half = divmod(k, 2)
                        pool.wait_ge(S["scan_done"], k + 1)
                        nc.gpsimd.tensor_tensor(st[:, k % 3], st[:, k % 3],
                                                Cn[:, state % 2, :].unsqueeze(1).broadcast_to([P, 2, T]),
                                                ALU.mult).then_inc(S["gated"], 1)
                        pool.wait_ge(S["gated"], k + 1)
                        nc.gpsimd.tensor_tensor(y[:, 2 * half:2 * half + 2, :], y[:, 2 * half:2 * half + 2, :],
                                                st[:, k % 3], ALU.add).then_inc(S["piece_done"], 1)
                        if k + 2 < 2 * NS and not dve_drives(k + 2):
                            drive(pool, nc.gpsimd, k + 2, S["dbu_done"])
            clear(nc, sems)



PREPARE = {
    3: (("x0", 0, 0), ("x0", 0, 1)), 4: (("x0", 0, 2), ("x0", 0, 3)), 5: (("stats", 1, 0),),
    6: (("stats", 1, 1), ("stats", 1, 2)), 7: (("stats", 1, 3), ("var", 1, 0)), 9: (("guess", 1, 0), ("newton", 1, 0),
    ("norm", 1, 0), ("norm", 1, 1)), 10: (("norm", 1, 2), ("norm", 1, 3)), 11: (("tanh", 0, 0), ("tanh", 0, 1), ("yx", 0, 0)),
    12: (("yx", 0, 1), ("gmul", 0, 0)), 13: (("yx", 0, 2), ("gmul", 0, 1)), 14: (("tanh", 0, 2), ("yx", 0, 3), ("gmul", 0, 2)),
    15: (("tanh", 0, 3), ("gmul", 0, 3)), 18: (("turn", 0, 0), ("stats", 2, 0)), 19: (("turn", 0, 1), ("stats", 2, 1)),
    20: (("turn", 0, 2), ("stats", 2, 2)), 21: (("turn", 0, 3), ("stats", 2, 3), ("var", 2, 0)),
    23: (("guess", 2, 0), ("newton", 2, 0), ("norm", 2, 0), ("norm", 2, 1)), 24: (("norm", 2, 2), ("norm", 2, 3)),
    27: (("x2T", 0, 0),), 28: (("x2T", 0, 1),), 29: (("x2T", 0, 2),), 30: (("x2T", 0, 3),),
    32: (("gate", 0, 0),), 33: (("gate", 0, 1),),
}
PSUM_KINDS = ("turn", "x2T", "gate")
UNITS = [("s", 0, t) for t in range(2)] + [("e", e, t) for e in range(NE) for t in range(2)]
NU = len(UNITS)
LAG = 3


def expert_phase(nc, d, s):
    with ExitStack() as ctx:
        def sb(name, shape, dt=F32):
            return ctx.enter_context(nc.sbuf_tensor(name, shape, dt))

        def pair(name, shape):
            return sb(name + "_hi", shape, F32R), sb(name + "_lo", shape, F32R)

        def ps(name, shape):
            return ctx.enter_context(nc.psum_tensor(name, shape, F32))

        def f32(ap):
            return ap.bitcast(F32)

        cw = pair("cw", [P, WCOLS])
        x1 = sb("x1", [P, TT, HID])
        x3 = sb("x3", [P, TT, HID])
        yg = sb("yg", [P, CT, T])
        gate = sb("gate", [P, 2, HID])
        outb = sb("outb", [P, HID])
        rbias = sb("rbias", [P, NE])
        x2T = pair("x2T", [P, KT, T])
        xl = pair("xl", [P, T])
        lat = xl
        wb = sb("wb", [P, 3, T])
        act_ = sb("act_buf", [P, 3, T])
        hid = pair("hid", [P, 3, T])
        stats = sb("stats", [P, TT, 6])
        mv = sb("mv", [P, TT, 2])
        var = sb("mvar", [P, TT])
        rstd = sb("rstd", [P, TT])
        tmp = sb("mtmp", [P, TT])
        ex = sb("ex", [P, TT, NE])
        prb = sb("prb", [P, TT, NE])
        sel = sb("sel", [P, TT, NE])
        top = sb("top", [P, TT, 8])
        wsum = sb("wsum", [P, TT])
        logits = gate[0:NE, 1, :]
        wT = gate[0:NE, 0, :]
        psGU = ps("psGU", [P, 3, 2, T])
        psA = ps("psA", [P, T])
        psM = ps("psM", [P, T])

        c_load = ctx.enter_context(nc.semaphore("rows_loaded"))
        CH = 2 * T
        chunks = [(c, min(c + CH, WCOLS)) for c in range(0, WCOLS, CH)]
        stage = (x3[:, 0:2, :], x3[:, 2:4, :], act_[:, 0:2, :])
        NST = len(stage)
        w_load = [ctx.enter_context(nc.semaphore(f"cw_loaded{n}")) for n in range(NST)]
        w_hi = ctx.enter_context(nc.semaphore("cw_hi"))
        w_lo = ctx.enter_context(nc.semaphore("cw_lo"))

        names = ("acc_loaded", "y_loaded", "x0_done", "stat_step", "var_done", "ln_done", "guess_done", "norm_done",
                 "yx_done", "tanh_done", "yg_done", "ygT_done", "x2_added", "x2_done", "x2T_done", "x2T_hi", "x2T_lo",
                 "logits_ps", "logits_sb", "logits_done", "rexp_done", "route_step", "route_done", "wT_ps", "wT_sb", "wT_stored",
                 "wb_loaded0", "wb_loaded1", "wb_loaded2", "xl_done", "xl_hi", "xl_lo", "up_done", "relu_done",
                 "square_done", "weighted", "prod_done", "hid_hi", "hid_lo", "shared_ps", "shared_added", "down_done",
                 "lat_hi", "lat_lo", "out_ps", "x3_done", "out_done", "stored")
        sems = [ctx.enter_context(nc.semaphore(n)) for n in names]
        S = dict(zip(names, sems))

        def staged(n):
            a, z = chunks[n]
            return stage[n % NST].rearrange("p a b -> p (a b)")[:, 0:z - a]


        def load_x(sp, b):
            sp.dma_start(x1[:, :, :], d["acc"].rearrange("(b t p) n -> b p t n", b=B, p=P)[bass.ds(b, 1)]
                         .rearrange("b p t n -> p (b t) n")).then_inc(S["acc_loaded"], 16)

        def load_y(sp, b):
            sp.dma_start(yg[:, :, :].rearrange("p c t -> p (c t)"),
                         d["y"][bass.ds(b, 1), :, :].rearrange("b p n -> p (b n)")).then_inc(S["y_loaded"], 16)

        def three(out, lhs, rhs, at_l, at_r, start, stop):
            nc.tensor.matmul(out, at_l(lhs[0]), at_r(rhs[0]), start=start, stop=False)
            nc.tensor.matmul(out, at_l(lhs[0]), at_r(rhs[1]), start=False, stop=False)
            return nc.tensor.matmul(out, at_l(lhs[1]), at_r(rhs[0]), start=False, stop=stop)

        def prepare_pe(pe, kind, i, n):
            if kind == "turn":
                if n == 0:
                    pe.wait_ge(S["yg_done"], CT)
                else:
                    pe.wait_ge(S["x2_added"], n)
                for c in range(CT):
                    mm = nc.tensor.transpose(psM[:, c * P:(c + 1) * P], yg[:, c, n * P:(n + 1) * P], s["ident"][:, :])
                mm.then_inc(S["ygT_done"], 1)
            elif kind == "x2T":
                if n == 0:
                    pe.wait_ge(S["x2_done"], TT)
                else:
                    pe.wait_ge(S["x2T_hi"], n)
                    pe.wait_ge(S["x2T_lo"], n)
                for t in range(TT):
                    mm = nc.tensor.transpose(psM[:, t * P:(t + 1) * P], x1[:, t, n * P:(n + 1) * P], s["ident"][:, :])
                mm.then_inc(S["x2T_done"], 1)
            elif kind == "gate" and n == 0:
                pe.wait_ge(S["x2T_hi"], KT)
                pe.wait_ge(S["x2T_lo"], KT)
                for k in range(KT):
                    mm = three(psM[0:NE, :], cw, x2T, lambda a: a[:, WGT + k * NE:WGT + (k + 1) * NE],
                               lambda a: a[:, k, :], k == 0, k == KT - 1)
                mm.then_inc(S["logits_ps"], 1)
            elif kind == "gate":
                pe.wait_ge(S["logits_sb"], 1)
                for t in range(TT):
                    mm = nc.tensor.transpose(psM[:, t * NE:(t + 1) * NE], logits[:, t * P:(t + 1) * P],
                                             s["ident"][0:NE, 0:NE])
                mm.then_inc(S["logits_done"], 1)

        def guess(act, i):
            act.wait_ge(S["var_done"], i)
            nc.scalar.activation(rstd[:, :], var[:, :], ACT.Ln).then_inc(S["ln_done"], 1)
            act.wait_ge(S["ln_done"], i)
            nc.scalar.activation(rstd[:, :], rstd[:, :], ACT.Exp, scale=-0.5).then_inc(S["guess_done"], 1)

        def prepare_act(act, kind, i, n):
            if kind == "guess":
                guess(act, i)
            elif kind == "tanh":
                act.wait_ge(S["norm_done"], n + 1)
                if n >= 2:
                    act.wait_ge(S["yg_done"], n - 1)
                nc.scalar.activation(gate[:, n % 2, :], x1[:, n, :], ACT.Tanh, scale=0.5).then_inc(S["tanh_done"], 1)
                if n == CT - 1:
                    nc.scalar.preload_act_table_set("natural_log_exp_and_others")
            elif kind == "x2T":
                act.wait_ge(S["x2T_done"], n + 1)
                nc.scalar.copy(x2T[0][:, n, :], psM[:, :]).then_inc(S["x2T_hi"], 1)
            elif kind == "gate" and n == 0:
                act.wait_ge(S["logits_ps"], 1)
                nc.scalar.copy(logits, psM[0:NE, :]).then_inc(S["logits_sb"], 1)
            elif kind == "gate":
                act.wait_ge(S["logits_done"], 1)
                nc.scalar.activation(ex[:, :, :].rearrange("p a b -> p (a b)"), psM[:, 0:TT * NE], ACT.Exp,
                                     scale=-1.0).then_inc(S["rexp_done"], 1)

        def tile_stats(dve, step, x, t, ready):
            dve.wait_ge(ready, t + 1)
            step(nc.vector.bn_stats(stats[:, t, :], x[:, t, :]))
            step(nc.vector.bn_aggr(mv[:, t, :], stats[:, t, :]))

        def variance(dve):
            nc.vector.tensor_scalar(var[:, :], mv[:, :, 1], EPS, None, ALU.add).then_inc(S["var_done"], 1)

        def refine(dve, step, i):
            dve.wait_ge(S["guess_done"], i)
            rsqrt_newton(nc.vector, step, rstd[:, :], var[:, :], tmp[:, :])

        def normalise(x, t, done):
            nc.vector.tensor_scalar(x[:, t, :], x[:, t, :], mv[:, t, 0:1], rstd[:, t:t + 1],
                                    ALU.subtract, ALU.mult).then_inc(done, 1)

        def prepare_dve(dve, step, kind, i, n):
            if kind == "stats":
                tile_stats(dve, step, x1, n, S["x0_done" if i == 1 else "x2_added"])
            elif kind == "var":
                variance(dve)
            elif kind == "newton":
                refine(dve, step, i)
            elif kind == "norm":
                normalise(x1, n, S["norm_done" if i == 1 else "x2_done"])
            elif kind == "gmul":
                dve.wait_ge(S["tanh_done"], n + 1)
                dve.wait_ge(S["yx_done"], n + 1)
                nc.vector.scalar_tensor_tensor(yg[:, n, :], gate[:, n % 2, :], 1.0, yg[:, n, :], ALU.add, ALU.mult) \
                    .then_inc(S["yg_done"], 1)
            elif kind == "turn":
                dve.wait_ge(S["ygT_done"], n + 1)
                nc.vector.scalar_tensor_tensor(x1[:, n, :], psM[:, :], 0.5, x1[:, n, :], ALU.mult, ALU.add) \
                    .then_inc(S["x2_added"], 1)
            elif kind == "x2T":
                dve.wait_ge(S["x2T_hi"], n + 1)
                nc.vector.tensor_tensor(x2T[1][:, n, :], psM[:, :], f32(x2T[0][:, n, :]), ALU.subtract) \
                    .then_inc(S["x2T_lo"], 1)

        def prepare_pool(pool, kind, i, n):
            if kind == "x0":
                pool.wait_ge(S["acc_loaded"], 16)
                nc.gpsimd.tensor_tensor(x1[:, n, :], x1[:, n, :], outb[:, :], ALU.add).then_inc(S["x0_done"], 1)
            elif kind == "yx":
                pool.wait_ge(S["y_loaded"], 16)
                pool.wait_ge(S["norm_done"], n + 1)
                nc.gpsimd.tensor_tensor(yg[:, n, :], yg[:, n, :], x1[:, n, :], ALU.mult).then_inc(S["yx_done"], 1)

        pieces = [p for n in sorted(PREPARE) for p in PREPARE[n]]

        with nc.Block() as block:
            @block.sync
            def _(sp):
                sp.dma_start(outb[:, :], d["out_b"].broadcast_to([P, HID])).then_inc(c_load, 16)
                sp.dma_start(rbias[:, :], d["route_b"].broadcast_to([P, NE])).then_inc(c_load, 16)
                load_x(sp, 0)
                load_y(sp, 0)
                for n, (a, z) in enumerate(chunks):
                    if n >= NST:
                        sp.wait_ge(w_lo, n - NST + 1)
                    sp.dma_start(staged(n), d["cw"][:, a:z]).then_inc(w_load[n % NST], 16)

            @block.tensor
            def _(pe):
                pe.wait_ge(w_hi, 1)
                pe.wait_ge(w_lo, 1)
                for piece in pieces:
                    prepare_pe(pe, *piece)

            @block.scalar
            def _(act):
                nc.scalar.preload_act_table_set("natural_log_exp_and_others")
                mine = [p for p in pieces if p[0] in ("guess", "tanh", "x2T", "gate")]
                for n, (a, z) in enumerate(chunks):
                    act.wait_ge(w_load[n % NST], 16 * (n // NST + 1))
                    nc.scalar.copy(cw[0][:, a:z], staged(n)).then_inc(w_hi, 1)
                    if n >= 4 and n - 4 < len(mine):
                        prepare_act(act, *mine[n - 4])
                for piece in mine[len(chunks) - 4:]:
                    prepare_act(act, *piece)

            @block.gpsimd
            def _(pool):
                pool.wait_ge(c_load, 32)
                for n in range(TT):
                    prepare_pool(pool, "x0", 0, n)
                for n, (a, z) in enumerate(chunks):
                    pool.wait_ge(w_hi, n + 1)
                    nc.gpsimd.tensor_tensor(cw[1][:, a:z], staged(n), f32(cw[0][:, a:z]), ALU.subtract) \
                        .then_inc(w_lo, 1)
                    if 3 <= n < 3 + CT:
                        prepare_pool(pool, "yx", 0, n - 3)

            @block.vector
            def _(dve):
                step = chained(dve, S["stat_step"])
                for piece in pieces:
                    prepare_dve(dve, step, *piece)
        clear(nc, sems)

        with nc.Fori(0, B) as b:
            with nc.Block(no_gpsimd_drain=True) as block:
                @block.sync
                def _(sp):
                    load_y(sp, (b + 1) & (B - 1))
                    sp.wait_ge(S["wT_sb"], 1)
                    sp.dma_start(d["wT"], wT).then_inc(S["wT_stored"], 16)
                    sp.wait_ge(S["wT_stored"], 16)
                    for e in range(NE):
                        if e >= 3:
                            sp.wait_ge(S["weighted"], 2 * (e - 2))
                        sp.dma_start(wb[:, e % 3, :], d["wT"][e:e + 1, :].broadcast_to([P, T])) \
                            .then_inc(S[f"wb_loaded{e % 3}"], 16)
                        if e == 2:
                            sp.wait_ge(S["shared_added"], TT)
                            load_x(sp, (b + 1) & (B - 1))
                    for t in range(TT):
                        sp.wait_ge(S["out_done"], t + 1)
                        sp.dma_start(d["out"].rearrange("(b t p) n -> b t p n", b=B, p=P)[bass.ds(b, 1), t]
                                     .rearrange("b p n -> (b p) n"), x3[:, t, :]).then_inc(S["stored"], 16)
                    sp.wait_ge(S["stored"], 16 * TT)

                @block.tensor
                def _(pe):
                    def up(n):
                        kind, e, t = UNITS[n]
                        if n >= 3:
                            pe.wait_ge(S["prod_done"], n - 2)
                        if kind == "s":
                            for gu, w0 in ((0, SWG), (1, SW1)):
                                for k in range(KT):
                                    mm = three(psGU[:, n % 3, gu, :], cw, x2T,
                                               lambda a: a[:, w0 + k * 256 + t * P:w0 + k * 256 + (t + 1) * P],
                                               lambda a: a[:, k, :], k == 0, k == KT - 1)
                        else:
                            for gu, w0 in ((0, RWG), (1, RW1)):
                                mm = three(psGU[:, n % 3, gu, :], cw, xl,
                                           lambda a: a[:, w0 + e * 256 + t * P:w0 + e * 256 + (t + 1) * P],
                                           lambda a: a[:, :], True, True)
                        mm.then_inc(S["up_done"], 1)

                    def shared_down():
                        pe.wait_ge(S["hid_hi"], 2)
                        pe.wait_ge(S["hid_lo"], 2)
                        for t in range(TT):
                            if t >= 2:
                                pe.wait_ge(S["shared_added"], t - 1)
                            for h in range(2):
                                mm = three((psM, psA)[t % 2][:, :], hid, cw, lambda a: a[:, h, t * P:(t + 1) * P],
                                           lambda a: a[:, SW2 + h * HID:SW2 + (h + 1) * HID], h == 0, h == 1)
                            mm.then_inc(S["shared_ps"], 1)

                    def down(n):
                        _, e, t = UNITS[n]
                        pe.wait_ge(S["hid_hi"], n + 1)
                        pe.wait_ge(S["hid_lo"], n + 1)
                        if n == 2:
                            pe.wait_ge(S["shared_added"], TT)
                        mm = three(psA[:, :], cw, hid,
                                   lambda a: a[:, RW2 + (2 * e + t) * LAT:RW2 + (2 * e + t + 1) * LAT],
                                   lambda a: a[:, n % 3, :], n == 2, n == NU - 1)
                        mm.then_inc(S["down_done"], 1)

                    for n in range(NU):
                        if n == 2:
                            pe.wait_ge(S["wT_sb"], 1)
                            for k in range(KT):
                                mm = three(psM[:, :], cw, x2T, lambda a: a[:, WDN + k * LAT:WDN + (k + 1) * LAT],
                                           lambda a: a[:, k, :], k == 0, k == KT - 1)
                            mm.then_inc(S["xl_done"], 1)
                            pe.wait_ge(S["xl_hi"], 1)
                            pe.wait_ge(S["xl_lo"], 1)
                        up(n)
                        if n == 0:
                            pe.wait_ge(S["route_done"], 1)
                            for t in range(TT):
                                mm = nc.tensor.transpose(psM[0:NE, t * P:(t + 1) * P], sel[:, t, :], s["ident"][:, :])
                            mm.then_inc(S["wT_ps"], 1)
                        elif n == 3:
                            shared_down()
                        for piece in PREPARE.get(n, ()):
                            prepare_pe(pe, *piece)
                        if n - LAG >= 2:
                            down(n - LAG)
                    for n in range(NU - LAG, NU):
                        down(n)
                    pe.wait_ge(S["lat_hi"], 1)
                    pe.wait_ge(S["lat_lo"], 1)
                    for t in range(TT):
                        mm = three(psGU[:, t // 2, t % 2, :], lat, cw, lambda a: a[:, t * P:(t + 1) * P],
                                   lambda a: a[:, WUP:WUP + HID], True, True)
                        mm.then_inc(S["out_ps"], 1)

                @block.scalar
                def _(act):
                    def relu_square(n):
                        act.wait_ge(S["up_done"], n + 1)
                        if n >= 3:
                            act.wait_ge(S["hid_lo"], n - 2)
                        nc.scalar.activation(act_[:, n % 3, :], psGU[:, n % 3, 0, :], ACT.Relu) \
                            .then_inc(S["relu_done"], 1)
                        act.wait_ge(S["relu_done"], n + 1)
                        nc.scalar.activation(act_[:, n % 3, :], act_[:, n % 3, :], ACT.Square) \
                            .then_inc(S["square_done"], 1)

                    def high(n):
                        act.wait_ge(S["prod_done"], n + 1)
                        if n == 3:
                            act.wait_ge(S["shared_ps"], TT)
                        elif n >= 5:
                            act.wait_ge(S["down_done"], n - 4)
                        nc.scalar.copy(hid[0][:, n % 3, :], act_[:, n % 3, :]).then_inc(S["hid_hi"], 1)

                    nc.scalar.preload_act_table_set("natural_log_exp_and_others")
                    for n in range(NU):
                        if n == 2:
                            act.wait_ge(S["xl_done"], 1)
                            nc.scalar.copy(xl[0][:, :], psM[:, :]).then_inc(S["xl_hi"], 1)
                        relu_square(n)
                        for piece in PREPARE.get(n, ()):
                            if piece[0] in PSUM_KINDS:
                                prepare_act(act, *piece)
                        if n == 0:
                            act.wait_ge(S["wT_ps"], 1)
                            nc.scalar.copy(wT, psM[0:NE, :]).then_inc(S["wT_sb"], 1)
                        else:
                            high(n - 1)
                        for piece in PREPARE.get(n, ()):
                            if piece[0] not in PSUM_KINDS:
                                prepare_act(act, *piece)
                    high(NU - 1)
                    act.wait_ge(S["down_done"], NU - 2)
                    nc.scalar.copy(lat[0][:, :], psA[:, :]).then_inc(S["lat_hi"], 1)
                    guess(act, 3)

                @block.gpsimd
                def _(pool):
                    for n in range(2, NU):
                        _, e, t = UNITS[n]
                        pool.wait_ge(S["square_done"], n + 1)
                        pool.wait_ge(S[f"wb_loaded{e % 3}"], 16 * (e // 3 + 1))
                        nc.gpsimd.tensor_tensor(act_[:, n % 3, :], act_[:, n % 3, :], wb[:, e % 3, :], ALU.mult) \
                            .then_inc(S["weighted"], 1)
                        for piece in PREPARE.get(n, ()):
                            prepare_pool(pool, *piece)

                @block.vector
                def _(dve):
                    sstep = chained(dve, S["stat_step"])
                    rstep = chained(dve, S["route_step"])

                    rstep(nc.vector.tensor_scalar(ex[:, :, :], ex[:, :, :], 1.0, None, ALU.add))
                    rstep(nc.vector.reciprocal(prb[:, :, :], ex[:, :, :]))
                    rstep(nc.vector.tensor_tensor(ex[:, :, :], prb[:, :, :],
                                                  rbias[:, :].unsqueeze(1).broadcast_to([P, TT, NE]), ALU.add))
                    for t in range(TT):
                        rstep(nc.vector.max(top[:, t, :], ex[:, t, :]))
                        rstep(nc.vector.match_replace(out=sel[:, t, :], in_to_replace=top[:, t, :],
                                                      in_values=ex[:, t, :], imm_value=-3e38))
                    rstep(nc.vector.scalar_tensor_tensor(sel[:, :, :], sel[:, :, :], -3e38, prb[:, :, :],
                                                         ALU.is_equal, ALU.mult))
                    rstep(nc.vector.reduce_sum(wsum[:, :], sel[:, :, :], AX.X))
                    rstep(nc.vector.reciprocal(wsum[:, :], wsum[:, :]))
                    rstep(nc.vector.tensor_scalar(wsum[:, :], wsum[:, :], ROUTE_SCALE, None, ALU.mult))
                    nc.vector.tensor_tensor(sel[:, :, :], sel[:, :, :],
                                            wsum[:, :].unsqueeze(2).broadcast_to([P, TT, NE]), ALU.mult) \
                        .then_inc(S["route_done"], 1)

                    def low(n):
                        dve.wait_ge(S["hid_hi"], n + 1)
                        nc.vector.tensor_tensor(hid[1][:, n % 3, :], act_[:, n % 3, :], f32(hid[0][:, n % 3, :]),
                                                ALU.subtract).then_inc(S["hid_lo"], 1)

                    for n in range(NU):
                        if n == 2:
                            dve.wait_ge(S["xl_hi"], 1)
                            nc.vector.tensor_tensor(xl[1][:, :], psM[:, :], f32(xl[0][:, :]), ALU.subtract) \
                                .then_inc(S["xl_lo"], 1)
                        for piece in PREPARE.get(n, ()):
                            if piece[0] in PSUM_KINDS:
                                prepare_dve(dve, sstep, *piece)
                        if n < 2:
                            dve.wait_ge(S["square_done"], n + 1)
                        else:
                            dve.wait_ge(S["weighted"], n - 1)
                        a = act_[:, n % 3, :]
                        nc.vector.tensor_tensor(a, psGU[:, n % 3, 1, :], a, ALU.mult).then_inc(S["prod_done"], 1)
                        if n >= 1:
                            low(n - 1)
                        if n == 3:
                            for t in range(TT):
                                dve.wait_ge(S["shared_ps"], t + 1)
                                nc.vector.tensor_tensor(x3[:, t, :], (psM, psA)[t % 2][:, :], x1[:, t, :], ALU.add) \
                                    .then_inc(S["shared_added"], 1)
                        for piece in PREPARE.get(n, ()):
                            if piece[0] not in PSUM_KINDS:
                                prepare_dve(dve, sstep, *piece)
                    low(NU - 1)
                    dve.wait_ge(S["lat_hi"], 1)
                    nc.vector.tensor_tensor(lat[1][:, :], psA[:, :], f32(lat[0][:, :]), ALU.subtract) \
                        .then_inc(S["lat_lo"], 1)
                    for t in range(TT):
                        dve.wait_ge(S["out_ps"], t + 1)
                        nc.vector.tensor_tensor(x3[:, t, :], psGU[:, t // 2, t % 2, :], x3[:, t, :], ALU.add) \
                            .then_inc(S["x3_done"], 1)
                        tile_stats(dve, sstep, x3, t, S["x3_done"])
                    variance(dve)
                    refine(dve, sstep, 3)
                    for t in range(TT):
                        normalise(x3, t, S["out_done"])
            clear(nc, sems)


def layer(nc, d):
    with ExitStack() as ctx:
        def sb(name, shape, dt=F32):
            return ctx.enter_context(nc.sbuf_tensor(name, shape, dt))

        s = {
            "ident": sb("ident", [P, P]), "identb": sb("identb", [P, P], BF16), "maskb": sb("maskb", [P, P], BF16),
            "ones": sb("ones", [1, P]), "neglam": sb("neglam", [P, 1]), "negA": sb("negA", [P, CT * NS]),
            "Dcol": sb("Dcol", [P, CT]), "two": sb("two", [P, 1]),
        }
        d_loaded = ctx.enter_context(nc.semaphore("d_loaded"))
        with nc.Block() as block:
            @block.sync
            def _(sp):
                sp.dma_start(s["Dcol"][:, :], d["Dcol"]).then_inc(d_loaded, 16)
                sp.wait_ge(d_loaded, 16)
        setup(nc, d, s)
        scan_inputs(nc, d, s)
        attend_and_scan(nc, d, s)
        expert_phase(nc, d, s)


def lay_out(inputs):
    import numpy as np

    def rows(a, n):
        return a.reshape(n, P, -1).transpose(1, 0, 2)

    x = np.asarray(inputs["x"])
    wqkv = np.asarray(inputs["L0_attn_Wqkv_w"])
    bqkv = np.asarray(inputs["L0_attn_Wqkv_b"])
    NQ, NK = G * QC, G * KC
    ws, qkb, vb = [], [], []
    for g in range(G):
        idx = np.r_[g * QC:(g + 1) * QC, NQ + g * KC:NQ + (g + 1) * KC, NQ + NK + g * VC:NQ + NK + (g + 1) * VC]
        ws.append(rows(wqkv[idx].T, KT).reshape(P, -1))
        qkb.append(bqkv[idx[:QC + KC]].reshape(6, P).T)
        vb.append(bqkv[idx[QC + KC:]])
    ow = np.asarray(inputs["L0_attn_out_w"]).T
    i = {k: np.asarray(v) for k, v in inputs.items()}
    lam = np.stack([i["L0_attn_lambda_" + n] for n in ("q1", "k1", "q2", "k2")])
    scan_cols = np.concatenate([rows(i["L0_xattn_conv_w"].reshape(CT * P, TAPS), CT),
                                rows(i["L0_xattn_conv_b"][:, None], CT), rows(i["L0_xattn_dt_proj_b"][:, None], CT)], axis=2)

    def flat(a, n):
        return rows(a, n).reshape(P, -1)

    rw1 = i["L0_ffn_rw1"].transpose(2, 0, 1).reshape(LAT, -1)
    rwg = i["L0_ffn_rwg"].transpose(2, 0, 1).reshape(LAT, -1)
    rw2 = i["L0_ffn_rw2"].transpose(0, 2, 1).reshape(NE * 2, P, LAT).transpose(1, 0, 2).reshape(P, -1)
    cw = np.concatenate([flat(i["L0_ffn_Wg"].T, KT), flat(i["L0_ffn_sw1"].T, KT), flat(i["L0_ffn_swg"].T, KT), flat(i["L0_ffn_sw2"].T, 2),
                         flat(i["L0_ffn_Wdown"].T, KT), i["L0_ffn_Wup"].T,
                         rw1, rwg, rw2], axis=1)
    return {
        "x": x.reshape(B * T, HID),
        "xT": x.transpose(0, 2, 1).reshape(B, KT, P, T),
        "w": np.stack(ws), "qk_bias": np.stack(qkb), "v_bias": np.stack(vb),
        "ow": np.stack([rows(ow[g * 512:(g + 1) * 512], 4).reshape(P, -1) for g in range(G)]),
        "subln": i["L0_attn_subln_w"].reshape(2, P).T,
        "lam": lam, "out_b": i["L0_attn_out_b"][None, :],
        "ctxT": i["ctx_1024"].transpose(0, 2, 1).reshape(B, 2, P, T),
        "inT": i["L0_xattn_in_proj_w"].T, "xpT": i["L0_xattn_x_proj_w"].T, "dtT": i["L0_xattn_dt_proj_w"].T,
        "scan_cols": scan_cols,
        "alog": flat(i["L0_xattn_A_log"], CT), "Dcol": i["L0_xattn_D"].reshape(CT, P).T,
        "cw": cw, "route_b": i["L0_ffn_biases"][None, :],
    }


SCRATCH = {"acc": (B * T, HID), "u": (B, P, CT * T), "dt": (B, P, CT * T), "dtu": (B, P, CT * T),
           "bc": (B, 2 * NS, T), "y": (B, P, CT * T), "wT": (NE, T)}


def kernel(**inputs):
    import numpy as np
    import concourse.bacc as bacc
    from concourse.bass_utils import run_bass_kernel_spmd as run

    nc = bacc.Bacc("TRN2", target_bir_lowering=False, num_devices=1)
    arrays, d = {}, {}
    for name, a in lay_out(inputs).items():
        a = np.ascontiguousarray(a)
        arrays[f"in_{name}"] = a
        d[name] = nc.dram_tensor(f"in_{name}", a.shape, mybir.dt.from_np(a.dtype), kind="ExternalInput").ap()
    for name, shape in SCRATCH.items():
        d[name] = nc.dram_tensor(f"scratch_{name}", shape, F32, kind="Internal").ap()
    d["out"] = nc.dram_tensor("out", (B * T, HID), F32, kind="ExternalOutput").ap()
    layer(nc, d)
    r = run(nc, [arrays], core_ids=[0])
    return r.results[0]["out"].reshape(B, T, HID)
```

```python
import math
from contextlib import ExitStack

import concourse.bass as bass
from concourse import mybir

F32 = mybir.dt.float32
F32R = mybir.dt.float32r
BF16 = mybir.dt.bfloat16
ALU = mybir.AluOpType
ACT = mybir.ActivationFunctionType
AX = mybir.AxisListType

P = 128
B, T, HID = 4, 512, 512
KT = HID // P
TT = T // P
G = 4
HD = 128
E2 = 2 * HD
QC, KC, VC = 4 * HD, 2 * HD, E2
GC = QC + KC + VC
LAMBDA_INIT = 0.8 - 0.6 * math.exp(-0.3)
SCALE = HD ** -0.5
EPS = 1e-5
NEG = -1e30
CT = 4
NS = 16
RANK = 16
TAPS = 4
CTX = 256
NE = 16
LAT = 128
TOPK = 8
ROUTE_SCALE = 2.5
ATANH = (2.0000000078777487, 0.6666631593508026, 0.40024853723499904,
         0.27961418834331303, 0.2817465726538725)

WGT = 0
SW1 = WGT + KT * NE
SWG = SW1 + KT * 256
SW2 = SWG + KT * 256
WDN = SW2 + 2 * HID
WUP = WDN + KT * LAT
RW1 = WUP + HID
RWG = RW1 + NE * 256
RW2 = RWG + NE * 256
WCOLS = RW2 + NE * 2 * LAT


def rsqrt_newton(dve, step, y, v, tmp):
    step(dve.scalar_tensor_tensor(tmp, y, -0.5, y, ALU.mult, ALU.mult))
    step(dve.tensor_tensor(tmp, tmp, v, ALU.mult))
    step(dve.scalar_tensor_tensor(y, tmp, 1.5, y, ALU.add, ALU.mult))


def chained(engine, sem):
    count = [0]

    def step(ins):
        count[0] += 1
        ins.then_inc(sem, 1)
        engine.wait_ge(sem, count[0])

    return step


def clear(nc, sems):
    nums = [s.num for s in sems]
    assert nums == list(range(nums[0], nums[0] + len(nums)))
    nc.vector.sem_clear(range(nums[0], nums[-1] + 1))
    nc.all_engine_barrier(sem_only=True)


def setup(nc, d, s):
    with ExitStack() as ctx:
        def sb(name, shape, dt=F32):
            return ctx.enter_context(nc.sbuf_tensor(name, shape, dt))

        lams = sb("lams", [P, 4, P])
        prod = sb("lam_prod", [P, 2, P])
        lsum = sb("lam_sum", [P, 2])
        lexp = sb("lam_exp", [P, 2])
        alog = sb("alog", [P, CT * NS])
        sems = [ctx.enter_context(nc.semaphore(n)) for n in
                ("loaded", "cleared", "const_done", "lam_step", "act_step")]
        loaded, cleared, const_done, lam_step, act_step = sems
        with nc.Block() as block:
            @block.sync
            def _(sp):
                for n in range(4):
                    sp.dma_start(lams[:, n, :], d["lam"][n:n + 1, :].broadcast_to([P, P])).then_inc(loaded, 16)
                sp.dma_start(alog[:, :], d["alog"]).then_inc(loaded, 16)
                sp.dma_start(s["Dcol"][:, :], d["Dcol"]).then_inc(loaded, 16)

            @block.gpsimd
            def _(pool):
                nc.gpsimd.memset(s["ident"][:, :], 0.0).then_inc(cleared, 1)
                nc.gpsimd.memset(s["identb"][:, :], 0.0).then_inc(cleared, 1)
                nc.gpsimd.memset(s["maskb"][:, :], 0.0).then_inc(cleared, 1)
                pool.wait_ge(cleared, 3)
                for m in ("ident", "identb"):
                    nc.gpsimd.affine_select(out=s[m][:, :], in_=s[m][:, :], compare_op=ALU.not_equal, fill=1.0,
                                            base=0, pattern=[[-1, P]], channel_multiplier=1).then_inc(const_done, 1)
                nc.gpsimd.affine_select(out=s["maskb"][:, :], in_=s["maskb"][:, :], compare_op=ALU.is_ge, fill=NEG,
                                        base=0, pattern=[[-1, P]], channel_multiplier=1).then_inc(const_done, 1)
                nc.gpsimd.memset(s["ones"][:, :], 1.0).then_inc(const_done, 1)
                nc.gpsimd.memset(s["two"][:, :], 2.0).then_inc(const_done, 1)
                pool.wait_ge(const_done, 5)

            @block.vector
            def _(dve):
                step = chained(dve, lam_step)
                dve.wait_ge(loaded, 96)
                for n in range(2):
                    step(nc.vector.tensor_tensor(prod[:, n, :], lams[:, 2 * n, :], lams[:, 2 * n + 1, :], ALU.mult))
                step(nc.vector.reduce_sum(lsum[:, :], prod[:, :, :], AX.X))
                dve.wait_ge(act_step, 2)
                step(nc.vector.tensor_tensor(s["neglam"][:, :], lexp[:, 1:2], lexp[:, 0:1], ALU.subtract))
                step(nc.vector.tensor_scalar(s["neglam"][:, :], s["neglam"][:, :], -LAMBDA_INIT, None, ALU.add))
                step(nc.vector.tensor_scalar(s["negA"][:, :], s["negA"][:, :], -1.0, None, ALU.mult))

            @block.scalar
            def _(act):
                act.wait_ge(loaded, 96)
                nc.scalar.activation(s["negA"][:, :], alog[:, :], ACT.Exp).then_inc(act_step, 1)
                act.wait_ge(lam_step, 3)
                nc.scalar.activation(lexp[:, :], lsum[:, :], ACT.Exp).then_inc(act_step, 1)


def scan_inputs(nc, d, s, copied):
    with ExitStack() as ctx:
        def sb(name, shape, dt=F32):
            return ctx.enter_context(nc.sbuf_tensor(name, shape, dt))

        win = sb("win", [P, 2, CT * P])
        wxp = sb("wxp", [P, CT, RANK + 2 * NS])
        wdt = sb("wdt", [RANK, CT * P])
        cols = sb("scan_cols", [P, CT, TAPS + 2])
        ctxT = sb("ctxT", [P, 2, T])
        xpad = sb("xpad", [P, CT, TAPS - 1 + T])
        conv = sb("conv", [P, CT, T])
        th = sb("tanh", [P, CT, T])
        u = sb("u", [P, CT, T])
        xdbl = sb("xdbl", [RANK + 2 * NS, T])
        ub = sb("u_back", [P, CT, T])
        v = sb("v", [P, CT, T])
        e = sb("e", [P, CT, T])
        z = sb("z", [P, CT, T])
        z2 = sb("z2", [P, CT, T])
        q = sb("q", [P, CT, T])
        psX = ctx.enter_context(nc.psum_tensor("psX", [P, CT, T], F32))
        psV = ctx.enter_context(nc.psum_tensor("psV", [P, 2, T], F32))
        psD = ctx.enter_context(nc.psum_tensor("psD", [RANK + 2 * NS, T], F32))
        w_loaded = ctx.enter_context(nc.semaphore("w_loaded"))
        pad_zero = ctx.enter_context(nc.semaphore("pad_zero"))
        halved = ctx.enter_context(nc.semaphore("halved"))
        names = ("ctx_loaded", "ub_loaded", "inproj_done", "pad_done", "conv_step", "tanh_done", "u_done",
                 "xdbl_ps", "xdbl_sb", "dt_ps", "v_done", "act_step", "guess_done", "recip_step", "recip_done",
                 "z_done", "square_step", "square_done", "poly_step", "dt_done", "dtu_done", "dtu_last", "stored")
        sems = [ctx.enter_context(nc.semaphore(n)) for n in names]
        S = dict(zip(names, sems))

        def load_ctx(sp, b, sem):
            sp.dma_start(ctxT[:, :, :], d["ctxT"][bass.ds(b, 1), :, :, :].rearrange("b k p t -> p (b k) t")) \
                .then_inc(sem, 16)

        with nc.Block() as block:
            @block.sync
            def _(sp):
                sp.dma_start(win[:, :, :], d["inT"].rearrange("(k p) n -> p k n", p=P)).then_inc(w_loaded, 16)
                sp.dma_start(wxp[:, :, :], d["xpT"].rearrange("(k p) n -> p k n", p=P)).then_inc(w_loaded, 16)
                sp.dma_start(wdt[:, :], d["dtT"]).then_inc(w_loaded, 16)
                sp.dma_start(cols[:, :, :], d["scan_cols"]).then_inc(w_loaded, 16)
                load_ctx(sp, 0, w_loaded)
                sp.wait_ge(w_loaded, 80)
                sp.dma_start(d["acc"], d["x"]).then_inc(copied, 16)

            @block.gpsimd
            def _(pool):
                nc.gpsimd.memset(xpad[:, :, 0:TAPS - 1], 0.0).then_inc(pad_zero, 1)
                pool.wait_ge(pad_zero, 1)

            @block.vector
            def _(dve):
                dve.wait_ge(w_loaded, 80)
                nc.vector.tensor_scalar(cols[:, :, 0:TAPS + 1], cols[:, :, 0:TAPS + 1], 0.5, None, ALU.mult) \
                    .then_inc(halved, 1)

        def stages(front, back):
            def half(buf, h):
                return buf[:, 2 * h:2 * h + 2, :]

            with nc.Block(no_gpsimd_drain=True) as block:
                @block.sync
                def _(sp):
                    def store(name, b, h, buf):
                        sp.dma_start(d[name][bass.ds(b, 1), :, 2 * h * T:2 * (h + 1) * T].rearrange("b p n -> p (b n)"),
                                     half(buf, h).rearrange("p c t -> p (c t)")).then_inc(S["stored"], 16)

                    if back is not None:
                        sp.dma_start(ub[:, :, :].rearrange("p c t -> p (c t)"),
                                     d["u"][bass.ds(back, 1), :, :].rearrange("b p n -> p (b n)")) \
                            .then_inc(S["ub_loaded"], 16)
                    if front is not None:
                        sp.wait_ge(S["inproj_done"], CT)
                        load_ctx(sp, (front + 1) & (B - 1), S["ctx_loaded"])
                    if back is not None:
                        sp.wait_ge(S["dt_done"], 1)
                        store("dt", back, 0, q)
                        sp.wait_ge(S["dtu_done"], 1)
                        store("dtu", back, 0, z)
                    if front is not None:
                        for h in range(2):
                            sp.wait_ge(S["u_done"], h + 1)
                            store("u", front, h, u)
                        sp.wait_ge(S["xdbl_sb"], 1)
                        sp.dma_start(d["bc"][bass.ds(front, 1), :, :].rearrange("b p n -> p (b n)"),
                                     xdbl[RANK:, :]).then_inc(S["stored"], 16)
                    if back is not None:
                        sp.wait_ge(S["dt_done"], 2)
                        store("dt", back, 1, q)
                        sp.wait_ge(S["dtu_last"], 1)
                        store("dtu", back, 1, z)
                    if front is not None:
                        sp.wait_ge(S["ctx_loaded"], 16)
                    sp.wait_ge(S["stored"], 16 * (3 * (front is not None) + 4 * (back is not None)))

                @block.tensor
                def _(pe):
                    def project(c):
                        if front is not None:
                            for k in range(2):
                                mm = nc.tensor.matmul(psX[:, c, :], win[:, k, c * P:(c + 1) * P], ctxT[:, k, :],
                                                      start=k == 0, stop=k == 1)
                            mm.then_inc(S["inproj_done"], 1)

                    def dt_project(c):
                        if back is not None:
                            if c >= 2:
                                pe.wait_ge(S["v_done"], c - 1)
                            nc.tensor.matmul(psV[:, c % 2, :], wdt[:, c * P:(c + 1) * P], xdbl[0:RANK, :],
                                             start=True, stop=True).then_inc(S["dt_ps"], 1)

                    for h in range(2):
                        project(2 * h)
                        dt_project(2 * h)
                        dt_project(2 * h + 1)
                        project(2 * h + 1)
                    if front is not None:
                        for c in range(CT):
                            pe.wait_ge(S["u_done"], c // 2 + 1)
                            mm = nc.tensor.matmul(psD[:, :], wxp[:, c, :], u[:, c, :], start=c == 0, stop=c == CT - 1)
                        mm.then_inc(S["xdbl_ps"], 1)

                @block.scalar
                def _(act):
                    def pad(c):
                        if front is not None:
                            act.wait_ge(S["inproj_done"], c + 1)
                            nc.scalar.copy(xpad[:, c, TAPS - 1:], psX[:, c, :]).then_inc(S["pad_done"], 1)

                    def square(h):
                        if back is not None:
                            act.wait_ge(S["z_done"], h + 1)
                            nc.scalar.activation(half(z2, h), half(z, h), ACT.Square).then_inc(S["square_step"], 1)
                            act.wait_ge(S["square_step"], h + 1)
                            nc.scalar.activation(half(q, h), half(z2, h), ACT.Copy, scale=ATANH[4]) \
                                .then_inc(S["square_done"], 1)

                    step = chained(act, S["act_step"])
                    for h in range(2):
                        pad(2 * h)
                        if back is not None:
                            for c in (2 * h, 2 * h + 1):
                                act.wait_ge(S["dt_ps"], c + 1)
                                nc.scalar.activation(v[:, c, :], psV[:, c % 2, :], ACT.Identity,
                                                     bias=cols[:, c, TAPS + 1:TAPS + 2]).then_inc(S["v_done"], 1)
                            act.wait_ge(S["v_done"], 2 * h + 2)
                            step(nc.scalar.activation(half(z, h), half(v, h), ACT.Abs))
                        pad(2 * h + 1)
                        if back is not None:
                            step(nc.scalar.activation(half(e, h), half(z, h), ACT.Exp, scale=-1.0))
                            step(nc.scalar.activation(half(z2, h), half(e, h), ACT.Ln, bias=s["two"][:, :]))
                            nc.scalar.activation(half(q, h), half(z2, h), ACT.Exp, scale=-1.0) \
                                .then_inc(S["guess_done"], 1)
                    square(0)
                    if front is not None:
                        for c in range(CT):
                            act.wait_ge(S["conv_step"], 8 * (c // 2) + 7 + c % 2)
                            nc.scalar.activation(th[:, c, :], conv[:, c, :], ACT.Tanh).then_inc(S["tanh_done"], 1)
                        nc.scalar.preload_act_table_set("natural_log_exp_and_others")
                    square(1)
                    if front is not None:
                        act.wait_ge(S["xdbl_ps"], 1)
                        nc.scalar.copy(xdbl[:, :], psD[:, :]).then_inc(S["xdbl_sb"], 1)

                @block.gpsimd
                def _(pool):
                    if back is not None:
                        def scaled(h):
                            pool.wait_ge(S["recip_done"], h + 1)
                            nc.gpsimd.tensor_tensor(half(z, h), half(z2, h), half(e, h), ALU.mult) \
                                .then_inc(S["z_done"], 1)

                        scaled(0)
                        scaled(1)
                        pool.wait_ge(S["ub_loaded"], 16)
                        pool.wait_ge(S["dt_done"], 1)
                        nc.gpsimd.tensor_tensor(half(z, 0), half(q, 0), half(ub, 0), ALU.mult) \
                            .then_inc(S["dtu_done"], 1)

                @block.vector
                def _(dve):
                    def convolve(h):
                        for n in range(2 * TAPS):
                            j, c = n // 2, 2 * h + n % 2
                            if j == 0:
                                dve.wait_ge(S["pad_done"], c + 1)
                                ins = nc.vector.tensor_scalar(conv[:, c, :], xpad[:, c, 0:T], cols[:, c, 0:1],
                                                              cols[:, c, TAPS:TAPS + 1], ALU.mult, ALU.add)
                            else:
                                dve.wait_ge(S["conv_step"], 8 * h + n - 1)
                                ins = nc.vector.scalar_tensor_tensor(conv[:, c, :], xpad[:, c, j:j + T],
                                                                     cols[:, c, j:j + 1], conv[:, c, :],
                                                                     ALU.mult, ALU.add)
                            ins.then_inc(S["conv_step"], 1)

                    def reciprocal(h):
                        dve.wait_ge(S["guess_done"], h + 1)
                        nc.vector.scalar_tensor_tensor(half(z2, h), half(e, h), 2.0, half(q, h), ALU.add, ALU.mult) \
                            .then_inc(S["recip_step"], 1)
                        dve.wait_ge(S["recip_step"], h + 1)
                        nc.vector.scalar_tensor_tensor(half(z2, h), half(z2, h), 2.0, half(q, h),
                                                       ALU.subtract, ALU.mult).then_inc(S["recip_done"], 1)

                    def silu(h):
                        dve.wait_ge(S["tanh_done"], 2 * h + 2)
                        dve.wait_ge(S["conv_step"], 8 * h + 8)
                        nc.vector.scalar_tensor_tensor(half(u, h), half(th, h), 1.0, half(conv, h), ALU.add, ALU.mult) \
                            .then_inc(S["u_done"], 1)

                    def softplus(h, step):
                        dve.wait_ge(S["square_done"], h + 1)
                        for n in (3, 2, 1):
                            step(nc.vector.scalar_tensor_tensor(half(q, h), half(q, h), ATANH[n], half(z2, h),
                                                                ALU.add, ALU.mult))
                        step(nc.vector.scalar_tensor_tensor(half(q, h), half(q, h), ATANH[0], half(z, h),
                                                            ALU.add, ALU.mult))
                        nc.vector.scalar_tensor_tensor(half(q, h), half(v, h), 0.0, half(q, h),
                                                       ALU.max, ALU.subtract).then_inc(S["dt_done"], 1)

                    step = chained(dve, S["poly_step"])
                    for h in range(2):
                        if front is not None:
                            convolve(h)
                        if back is not None:
                            reciprocal(h)
                    if back is not None:
                        dve.wait_ge(S["ub_loaded"], 16)
                        softplus(0, step)
                    if front is not None:
                        silu(0)
                        silu(1)
                    if back is not None:
                        softplus(1, step)
                        dve.wait_ge(S["dt_done"], 2)
                        nc.vector.tensor_tensor(half(z, 1), half(q, 1), half(ub, 1), ALU.mult) \
                            .then_inc(S["dtu_last"], 1)
            clear(nc, sems)

        stages(0, None)
        with nc.Fori(0, B - 1) as b:
            stages(b + 1, b)
        stages(None, B - 1)



TRAILS = (("PV", 4), ("W", 5), ("R", 5), ("OT", 6), ("H", 6), ("OUT", 7), ("A", 8))
Q_TILES = (1, 2, 0, 3)
INPUT_SLOTS = (7, 10)
WEIGHT_SLOTS = (4, 5, 6, 9)
SCAN_SLOTS = (0, 1, 2, 3, 6, 8, 9, 11)


def attention_slots():
    slots = [[] for _ in range(12 * B + 7)]
    for j in range(B):
        at = 12 * j
        for n, item in enumerate((("K", j, 0), ("Q", j, 0), ("Q", j, 1), ("V", j, 0))):
            slots[at + n].append(item)
        for u in range(8):
            slots[at + 4 + u] += [("S", j, u), ("C", j, u)]
            slots[at + 5 + u].append(("T", j, u))
            slots[at + 6 + u].append(("L", j, u))
        for qt in range(TT):
            for kind, trail in TRAILS:
                slots[at + 4 + 2 * qt + trail].append((kind, j, qt))
        for n, slot in enumerate(INPUT_SLOTS):
            slots[at + slot].append(("X", j + 1, n))
        for n, slot in enumerate(SCAN_SLOTS):
            slots[at + slot].append(("M", j, n))
    for n, slot in enumerate(WEIGHT_SLOTS):
        slots[12 * (B - 1) + slot].append(("N", B - 1, n))
    slots[12 * B].append(("M", B, 0))
    slots[12 * B + 2].append(("Y", 0, 0))
    return slots


PE_ORDER = "K V Q S PV OT OUT T"
ACT_PROJ = "L K R Q M H N X V PV"
ACT_UNIT = "X L H M N S R PV"
DVE_PROJ = "A L N H W M K V X Q R"
DVE_UNIT = "A L S X W H M N R C"
SP_ORDER = "M V A Y"


def in_order(slots, proj, unit=None):
    out = []
    for n, items in enumerate(slots):
        ranks = (unit if unit and n % 12 >= 4 else proj).split()
        out += sorted((i for i in items if i[0] in ranks), key=lambda i: ranks.index(i[0]))
    return out


W_CUTS = ((QC, QC + KC, 1.0), (0, 2 * HD, SCALE), (2 * HD, QC, SCALE), (QC + KC, GC, 1.0))


def dve_drives(k):
    return k % 8 in (1, 3)


DVE_DRIVES = sum(dve_drives(k) for k in range(2 * NS))


def attend_and_scan(nc, d, s, copied):
    slots = attention_slots()
    with ExitStack() as ctx:
        def sb(name, shape, dt=F32):
            return ctx.enter_context(nc.sbuf_tensor(name, shape, dt))

        def pair(name, shape):
            return sb(name + "_hi", shape, F32R), sb(name + "_lo", shape, F32R)

        def ps(name, shape):
            return ctx.enter_context(nc.psum_tensor(name, shape, F32))

        wraw = sb("wraw", [P, KT, GC])
        w = pair("w", [P, KT, GC])
        ow = pair("ow", [P, 4, HID])
        bias = sb("qk_bias", [P, 6])
        vbias = sb("v_bias", [1, VC])
        subln = sb("subln", [P, 2])
        xraw = sb("xraw", [P, KT, T])
        x = pair("x", [P, KT, T])
        qT = pair("qT", [P, 4, T])
        kT = pair("kT", [P, 2, T])
        v = pair("v", [P, TT, E2])
        prob = sb("prob", [P, 2, 2, T])
        pT = pair("pT", [P, 3, TT, P])
        junk = sb("junk", [P, E2])
        head = sb("head", [P, 2, E2])
        hT = pair("hT", [P, 4, P])
        acc = sb("acc_sb", [P, 2, HID])
        negmax = sb("negmax", [P, 2, 2])
        rowsum = sb("rowsum", [P, TT, 2, 2])
        rinv = sb("rinv", [P, 2])
        coef = sb("coef", [P, 2])
        msq = sb("msq", [P, 2, 2])
        var = sb("var", [P, 2, 2])
        rms = sb("rms", [P, 2, 2])
        tmp = sb("rms_tmp", [P, 2])
        nrm = sb("nrm", [P, 2])
        dt = sb("dt_sb", [P, CT, T])
        dtu = sb("dtu_sb", [P, CT, T])
        y = sb("y_sb", [P, CT, T])
        Bn = sb("Bn", [P, 2, T])
        Cn = sb("Cn", [P, 2, T])
        dA = sb("dA", [P, 2, 2, T])
        st = sb("state", [P, 3, 2, T])

        psBig = ps("psBig", [P, 2, 2, T])
        psT = ps("psT", [P, TT, P])
        psPV = ps("psPV", [P, 2, 2, E2])
        psO = ps("psO", [P, HID])

        zeroed = ctx.enter_context(nc.semaphore("dA_zeroed"))
        names = ("scan_loaded", "w_loaded", "b_loaded", "ow_loaded", "x_loaded", "acc_loaded0", "acc_loaded1", "acc_stored0", "acc_stored1", "w_hi", "w_lo", "ow_hi",
                 "ow_lo", "ow_col", "b_scaled", "x_hi", "x_lo", "proj_done", "proj_hi", "proj_lo", "scores_done", "max_done",
                 "exp_done", "probs_done", "comb_step", "pt_done", "pt_hi", "pt_lo", "pv_done", "sq_done",
                 "var_done", "var_step", "ln_done", "guess_done", "rms_step", "head_done", "ot_done", "ot_hi",
                 "ot_lo", "out_done", "acc_done", "u_loaded", "bc_loaded0", "bc_loaded1", "dA_done", "dbu_done", "dbu_dve", "scan_done",
                 "gated", "piece_done", "y_init", "y_stored")
        sems = [ctx.enter_context(nc.semaphore(n)) for n in names]
        S = dict(zip(names, sems))

        first_loaded = ctx.enter_context(nc.semaphore("first_loaded"))

        def load_group(sp, g, sem):
            sp.dma_start(wraw[:, :, :], d["w"][bass.ds(g, 1), :, :].rearrange("g p n -> p (g n)")
                         .rearrange("p (k n) -> p k n", k=KT)).then_inc(sem, 16)

        def load_scan(sp, g, sem):
            for buf, src in ((dt, "dt"), (dtu, "dtu")):
                sp.dma_start(buf[:, :, :].rearrange("p c t -> p (c t)"),
                             d[src][bass.ds(g, 1), :, :].rearrange("b p n -> p (b n)")).then_inc(sem, 16)

        def load_x0(sp, sem):
            sp.dma_start(xraw[:, :, :], d["xT"][0].rearrange("k p t -> p k t")).then_inc(sem, 16)

        def f32(ap):
            return ap.bitcast(F32)

        def w_high(n, sem):
            c0, c1, f = W_CUTS[n]
            nc.scalar.activation(w[0][:, :, c0:c1], wraw[:, :, c0:c1], ACT.Copy, scale=f).then_inc(sem, 1)

        def w_low(n, sem):
            c0, c1, f = W_CUTS[n]
            nc.vector.scalar_tensor_tensor(w[1][:, :, c0:c1], wraw[:, :, c0:c1], f, f32(w[0][:, :, c0:c1]),
                                           ALU.mult, ALU.subtract).then_inc(sem, 1)

        def x_high(n, sem):
            nc.scalar.copy(x[0][:, 2 * n:2 * n + 2, :], xraw[:, 2 * n:2 * n + 2, :]).then_inc(sem, 1)

        def x_low(n, sem):
            nc.vector.tensor_tensor(x[1][:, 2 * n:2 * n + 2, :], xraw[:, 2 * n:2 * n + 2, :],
                                    f32(x[0][:, 2 * n:2 * n + 2, :]), ALU.subtract).then_inc(sem, 1)

        first_hi = ctx.enter_context(nc.semaphore("first_hi"))
        first_lo = ctx.enter_context(nc.semaphore("first_lo"))

        with nc.Block() as block:
            @block.sync
            def _(sp):
                load_group(sp, 0, first_loaded)
                load_x0(sp, first_loaded)
                load_scan(sp, 0, first_loaded)
                sp.wait_ge(copied, 16)

            @block.scalar
            def _(act):
                nc.scalar.preload_act_table_set("natural_log_exp_and_others")
                act.wait_ge(first_loaded, 64)
                for n in range(4):
                    w_high(n, first_hi)
                for n in range(2):
                    x_high(n, first_hi)

            @block.vector
            def _(dve):
                for n in range(4):
                    dve.wait_ge(first_hi, n + 1)
                    w_low(n, first_lo)
                for n in range(2):
                    dve.wait_ge(first_hi, 4 + n + 1)
                    x_low(n, first_lo)

            @block.gpsimd
            def _(pool):
                nc.gpsimd.memset(dA[:, :, :, 0:1], 0.0).then_inc(zeroed, 1)
                pool.wait_ge(zeroed, 1)

        with nc.Fori(0, G) as g:
            with nc.Block(no_gpsimd_drain=True) as block:

                def wait_big_free(eng, w_):
                    if w_ >= 2:
                        j, r = divmod(w_ - 2, 12)
                        if r < 4:
                            eng.wait_ge(S["proj_hi"], 4 * j + r + 1)
                            eng.wait_ge(S["proj_lo"], 4 * j + r + 1)
                        else:
                            eng.wait_ge(S["exp_done"], 8 * j + r - 4 + 1)

                def use_of(kind, n):
                    return {"K": 0, "Q": 1 + n, "V": 3, "S": 4 + n}[kind]

                @block.sync
                def _(sp):
                    sp.dma_start(bias[:, :], d["qk_bias"][bass.ds(g, 1), :, :].rearrange("g p n -> p (g n)")) \
                        .then_inc(S["b_loaded"], 16)
                    sp.dma_start(vbias[:, :], d["v_bias"][bass.ds(g, 1), :]).then_inc(S["b_loaded"], 16)
                    sp.dma_start(subln[:, :], d["subln"]).then_inc(S["b_loaded"], 16)
                    sp.dma_start(y[:, :, :].rearrange("p c t -> p (c t)"),
                                 d["u"][bass.ds(g, 1), :, :].rearrange("b p n -> p (b n)")).then_inc(S["u_loaded"], 16)

                    def load_bc(n):
                        if n >= 2:
                            sp.wait_ge(S["piece_done"], 2 * (n - 2) + 2)
                        for buf, row in ((Bn, n), (Cn, NS + n)):
                            sp.dma_start(buf[:, n % 2, :], d["bc"][bass.ds(g, 1), row:row + 1, :]
                                         .rearrange("b n t -> (b n) t").broadcast_to([P, T])).then_inc(S[f"bc_loaded{n % 2}"], 16)

                    def acc_rows(n):
                        row = (n // TT * TT + Q_TILES[n % TT]) * P
                        return d["acc"][row:row + P, :]

                    def load_acc(n):
                        if n >= 2:
                            sp.wait_ge(S[f"acc_stored{n % 2}"], 16 * (n // 2))
                        sp.dma_start(acc[:, n % 2, :], acc_rows(n)).then_inc(S[f"acc_loaded{n % 2}"], 16)

                    load_bc(0)
                    load_bc(1)
                    load_acc(0)
                    load_acc(1)
                    sp.dma_start(wraw[:, :, 0:HID], d["ow"][bass.ds(g, 1), :, :].rearrange("g p n -> p (g n)")
                                 .rearrange("p (k n) -> p k n", k=4)).then_inc(S["ow_loaded"], 16)
                    for kind, j, n in in_order(slots, SP_ORDER):
                        if kind == "M":
                            k = 8 * j + n
                            if k % 2 == 1 and 2 <= (k + 1) // 2 < NS:
                                load_bc((k + 1) // 2)
                            elif k == 2 * NS:
                                sp.wait_ge(S["dA_done"], 2 * NS)
                                sp.wait_ge(S["dbu_done"], 2 * NS - DVE_DRIVES)
                                sp.wait_ge(S["dbu_dve"], DVE_DRIVES)
                                load_scan(sp, (g + 1) & (G - 1), S["scan_loaded"])
                        elif kind == "Y":
                            sp.wait_ge(S["piece_done"], 2 * NS)
                            sp.dma_start(d["y"][bass.ds(g, 1), :, :].rearrange("b p n -> p (b n)"),
                                         y[:, :, :].rearrange("p c t -> p (c t)")).then_inc(S["y_stored"], 16)
                        elif kind == "V" and j == 1:
                            sp.wait_ge(S["ow_hi"], 4)
                            sp.wait_ge(S["ow_lo"], 4)
                            load_group(sp, (g + 1) & (G - 1), S["w_loaded"])
                        if kind == "V":
                            if j > 0:
                                sp.wait_ge(S["x_hi"], 2 * j)
                                sp.wait_ge(S["x_lo"], 2 * j)
                            sp.dma_start(xraw[:, :, :], d["xT"][(j + 1) % B].rearrange("k p t -> p k t")) \
                                .then_inc(S["x_loaded"], 16)
                        elif kind == "A":
                            m = 4 * j + n
                            sp.wait_ge(S["acc_done"], m + 1)
                            sp.dma_start(acc_rows(m), acc[:, m % 2, :]).then_inc(S[f"acc_stored{m % 2}"], 16)
                            if m + 2 < 4 * B:
                                load_acc(m + 2)
                    sp.wait_ge(S["acc_stored0"], 16 * 2 * B)
                    sp.wait_ge(S["acc_stored1"], 16 * 2 * B)
                    sp.wait_ge(S["y_stored"], 16)
                    sp.wait_ge(S["scan_loaded"], 32)

                @block.tensor
                def _(pe):
                    def three(out, lhs, rhs, at_l, at_r, start, stop):
                        nc.tensor.matmul(out, at_l(lhs[0]), at_r(rhs[0]), start=start, stop=False)
                        nc.tensor.matmul(out, at_l(lhs[0]), at_r(rhs[1]), start=False, stop=False)
                        return nc.tensor.matmul(out, at_l(lhs[1]), at_r(rhs[0]), start=False, stop=stop)

                    for kind, j, n in in_order(slots, PE_ORDER):
                        if kind in ("K", "Q", "V"):
                            r = use_of(kind, n)
                            wait_big_free(pe, 12 * j + r)
                            if kind == "K" and j > 0:
                                pe.wait_ge(S["x_hi"], 2 * j)
                                pe.wait_ge(S["x_lo"], 2 * j)
                            if kind == "V" and j == 0:
                                pe.wait_ge(S["b_loaded"], 48)
                            big = psBig[:, r % 2]
                            if kind == "V":
                                vps = big.rearrange("p a (b n) -> p (a b) n", b=2)
                                for t in range(TT):
                                    for k in range(KT):
                                        three(vps[:, t, :], x, w, lambda a: a[:, k, t * P:(t + 1) * P],
                                              lambda a: a[:, k, QC + KC:GC], k == 0, False)
                                    mm = nc.tensor.matmul(vps[:, t, :], s["ones"][0:1, :], vbias[:, :],
                                                          start=False, stop=True)
                            else:
                                c0 = QC if kind == "K" else 2 * n * HD
                                for m in range(2):
                                    for k in range(KT):
                                        mm = three(big[:, m, :], w, x,
                                                   lambda a: a[:, k, c0 + m * HD:c0 + (m + 1) * HD],
                                                   lambda a: a[:, k, :], k == 0, k == KT - 1)
                            mm.then_inc(S["proj_done"], 1)
                        elif kind == "S":
                            qt, h = Q_TILES[n // 2], n % 2
                            wait_big_free(pe, 12 * j + 4 + n)
                            if n == 0:
                                pe.wait_ge(S["proj_hi"], 4 * j + 4)
                                pe.wait_ge(S["proj_lo"], 4 * j + 4)
                            wd = (qt + 1) * P
                            for m in range(2):
                                out = psBig[:, n % 2, m, 0:wd]
                                three(out, qT, kT, lambda a: a[:, 2 * h + m, qt * P:wd], lambda a: a[:, m, 0:wd],
                                      True, False)
                                mm = nc.tensor.matmul(psBig[:, n % 2, m, qt * P:wd], s["identb"][:, :], s["maskb"][:, :],
                                                      start=False, stop=True)
                            mm.then_inc(S["scores_done"], 1)
                        elif kind == "T":
                            qt = Q_TILES[n // 2]
                            pe.wait_ge(S["probs_done"], 8 * j + n + 1)
                            if 8 * j + n > 0:
                                pe.wait_ge(S["pt_hi"], 8 * j + n)
                                pe.wait_ge(S["pt_lo"], 8 * j + n)
                            for kt in range(qt + 1):
                                mm = nc.tensor.transpose(psT[:, kt, :], prob[:, n % 2, 0, kt * P:(kt + 1) * P],
                                                         s["ident"][:, :])
                            mm.then_inc(S["pt_done"], 1)
                        elif kind == "PV":
                            m = 4 * j + n
                            pe.wait_ge(S["pt_hi"], 2 * m + 2)
                            pe.wait_ge(S["pt_lo"], 2 * m + 2)
                            if m > 1:
                                pe.wait_ge(S["head_done"], m - 1)
                            for h in range(2):
                                for kt in range(Q_TILES[n] + 1):
                                    mm = three(psPV[:, n % 2, h, :], pT, v, lambda a: a[:, (2 * m + h) % 3, kt, :],
                                               lambda a: a[:, kt, :],
                                               kt == 0, kt == Q_TILES[n])
                            mm.then_inc(S["pv_done"], 1)
                        elif kind == "OT":
                            m = 4 * j + n
                            pe.wait_ge(S["head_done"], m + 1)
                            if m > 0:
                                pe.wait_ge(S["acc_done"], m)
                            for r in range(4):
                                mm = nc.tensor.transpose(psO[:, r * P:(r + 1) * P], head[:, r // 2, (r % 2) * P:(r % 2 + 1) * P],
                                                         s["ident"][:, :])
                            mm.then_inc(S["ot_done"], 1)
                        elif kind == "OUT":
                            m = 4 * j + n
                            if m == 0:
                                pe.wait_ge(S["ow_hi"], 4)
                                pe.wait_ge(S["ow_lo"], 4)
                            pe.wait_ge(S["ot_hi"], m + 1)
                            pe.wait_ge(S["ot_lo"], m + 1)
                            for r in range(4):
                                mm = three(psO[:, :], hT, ow, lambda a: a[:, r, :], lambda a: a[:, r, :],
                                           r == 0, r == 3)
                            mm.then_inc(S["out_done"], 1)

                def split_x(eng, j, n):
                    if n == 0:
                        eng.wait_ge(S["x_loaded"], 16 * j)
                        eng.wait_ge(S["proj_done"], 4 * j)

                def split_w(eng):
                    eng.wait_ge(S["w_loaded"], 16)
                    eng.wait_ge(S["proj_done"], 4 * B)

                @block.scalar
                def _(act):
                    act.wait_ge(S["b_scaled"], 1)
                    for kind, j, n in in_order(slots, ACT_PROJ, ACT_UNIT):
                        if kind in ("K", "Q", "V"):
                            r = use_of(kind, n)
                            if kind == "V" and j == 0:
                                act.wait_ge(S["ow_loaded"], 16)
                                act.wait_ge(S["ow_col"], 1)
                                for t in range(4):
                                    nc.scalar.activation(ow[0][:, t, :], wraw[:, t, 0:HID], ACT.Copy,
                                                         scale=subln[:, t % 2:t % 2 + 1]).then_inc(S["ow_hi"], 1)
                            act.wait_ge(S["proj_done"], 4 * j + r + 1)
                            big = psBig[:, r % 2]
                            if kind == "V":
                                ins = nc.scalar.copy(v[0][:, :, :].rearrange("p a b -> p (a b)"),
                                                     big.rearrange("p a b -> p (a b)"))
                            else:
                                dst, col = (kT, 4) if kind == "K" else (qT, 2 * n)
                                base = 0 if kind == "K" else 2 * n
                                for m in range(2):
                                    ins = nc.scalar.activation(dst[0][:, base + m, :], big[:, m, :], ACT.Identity,
                                                               bias=bias[:, col + m:col + m + 1])
                            ins.then_inc(S["proj_hi"], 1)
                        elif kind == "X":
                            split_x(act, j, n)
                            x_high(n, S["x_hi"])
                        elif kind == "N":
                            split_w(act)
                            w_high(n, S["w_hi"])
                        elif kind == "S":
                            u = 8 * j + n
                            wd = (Q_TILES[n // 2] + 1) * P
                            act.wait_ge(S["max_done"], u + 1)
                            if u >= 2:
                                act.wait_ge(S["pt_done"], u - 1)
                            for m in range(2):
                                ins = nc.scalar.activation(prob[:, n % 2, m, 0:wd], psBig[:, n % 2, m, 0:wd], ACT.Exp,
                                                           bias=negmax[:, n % 2, m:m + 1],
                                                           accum_out=rowsum[:, n // 2, n % 2, m:m + 1])
                            ins.then_inc(S["exp_done"], 1)
                        elif kind == "L":
                            u = 8 * j + n
                            act.wait_ge(S["pt_done"], u + 1)
                            if u >= 3:
                                act.wait_ge(S["pv_done"], (u - 3) // 2 + 1)
                            nc.scalar.copy(pT[0][:, u % 3, 0:Q_TILES[n // 2] + 1, :], psT[:, 0:Q_TILES[n // 2] + 1, :]) \
                                .then_inc(S["pt_hi"], 1)
                        elif kind == "PV":
                            m = 4 * j + n
                            act.wait_ge(S["pv_done"], m + 1)
                            for h in range(2):
                                if h or m:
                                    act.wait_ge(S["sq_done"], 2 * m + h)
                                nc.scalar.activation(junk[:, :], psPV[:, n % 2, h, :], ACT.Square,
                                                     accum_out=msq[:, n % 2, h:h + 1]).then_inc(S["sq_done"], 1)
                        elif kind == "R":
                            m = 4 * j + n
                            act.wait_ge(S["var_done"], m + 1)
                            nc.scalar.activation(rms[:, n % 2, :], var[:, n % 2, :], ACT.Ln).then_inc(S["ln_done"], 1)
                            act.wait_ge(S["ln_done"], m + 1)
                            nc.scalar.activation(rms[:, n % 2, :], rms[:, n % 2, :], ACT.Exp, scale=-0.5) \
                                .then_inc(S["guess_done"], 1)
                        elif kind == "H":
                            m = 4 * j + n
                            act.wait_ge(S["ot_done"], m + 1)
                            if m > 0:
                                act.wait_ge(S["out_done"], m)
                            nc.scalar.copy(hT[0][:, :, :].rearrange("p r t -> p (r t)"), psO[:, :]).then_inc(S["ot_hi"], 1)
                        elif kind == "M" and j < B:
                            k = 8 * j + n
                            state, half = divmod(k, 2)
                            if k >= 2:
                                act.wait_ge(S["scan_done"], k - 1)
                            for c in range(2):
                                ct = 2 * half + c
                                ins = nc.scalar.activation(dA[:, k % 2, c, 1:T], dt[:, ct, 1:T], ACT.Exp,
                                                           scale=s["negA"][:, ct * NS + state:ct * NS + state + 1])
                            ins.then_inc(S["dA_done"], 1)

                def drive(eng, unit, k, done):
                    state, half = divmod(k, 2)
                    eng.wait_ge(S[f"bc_loaded{state % 2}"], 32 * (state // 2 + 1))
                    if k >= 3:
                        eng.wait_ge(S["piece_done"], k - 2)
                    unit.tensor_tensor(st[:, k % 3], dtu[:, 2 * half:2 * half + 2, :],
                                       Bn[:, state % 2, :].unsqueeze(1).broadcast_to([P, 2, T]),
                                       ALU.mult).then_inc(done, 1)

                def scan_piece(dve, k):
                    dve.wait_ge(S["dA_done"], k + 1)
                    if dve_drives(k):
                        dve.wait_ge(S["dbu_dve"], sum(dve_drives(i) for i in range(k + 1)))
                    else:
                        dve.wait_ge(S["dbu_done"], sum(not dve_drives(i) for i in range(k + 1)))
                    flat = st[:, k % 3].rearrange("p c t -> p (c t)")
                    nc.vector.tensor_tensor_scan(flat, dA[:, k % 2].rearrange("p c t -> p (c t)"), flat, 0.0,
                                                 ALU.mult, ALU.add).then_inc(S["scan_done"], 1)

                @block.vector
                def _(dve):
                    def newton(i, j, n):
                        m = 4 * j + n
                        guess, v_ = rms[:, n % 2, :], var[:, n % 2, :]
                        if i == 0:
                            dve.wait_ge(S["guess_done"], m + 1)
                            ins = nc.vector.scalar_tensor_tensor(tmp[:, :], guess, -0.5, guess, ALU.mult, ALU.mult)
                        elif i == 1:
                            dve.wait_ge(S["rms_step"], 3 * m + 1)
                            ins = nc.vector.tensor_tensor(tmp[:, :], tmp[:, :], v_, ALU.mult)
                        else:
                            dve.wait_ge(S["rms_step"], 3 * m + 2)
                            ins = nc.vector.scalar_tensor_tensor(guess, tmp[:, :], 1.5, guess, ALU.add, ALU.mult)
                        ins.then_inc(S["rms_step"], 1)

                    def scale_heads(j, n):
                        m = 4 * j + n
                        dve.wait_ge(S["rms_step"], 3 * m + 3)
                        if m > 0:
                            dve.wait_ge(S["ot_done"], m)
                        for h in range(2):
                            ins = nc.vector.tensor_scalar(head[:, h, :], psPV[:, n % 2, h, :], rms[:, n % 2, h:h + 1],
                                                          None, ALU.mult)
                        ins.then_inc(S["head_done"], 1)

                    dve.wait_ge(S["b_loaded"], 48)
                    nc.vector.tensor_scalar(bias[:, 0:4], bias[:, 0:4], SCALE, None, ALU.mult) \
                        .then_inc(S["b_scaled"], 1)
                    dve.wait_ge(S["b_scaled"], 1)
                    nc.vector.tensor_scalar(subln[:, :], subln[:, :], 1.0 - LAMBDA_INIT, None, ALU.mult) \
                        .then_inc(S["ow_col"], 1)
                    for kind, j, n in in_order(slots, DVE_PROJ, DVE_UNIT):
                        if kind in ("K", "Q", "V"):
                            r = use_of(kind, n)
                            if kind == "V" and j == 0:
                                for t in range(4):
                                    dve.wait_ge(S["ow_hi"], t + 1)
                                    nc.vector.scalar_tensor_tensor(ow[1][:, t, :], wraw[:, t, 0:HID],
                                                                   subln[:, t % 2:t % 2 + 1], f32(ow[0][:, t, :]),
                                                                   ALU.mult, ALU.subtract).then_inc(S["ow_lo"], 1)
                            dve.wait_ge(S["proj_hi"], 4 * j + r + 1)
                            big = psBig[:, r % 2]
                            if kind == "V":
                                ins = nc.vector.tensor_tensor(v[1][:, :, :].rearrange("p a b -> p (a b)"),
                                                              big.rearrange("p a b -> p (a b)"),
                                                              f32(v[0][:, :, :].rearrange("p a b -> p (a b)")),
                                                              ALU.subtract)
                            else:
                                dst, col = (kT, 4) if kind == "K" else (qT, 2 * n)
                                base = 0 if kind == "K" else 2 * n
                                for m in range(2):
                                    ins = nc.vector.scalar_tensor_tensor(
                                        dst[1][:, base + m, :], big[:, m, :], bias[:, col + m:col + m + 1],
                                        f32(dst[0][:, base + m, :]), ALU.add, ALU.subtract)
                            ins.then_inc(S["proj_lo"], 1)
                        elif kind == "X":
                            split_x(dve, j, n)
                            dve.wait_ge(S["x_hi"], 2 * (j - 1) + n + 1)
                            x_low(n, S["x_lo"])
                        elif kind == "N":
                            split_w(dve)
                            dve.wait_ge(S["w_hi"], n + 1)
                            w_low(n, S["w_lo"])
                        elif kind == "S":
                            u = 8 * j + n
                            wd = (Q_TILES[n // 2] + 1) * P
                            dve.wait_ge(S["scores_done"], u + 1)
                            nc.vector.reduce_max(negmax[:, n % 2, :], psBig[:, n % 2, :, 0:wd], AX.X, negate=True) \
                                .then_inc(S["max_done"], 1)
                        elif kind == "C":
                            u = 8 * j + n
                            qt, h = divmod(n, 2)
                            wd = (Q_TILES[qt] + 1) * P
                            due = (n - 5) // 2 if n in (5, 7) else None
                            sums = rowsum[:, qt, h, :]
                            dve.wait_ge(S["exp_done"], u + 1)
                            nc.vector.reciprocal(rinv[:, n % 2:n % 2 + 1], sums[:, 1:2]).then_inc(S["comb_step"], 1)
                            if due is not None:
                                newton(0, j, due)
                            dve.wait_ge(S["comb_step"], 2 * u + 1)
                            nc.vector.scalar_tensor_tensor(coef[:, n % 2:n % 2 + 1], rinv[:, n % 2:n % 2 + 1],
                                                           s["neglam"][:, :], sums[:, 0:1],
                                                           ALU.mult, ALU.mult).then_inc(S["comb_step"], 1)
                            if due is not None:
                                newton(1, j, due)
                            dve.wait_ge(S["comb_step"], 2 * u + 2)
                            nc.vector.scalar_tensor_tensor(prob[:, n % 2, 0, 0:wd], prob[:, n % 2, 1, 0:wd],
                                                           coef[:, n % 2:n % 2 + 1], prob[:, n % 2, 0, 0:wd],
                                                           ALU.mult, ALU.add).then_inc(S["probs_done"], 1)
                            if due is not None:
                                newton(2, j, due)
                                scale_heads(j, due)
                        elif kind == "L":
                            u = 8 * j + n
                            dve.wait_ge(S["pt_hi"], u + 1)
                            nc.vector.tensor_tensor(pT[1][:, u % 3, 0:Q_TILES[n // 2] + 1, :], psT[:, 0:Q_TILES[n // 2] + 1, :],
                                                    f32(pT[0][:, u % 3, 0:Q_TILES[n // 2] + 1, :]), ALU.subtract) \
                                .then_inc(S["pt_lo"], 1)
                        elif kind == "W":
                            m = 4 * j + n
                            sums = rowsum[:, n, :, 0]
                            nc.vector.scalar_tensor_tensor(nrm[:, :], sums, EPS, sums, ALU.mult, ALU.mult) \
                                .then_inc(S["var_step"], 1)
                            dve.wait_ge(S["sq_done"], 2 * m + 2)
                            dve.wait_ge(S["var_step"], m + 1)
                            nc.vector.scalar_tensor_tensor(var[:, n % 2, :], msq[:, n % 2, :], 1.0 / E2, nrm[:, :],
                                                           ALU.mult, ALU.add).then_inc(S["var_done"], 1)
                        elif kind == "R" and n >= 2:
                            for i in range(3):
                                newton(i, j, n)
                            scale_heads(j, n)
                        elif kind == "H":
                            m = 4 * j + n
                            dve.wait_ge(S["ot_hi"], m + 1)
                            nc.vector.tensor_tensor(hT[1][:, :, :].rearrange("p r t -> p (r t)"), psO[:, :],
                                                    f32(hT[0][:, :, :].rearrange("p r t -> p (r t)")),
                                                    ALU.subtract).then_inc(S["ot_lo"], 1)
                        elif kind == "A":
                            m = 4 * j + n
                            dve.wait_ge(S["out_done"], m + 1)
                            dve.wait_ge(S[f"acc_loaded{m % 2}"], 16 * (m // 2 + 1))
                            nc.vector.tensor_tensor(acc[:, m % 2, :], psO[:, :], acc[:, m % 2, :], ALU.add) \
                                .then_inc(S["acc_done"], 1)
                        elif kind == "M":
                            k = 8 * j + n
                            if k == 0:
                                dve.wait_ge(S["u_loaded"], 16)
                                for c in range(CT):
                                    nc.vector.tensor_scalar(y[:, c, :], y[:, c, :], s["Dcol"][:, c:c + 1], None,
                                                            ALU.mult).then_inc(S["y_init"], 1)
                            if k < 2 * NS and dve_drives(k):
                                drive(dve, nc.vector, k, S["dbu_dve"])
                            if k > 0:
                                scan_piece(dve, k - 1)

                @block.gpsimd
                def _(pool):
                    drive(pool, nc.gpsimd, 0, S["dbu_done"])
                    pool.wait_ge(S["y_init"], CT)
                    for k in range(2 * NS):
                        state, half = divmod(k, 2)
                        pool.wait_ge(S["scan_done"], k + 1)
                        nc.gpsimd.tensor_tensor(st[:, k % 3], st[:, k % 3],
                                                Cn[:, state % 2, :].unsqueeze(1).broadcast_to([P, 2, T]),
                                                ALU.mult).then_inc(S["gated"], 1)
                        pool.wait_ge(S["gated"], k + 1)
                        nc.gpsimd.tensor_tensor(y[:, 2 * half:2 * half + 2, :], y[:, 2 * half:2 * half + 2, :],
                                                st[:, k % 3], ALU.add).then_inc(S["piece_done"], 1)
                        if k + 2 < 2 * NS and not dve_drives(k + 2):
                            drive(pool, nc.gpsimd, k + 2, S["dbu_done"])
            clear(nc, sems)



PREPARE = {
    3: (("x0", 0, 0),),
    4: (("x0", 0, 1),),
    6: (("x0", 0, 2), ("stats", 1, 0)),
    7: (("stats", 1, 1), ("stats", 1, 2), ("x0", 0, 3)),
    9: (("stats", 1, 3), ("var", 1, 0)),
    10: (("guess", 1, 0), ("newton", 1, 0), ("norm", 1, 0), ("norm", 1, 1)),
    11: (("norm", 1, 2), ("norm", 1, 3)),
    12: (("tanh", 0, 0), ("tanh", 0, 1), ("yx", 0, 0), ("gmul", 0, 0)),
    14: (("yx", 0, 1), ("yx", 0, 2), ("gmul", 0, 1), ("tanh", 0, 2)),
    15: (("gmul", 0, 2), ("gmul", 0, 3), ("yx", 0, 3), ("tanh", 0, 3)),
    19: (("turn", 0, 0), ("stats", 2, 0)),
    20: (("turn", 0, 1), ("stats", 2, 1)),
    21: (("turn", 0, 2),),
    22: (("turn", 0, 3), ("stats", 2, 2), ("stats", 2, 3), ("var", 2, 0)),
    24: (("guess", 2, 0), ("newton", 2, 0), ("norm", 2, 0), ("norm", 2, 1)),
    25: (("norm", 2, 2), ("norm", 2, 3)),
    28: (("x2T", 0, 0),),
    29: (("x2T", 0, 1),),
    30: (("x2T", 0, 2),),
    31: (("x2T", 0, 3),),
    33: (("gate", 0, 0),),
    34: (("gate", 0, 1),),
}
PSUM_KINDS = ("turn", "x2T", "gate")
UNITS = [("s", 0, t) for t in range(2)] + [("e", e, t) for e in range(NE) for t in range(2)]
NU = len(UNITS)
LAG = 3


def expert_phase(nc, d, s):
    with ExitStack() as ctx:
        def sb(name, shape, dt=F32):
            return ctx.enter_context(nc.sbuf_tensor(name, shape, dt))

        def pair(name, shape):
            return sb(name + "_hi", shape, F32R), sb(name + "_lo", shape, F32R)

        def ps(name, shape):
            return ctx.enter_context(nc.psum_tensor(name, shape, F32))

        def f32(ap):
            return ap.bitcast(F32)

        cw = pair("cw", [P, WCOLS])
        x1 = sb("x1", [P, TT, HID])
        x3 = sb("x3", [P, TT, HID])
        yg = sb("yg", [P, CT, T])
        gate = sb("gate", [P, 2, HID])
        outb = sb("outb", [P, HID])
        rbias = sb("rbias", [P, NE])
        x2T = pair("x2T", [P, KT, T])
        xl = pair("xl", [P, T])
        lat = xl
        wb = sb("wb", [P, 3, T])
        act_ = sb("act_buf", [P, 3, T])
        hid = pair("hid", [P, 3, T])
        stats = sb("stats", [P, TT, 6])
        mv = sb("mv", [P, TT, 2])
        var = sb("mvar", [P, TT])
        rstd = sb("rstd", [P, TT])
        tmp = sb("mtmp", [P, TT])
        ex = sb("ex", [P, TT, NE])
        prb = sb("prb", [P, TT, NE])
        sel = sb("sel", [P, TT, NE])
        top = sb("top", [P, TT, 8])
        wsum = sb("wsum", [P, TT])
        logits = gate[0:NE, 1, :]
        wT = gate[0:NE, 0, :]
        psGU = ps("psGU", [P, 3, 2, T])
        psA = ps("psA", [P, T])
        psM = ps("psM", [P, T])

        c_load = ctx.enter_context(nc.semaphore("rows_loaded"))
        CH = 2 * T
        chunks = [(c, min(c + CH, WCOLS)) for c in range(0, WCOLS, CH)]
        LATE = 4
        late = chunks[-LATE:]
        chunks = chunks[:-LATE]
        late_loaded = [ctx.enter_context(nc.semaphore(f"late_loaded{n}")) for n in range(2)]
        late_hi = ctx.enter_context(nc.semaphore("late_hi"))
        late_lo = ctx.enter_context(nc.semaphore("late_lo"))
        stage = (x3[:, 0:2, :], x3[:, 2:4, :], act_[:, 0:2, :])
        NST = len(stage)
        w_load = [ctx.enter_context(nc.semaphore(f"cw_loaded{n}")) for n in range(NST)]
        w_hi = ctx.enter_context(nc.semaphore("cw_hi"))
        w_lo = ctx.enter_context(nc.semaphore("cw_lo"))

        names = ("acc_loaded0", "acc_loaded1", "y_loaded", "x0_done", "stat_step", "var_done", "ln_done", "guess_done", "norm_done",
                 "yx_done", "tanh_done", "yg_done", "ygT_done", "x2_added", "x2_done", "x2T_done", "x2T_hi", "x2T_lo",
                 "logits_ps", "logits_sb", "logits_done", "rexp_done", "route_step", "route_done", "wT_ps", "wT_sb", "wT_stored",
                 "wb_loaded0", "wb_loaded1", "wb_loaded2", "xl_done", "xl_hi", "xl_lo", "up_done", "relu_done",
                 "square_done", "weighted", "prod_done", "hid_hi", "hid_lo", "shared_ps", "shared_added", "down_done",
                 "lat_hi", "lat_lo", "out_ps", "x3_done", "out_done", "stored")
        sems = [ctx.enter_context(nc.semaphore(n)) for n in names]
        S = dict(zip(names, sems))

        def staged(n):
            a, z = chunks[n]
            return stage[n % NST].rearrange("p a b -> p (a b)")[:, 0:z - a]

        def late_stage(n):
            a, z = late[n]
            return yg[:, 2 * (n % 2):2 * (n % 2) + 2, :].rearrange("p a b -> p (a b)")[:, 0:z - a]

        def load_late(sp, n):
            if n >= 2:
                sp.wait_ge(late_lo, n - 1)
            sp.dma_start(late_stage(n), d["cw"][:, late[n][0]:late[n][1]]).then_inc(late_loaded[n % 2], 16)

        def late_high(act, n):
            act.wait_ge(late_loaded[n % 2], 16 * (n // 2 + 1))
            nc.scalar.copy(cw[0][:, late[n][0]:late[n][1]], late_stage(n)).then_inc(late_hi, 1)

        def late_low(pool, n):
            a, z = late[n]
            pool.wait_ge(late_hi, n + 1)
            nc.gpsimd.tensor_tensor(cw[1][:, a:z], late_stage(n), f32(cw[0][:, a:z]), ALU.subtract).then_inc(late_lo, 1)


        def load_x(sp, b, h):
            sp.dma_start(x1[:, 2 * h:2 * h + 2, :],
                         d["acc"].rearrange("(b t p) n -> b p t n", b=B, p=P)[bass.ds(b, 1), :, 2 * h:2 * h + 2, :]
                         .rearrange("b p t n -> p (b t) n")).then_inc(S[f"acc_loaded{h}"], 16)

        def load_y(sp, b):
            sp.dma_start(yg[:, :, :].rearrange("p c t -> p (c t)"),
                         d["y"][bass.ds(b, 1), :, :].rearrange("b p n -> p (b n)")).then_inc(S["y_loaded"], 16)

        def three(out, lhs, rhs, at_l, at_r, start, stop):
            nc.tensor.matmul(out, at_l(lhs[0]), at_r(rhs[0]), start=start, stop=False)
            nc.tensor.matmul(out, at_l(lhs[0]), at_r(rhs[1]), start=False, stop=False)
            return nc.tensor.matmul(out, at_l(lhs[1]), at_r(rhs[0]), start=False, stop=stop)

        def prepare_pe(pe, kind, i, n):
            if kind == "turn":
                if n == 0:
                    pe.wait_ge(S["yg_done"], CT)
                else:
                    pe.wait_ge(S["x2_added"], n)
                for c in range(CT):
                    mm = nc.tensor.transpose(psM[:, c * P:(c + 1) * P], yg[:, c, n * P:(n + 1) * P], s["ident"][:, :])
                mm.then_inc(S["ygT_done"], 1)
            elif kind == "x2T":
                if n == 0:
                    pe.wait_ge(S["x2_done"], TT)
                else:
                    pe.wait_ge(S["x2T_hi"], n)
                    pe.wait_ge(S["x2T_lo"], n)
                for t in range(TT):
                    mm = nc.tensor.transpose(psM[:, t * P:(t + 1) * P], x1[:, t, n * P:(n + 1) * P], s["ident"][:, :])
                mm.then_inc(S["x2T_done"], 1)
            elif kind == "gate" and n == 0:
                pe.wait_ge(S["x2T_hi"], KT)
                pe.wait_ge(S["x2T_lo"], KT)
                for k in range(KT):
                    mm = three(psM[0:NE, :], cw, x2T, lambda a: a[:, WGT + k * NE:WGT + (k + 1) * NE],
                               lambda a: a[:, k, :], k == 0, k == KT - 1)
                mm.then_inc(S["logits_ps"], 1)
            elif kind == "gate":
                pe.wait_ge(S["logits_sb"], 1)
                for t in range(TT):
                    mm = nc.tensor.transpose(psM[:, t * NE:(t + 1) * NE], logits[:, t * P:(t + 1) * P],
                                             s["ident"][0:NE, 0:NE])
                mm.then_inc(S["logits_done"], 1)

        def guess(act, i):
            act.wait_ge(S["var_done"], i)
            nc.scalar.activation(rstd[:, :], var[:, :], ACT.Ln).then_inc(S["ln_done"], 1)
            act.wait_ge(S["ln_done"], i)
            nc.scalar.activation(rstd[:, :], rstd[:, :], ACT.Exp, scale=-0.5).then_inc(S["guess_done"], 1)

        def prepare_act(act, kind, i, n, before=0):
            if kind == "guess":
                guess(act, before + i)
            elif kind == "tanh":
                act.wait_ge(S["norm_done"], n + 1)
                if n >= 2:
                    act.wait_ge(S["yg_done"], n - 1)
                nc.scalar.activation(gate[:, n % 2, :], x1[:, n, :], ACT.Tanh, scale=0.5).then_inc(S["tanh_done"], 1)
                if n == CT - 1:
                    nc.scalar.preload_act_table_set("natural_log_exp_and_others")
            elif kind == "x2T":
                act.wait_ge(S["x2T_done"], n + 1)
                nc.scalar.copy(x2T[0][:, n, :], psM[:, :]).then_inc(S["x2T_hi"], 1)
            elif kind == "gate" and n == 0:
                act.wait_ge(S["logits_ps"], 1)
                nc.scalar.copy(logits, psM[0:NE, :]).then_inc(S["logits_sb"], 1)
            elif kind == "gate":
                act.wait_ge(S["logits_done"], 1)
                nc.scalar.activation(ex[:, :, :].rearrange("p a b -> p (a b)"), psM[:, 0:TT * NE], ACT.Exp,
                                     scale=-1.0).then_inc(S["rexp_done"], 1)

        def tile_stats(dve, step, x, t, ready):
            dve.wait_ge(ready, t + 1)
            step(nc.vector.bn_stats(stats[:, t, :], x[:, t, :]))
            step(nc.vector.bn_aggr(mv[:, t, :], stats[:, t, :]))

        def variance(dve):
            nc.vector.tensor_scalar(var[:, :], mv[:, :, 1], EPS, None, ALU.add).then_inc(S["var_done"], 1)

        def refine(dve, step, i):
            dve.wait_ge(S["guess_done"], i)
            rsqrt_newton(nc.vector, step, rstd[:, :], var[:, :], tmp[:, :])

        def normalise(x, t, done):
            nc.vector.tensor_scalar(x[:, t, :], x[:, t, :], mv[:, t, 0:1], rstd[:, t:t + 1],
                                    ALU.subtract, ALU.mult).then_inc(done, 1)

        def prepare_dve(dve, step, kind, i, n, before=0):
            if kind == "stats":
                tile_stats(dve, step, x1, n, S["x0_done" if i == 1 else "x2_added"])
            elif kind == "var":
                variance(dve)
            elif kind == "newton":
                refine(dve, step, before + i)
            elif kind == "norm":
                normalise(x1, n, S["norm_done" if i == 1 else "x2_done"])
            elif kind == "gmul":
                dve.wait_ge(S["tanh_done"], n + 1)
                dve.wait_ge(S["yx_done"], n + 1)
                nc.vector.scalar_tensor_tensor(yg[:, n, :], gate[:, n % 2, :], 1.0, yg[:, n, :], ALU.add, ALU.mult) \
                    .then_inc(S["yg_done"], 1)
            elif kind == "turn":
                dve.wait_ge(S["ygT_done"], n + 1)
                nc.vector.scalar_tensor_tensor(x1[:, n, :], psM[:, :], 0.5, x1[:, n, :], ALU.mult, ALU.add) \
                    .then_inc(S["x2_added"], 1)
            elif kind == "x2T":
                dve.wait_ge(S["x2T_hi"], n + 1)
                nc.vector.tensor_tensor(x2T[1][:, n, :], psM[:, :], f32(x2T[0][:, n, :]), ALU.subtract) \
                    .then_inc(S["x2T_lo"], 1)

        def prepare_pool(pool, kind, i, n):
            if kind == "x0":
                pool.wait_ge(S[f"acc_loaded{n // 2}"], 16)
                nc.gpsimd.tensor_tensor(x1[:, n, :], x1[:, n, :], outb[:, :], ALU.add).then_inc(S["x0_done"], 1)
            elif kind == "yx":
                pool.wait_ge(S["y_loaded"], 16)
                pool.wait_ge(S["norm_done"], n + 1)
                nc.gpsimd.tensor_tensor(yg[:, n, :], yg[:, n, :], x1[:, n, :], ALU.mult).then_inc(S["yx_done"], 1)

        pieces = [p for n in sorted(PREPARE) for p in PREPARE[n]]

        with nc.Block() as block:
            @block.sync
            def _(sp):
                sp.dma_start(outb[:, :], d["out_b"].broadcast_to([P, HID])).then_inc(c_load, 16)
                sp.dma_start(rbias[:, :], d["route_b"].broadcast_to([P, NE])).then_inc(c_load, 16)
                load_x(sp, 0, 0)
                load_x(sp, 0, 1)
                load_y(sp, 0)
                for n, (a, z) in enumerate(chunks):
                    if n >= NST:
                        sp.wait_ge(w_lo, n - NST + 1)
                    sp.dma_start(staged(n), d["cw"][:, a:z]).then_inc(w_load[n % NST], 16)

            @block.tensor
            def _(pe):
                pe.wait_ge(w_hi, 1)
                pe.wait_ge(w_lo, 1)
                for piece in pieces:
                    prepare_pe(pe, *piece)

            @block.scalar
            def _(act):
                nc.scalar.preload_act_table_set("natural_log_exp_and_others")
                PAUSE = 8
                mine = [p for p in pieces if p[0] in ("guess", "tanh", "x2T", "gate")]
                for n, (a, z) in enumerate(chunks):
                    if n < 5 or n >= PAUSE:
                        for piece in mine[n if n < 5 else n - PAUSE + 5:][:1]:
                            prepare_act(act, *piece)
                    act.wait_ge(w_load[n % NST], 16 * (n // NST + 1))
                    nc.scalar.copy(cw[0][:, a:z], staged(n)).then_inc(w_hi, 1)
                for piece in mine[len(chunks) - PAUSE + 5:]:
                    prepare_act(act, *piece)

            @block.gpsimd
            def _(pool):
                pool.wait_ge(c_load, 32)
                for n in range(TT):
                    prepare_pool(pool, "x0", 0, n)
                for n, (a, z) in enumerate(chunks):
                    if n < CT:
                        prepare_pool(pool, "yx", 0, n)
                    pool.wait_ge(w_hi, n + 1)
                    nc.gpsimd.tensor_tensor(cw[1][:, a:z], staged(n), f32(cw[0][:, a:z]), ALU.subtract) \
                        .then_inc(w_lo, 1)

            @block.vector
            def _(dve):
                step = chained(dve, S["stat_step"])
                for piece in pieces:
                    prepare_dve(dve, step, *piece)
        clear(nc, sems)

        def store_out(sp, b):
            for t in range(TT):
                sp.wait_ge(S["out_done"], t + 1)
                sp.dma_start(d["out"].rearrange("(b t p) n -> b t p n", b=B, p=P)[bass.ds(b, 1), t]
                             .rearrange("b p n -> (b p) n"), x3[:, t, :]).then_inc(S["stored"], 16)

        def last_norm(dve, step):
            for t in range(TT):
                step(nc.vector.bn_stats(stats[:, t, :], x3[:, t, :]))
                step(nc.vector.bn_aggr(mv[:, t, :], stats[:, t, :]))
            variance(dve)
            refine(dve, step, 1)
            for t in range(TT):
                normalise(x3, t, S["out_done"])

        def experts(b, finish):
            before = 1 if finish else 0
            with nc.Block(no_gpsimd_drain=True) as block:
                @block.sync
                def _(sp):
                    if finish:
                        load_y(sp, (b + 1) & (B - 1))
                    else:
                        load_late(sp, 0)
                        load_late(sp, 1)
                    sp.wait_ge(S["wT_sb"], 1)
                    sp.dma_start(d["wT"], wT).then_inc(S["wT_stored"], 16)
                    sp.wait_ge(S["wT_stored"], 16)
                    for e in range(NE):
                        if e >= 3:
                            sp.wait_ge(S["weighted"], 2 * (e - 2))
                        sp.dma_start(wb[:, e % 3, :], d["wT"][e:e + 1, :].broadcast_to([P, T])) \
                            .then_inc(S[f"wb_loaded{e % 3}"], 16)
                        if e == 2 and finish:
                            store_out(sp, b - 1)
                        elif e == 2:
                            for n in range(2, LATE):
                                load_late(sp, n)
                            sp.wait_ge(late_lo, LATE)
                            load_y(sp, (b + 1) & (B - 1))
                        if e == 2:
                            for h in range(2):
                                sp.wait_ge(S["shared_added"], 2 * h + 2)
                                load_x(sp, (b + 1) & (B - 1), h)

                @block.tensor
                def _(pe):
                    def up(n):
                        kind, e, t = UNITS[n]
                        if n >= 3:
                            pe.wait_ge(S["prod_done"], n - 2)
                        if kind == "s":
                            for gu, w0 in ((0, SWG), (1, SW1)):
                                for k in range(KT):
                                    mm = three(psGU[:, n % 3, gu, :], cw, x2T,
                                               lambda a: a[:, w0 + k * 256 + t * P:w0 + k * 256 + (t + 1) * P],
                                               lambda a: a[:, k, :], k == 0, k == KT - 1)
                        else:
                            for gu, w0 in ((0, RWG), (1, RW1)):
                                mm = three(psGU[:, n % 3, gu, :], cw, xl,
                                           lambda a: a[:, w0 + e * 256 + t * P:w0 + e * 256 + (t + 1) * P],
                                           lambda a: a[:, :], True, True)
                        mm.then_inc(S["up_done"], 1)

                    def shared_down():
                        pe.wait_ge(S["hid_hi"], 2)
                        pe.wait_ge(S["hid_lo"], 2)
                        for t in range(TT):
                            if t >= 2:
                                pe.wait_ge(S["shared_added"], t - 1)
                            for h in range(2):
                                mm = three((psM, psA)[t % 2][:, :], hid, cw, lambda a: a[:, h, t * P:(t + 1) * P],
                                           lambda a: a[:, SW2 + h * HID:SW2 + (h + 1) * HID], h == 0, h == 1)
                            mm.then_inc(S["shared_ps"], 1)

                    first_late = 2 + (late[0][0] - RW2) // LAT

                    def down(n):
                        _, e, t = UNITS[n]
                        pe.wait_ge(S["hid_hi"], n + 1)
                        pe.wait_ge(S["hid_lo"], n + 1)
                        if n == 2:
                            pe.wait_ge(S["shared_added"], TT)
                        if not finish and n == first_late:
                            pe.wait_ge(late_lo, LATE)
                        mm = three(psA[:, :], cw, hid,
                                   lambda a: a[:, RW2 + (2 * e + t) * LAT:RW2 + (2 * e + t + 1) * LAT],
                                   lambda a: a[:, n % 3, :], n == 2, n == NU - 1)
                        mm.then_inc(S["down_done"], 1)

                    for n in range(NU):
                        if n == 2:
                            pe.wait_ge(S["wT_sb"], 1)
                            for k in range(KT):
                                mm = three(psM[:, :], cw, x2T, lambda a: a[:, WDN + k * LAT:WDN + (k + 1) * LAT],
                                           lambda a: a[:, k, :], k == 0, k == KT - 1)
                            mm.then_inc(S["xl_done"], 1)
                            pe.wait_ge(S["xl_hi"], 1)
                            pe.wait_ge(S["xl_lo"], 1)
                        up(n)
                        if n == 0:
                            pe.wait_ge(S["route_done"], 1)
                            for t in range(TT):
                                mm = nc.tensor.transpose(psM[0:NE, t * P:(t + 1) * P], sel[:, t, :], s["ident"][:, :])
                            mm.then_inc(S["wT_ps"], 1)
                        elif n == 3:
                            shared_down()
                        for piece in PREPARE.get(n, ()):
                            prepare_pe(pe, *piece)
                        if n - LAG >= 2:
                            down(n - LAG)
                    down(NU - LAG)
                    for piece in PREPARE.get(NU, ()):
                        prepare_pe(pe, *piece)
                    for n in range(NU - LAG + 1, NU):
                        down(n)
                    pe.wait_ge(S["lat_hi"], 1)
                    pe.wait_ge(S["lat_lo"], 1)
                    for t in range(TT):
                        mm = three(psGU[:, t // 2, t % 2, :], lat, cw, lambda a: a[:, t * P:(t + 1) * P],
                                   lambda a: a[:, WUP:WUP + HID], True, True)
                        mm.then_inc(S["out_ps"], 1)

                @block.scalar
                def _(act):
                    def relu_square(n):
                        act.wait_ge(S["up_done"], n + 1)
                        if n >= 3:
                            act.wait_ge(S["hid_lo"], n - 2)
                        nc.scalar.activation(act_[:, n % 3, :], psGU[:, n % 3, 0, :], ACT.Relu) \
                            .then_inc(S["relu_done"], 1)
                        act.wait_ge(S["relu_done"], n + 1)
                        nc.scalar.activation(act_[:, n % 3, :], act_[:, n % 3, :], ACT.Square) \
                            .then_inc(S["square_done"], 1)

                    def high(n):
                        act.wait_ge(S["prod_done"], n + 1)
                        if n == 3:
                            act.wait_ge(S["shared_ps"], TT)
                        elif n >= 5:
                            act.wait_ge(S["down_done"], n - 4)
                        nc.scalar.copy(hid[0][:, n % 3, :], act_[:, n % 3, :]).then_inc(S["hid_hi"], 1)

                    nc.scalar.preload_act_table_set("natural_log_exp_and_others")
                    for n in range(NU):
                        if n == 2:
                            act.wait_ge(S["xl_done"], 1)
                            nc.scalar.copy(xl[0][:, :], psM[:, :]).then_inc(S["xl_hi"], 1)
                        relu_square(n)
                        for piece in PREPARE.get(n, ()):
                            if piece[0] in PSUM_KINDS:
                                prepare_act(act, *piece, before)
                        if n == 0:
                            act.wait_ge(S["wT_ps"], 1)
                            nc.scalar.copy(wT, psM[0:NE, :]).then_inc(S["wT_sb"], 1)
                            if finish:
                                guess(act, 1)
                            else:
                                late_high(act, 0)
                        else:
                            high(n - 1)
                        if 1 <= n < LATE and not finish:
                            late_high(act, n)
                        for piece in PREPARE.get(n, ()):
                            if piece[0] not in PSUM_KINDS:
                                prepare_act(act, *piece, before)
                    high(NU - 1)
                    for piece in PREPARE.get(NU, ()):
                        prepare_act(act, *piece, before)
                    act.wait_ge(S["down_done"], NU - 2)
                    nc.scalar.copy(lat[0][:, :], psA[:, :]).then_inc(S["lat_hi"], 1)

                @block.gpsimd
                def _(pool):
                    if not finish:
                        for n in range(2):
                            late_low(pool, n)
                    for n in range(2, NU):
                        _, e, t = UNITS[n]
                        pool.wait_ge(S["square_done"], n + 1)
                        pool.wait_ge(S[f"wb_loaded{e % 3}"], 16 * (e // 3 + 1))
                        nc.gpsimd.tensor_tensor(act_[:, n % 3, :], act_[:, n % 3, :], wb[:, e % 3, :], ALU.mult) \
                            .then_inc(S["weighted"], 1)
                        if n < LATE and not finish:
                            late_low(pool, n)
                        for piece in PREPARE.get(n, ()):
                            prepare_pool(pool, *piece)

                @block.vector
                def _(dve):
                    sstep = chained(dve, S["stat_step"])
                    rstep = chained(dve, S["route_step"])

                    rstep(nc.vector.tensor_scalar(ex[:, :, :], ex[:, :, :], 1.0, None, ALU.add))
                    rstep(nc.vector.reciprocal(prb[:, :, :], ex[:, :, :]))
                    rstep(nc.vector.tensor_tensor(ex[:, :, :], prb[:, :, :],
                                                  rbias[:, :].unsqueeze(1).broadcast_to([P, TT, NE]), ALU.add))
                    for t in range(TT):
                        rstep(nc.vector.max(top[:, t, :], ex[:, t, :]))
                        rstep(nc.vector.match_replace(out=sel[:, t, :], in_to_replace=top[:, t, :],
                                                      in_values=ex[:, t, :], imm_value=-3e38))
                    rstep(nc.vector.scalar_tensor_tensor(sel[:, :, :], sel[:, :, :], -3e38, prb[:, :, :],
                                                         ALU.is_equal, ALU.mult))
                    rstep(nc.vector.reduce_sum(wsum[:, :], sel[:, :, :], AX.X))
                    rstep(nc.vector.reciprocal(wsum[:, :], wsum[:, :]))
                    rstep(nc.vector.tensor_scalar(wsum[:, :], wsum[:, :], ROUTE_SCALE, None, ALU.mult))
                    nc.vector.tensor_tensor(sel[:, :, :], sel[:, :, :],
                                            wsum[:, :].unsqueeze(2).broadcast_to([P, TT, NE]), ALU.mult) \
                        .then_inc(S["route_done"], 1)

                    if finish:
                        last_norm(dve, sstep)

                    def low(n):
                        dve.wait_ge(S["hid_hi"], n + 1)
                        nc.vector.tensor_tensor(hid[1][:, n % 3, :], act_[:, n % 3, :], f32(hid[0][:, n % 3, :]),
                                                ALU.subtract).then_inc(S["hid_lo"], 1)

                    for n in range(NU):
                        if n == 2:
                            dve.wait_ge(S["xl_hi"], 1)
                            nc.vector.tensor_tensor(xl[1][:, :], psM[:, :], f32(xl[0][:, :]), ALU.subtract) \
                                .then_inc(S["xl_lo"], 1)
                        for piece in PREPARE.get(n, ()):
                            if piece[0] in PSUM_KINDS:
                                prepare_dve(dve, sstep, *piece, before)
                        if n < 2:
                            dve.wait_ge(S["square_done"], n + 1)
                        else:
                            dve.wait_ge(S["weighted"], n - 1)
                        a = act_[:, n % 3, :]
                        nc.vector.tensor_tensor(a, psGU[:, n % 3, 1, :], a, ALU.mult).then_inc(S["prod_done"], 1)
                        if n >= 1:
                            low(n - 1)
                        if n == 3:
                            if finish:
                                dve.wait_ge(S["stored"], 16 * TT)
                            for t in range(TT):
                                dve.wait_ge(S["shared_ps"], t + 1)
                                nc.vector.tensor_tensor(x3[:, t, :], (psM, psA)[t % 2][:, :], x1[:, t, :], ALU.add) \
                                    .then_inc(S["shared_added"], 1)
                        for piece in PREPARE.get(n, ()):
                            if piece[0] not in PSUM_KINDS:
                                prepare_dve(dve, sstep, *piece, before)
                    low(NU - 1)
                    dve.wait_ge(S["lat_hi"], 1)
                    nc.vector.tensor_tensor(lat[1][:, :], psA[:, :], f32(lat[0][:, :]), ALU.subtract) \
                        .then_inc(S["lat_lo"], 1)
                    for t in range(TT):
                        dve.wait_ge(S["out_ps"], t + 1)
                        nc.vector.tensor_tensor(x3[:, t, :], psGU[:, t // 2, t % 2, :], x3[:, t, :], ALU.add) \
                            .then_inc(S["x3_done"], 1)
            clear(nc, sems)

        experts(0, False)
        with nc.Fori(0, B - 1) as b:
            experts(b + 1, True)
        with nc.Block() as block:
            @block.sync
            def _(sp):
                store_out(sp, B - 1)
                sp.wait_ge(S["stored"], 16 * TT)

            @block.scalar
            def _(act):
                guess(act, 1)

            @block.vector
            def _(dve):
                last_norm(dve, chained(dve, S["stat_step"]))


def layer(nc, d):
    with ExitStack() as ctx:
        def sb(name, shape, dt=F32):
            return ctx.enter_context(nc.sbuf_tensor(name, shape, dt))

        s = {
            "ident": sb("ident", [P, P]), "identb": sb("identb", [P, P], BF16), "maskb": sb("maskb", [P, P], BF16),
            "ones": sb("ones", [1, P]), "neglam": sb("neglam", [P, 1]), "negA": sb("negA", [P, CT * NS]),
            "Dcol": sb("Dcol", [P, CT]), "two": sb("two", [P, 1]),
        }
        copied = ctx.enter_context(nc.semaphore("residual_copied"))
        setup(nc, d, s)
        scan_inputs(nc, d, s, copied)
        attend_and_scan(nc, d, s, copied)
        expert_phase(nc, d, s)


def lay_out(inputs):
    import numpy as np

    def rows(a, n):
        return a.reshape(n, P, -1).transpose(1, 0, 2)

    x = np.asarray(inputs["x"])
    wqkv = np.asarray(inputs["L0_attn_Wqkv_w"])
    bqkv = np.asarray(inputs["L0_attn_Wqkv_b"])
    NQ, NK = G * QC, G * KC
    ws, qkb, vb = [], [], []
    for g in range(G):
        idx = np.r_[g * QC:(g + 1) * QC, NQ + g * KC:NQ + (g + 1) * KC, NQ + NK + g * VC:NQ + NK + (g + 1) * VC]
        ws.append(rows(wqkv[idx].T, KT).reshape(P, -1))
        qkb.append(bqkv[idx[:QC + KC]].reshape(6, P).T)
        vb.append(bqkv[idx[QC + KC:]])
    ow = np.asarray(inputs["L0_attn_out_w"]).T
    i = {k: np.asarray(v) for k, v in inputs.items()}
    lam = np.stack([i["L0_attn_lambda_" + n] for n in ("q1", "k1", "q2", "k2")])
    scan_cols = np.concatenate([rows(i["L0_xattn_conv_w"].reshape(CT * P, TAPS), CT),
                                rows(i["L0_xattn_conv_b"][:, None], CT), rows(i["L0_xattn_dt_proj_b"][:, None], CT)], axis=2)

    def flat(a, n):
        return rows(a, n).reshape(P, -1)

    rw1 = i["L0_ffn_rw1"].transpose(2, 0, 1).reshape(LAT, -1)
    rwg = i["L0_ffn_rwg"].transpose(2, 0, 1).reshape(LAT, -1)
    rw2 = i["L0_ffn_rw2"].transpose(0, 2, 1).reshape(NE * 2, P, LAT).transpose(1, 0, 2).reshape(P, -1)
    cw = np.concatenate([flat(i["L0_ffn_Wg"].T, KT), flat(i["L0_ffn_sw1"].T, KT), flat(i["L0_ffn_swg"].T, KT), flat(i["L0_ffn_sw2"].T, 2),
                         flat(i["L0_ffn_Wdown"].T, KT), i["L0_ffn_Wup"].T,
                         rw1, rwg, rw2], axis=1)
    return {
        "x": x.reshape(B * T, HID),
        "xT": x.transpose(0, 2, 1).reshape(B, KT, P, T),
        "w": np.stack(ws), "qk_bias": np.stack(qkb), "v_bias": np.stack(vb),
        "ow": np.stack([rows(ow[g * 512:(g + 1) * 512], 4).reshape(P, -1) for g in range(G)]),
        "subln": i["L0_attn_subln_w"].reshape(2, P).T,
        "lam": lam, "out_b": i["L0_attn_out_b"][None, :],
        "ctxT": i["ctx_1024"].transpose(0, 2, 1).reshape(B, 2, P, T),
        "inT": i["L0_xattn_in_proj_w"].T, "xpT": i["L0_xattn_x_proj_w"].T, "dtT": i["L0_xattn_dt_proj_w"].T,
        "scan_cols": scan_cols,
        "alog": flat(i["L0_xattn_A_log"], CT), "Dcol": i["L0_xattn_D"].reshape(CT, P).T,
        "cw": cw, "route_b": i["L0_ffn_biases"][None, :],
    }


SCRATCH = {"acc": (B * T, HID), "u": (B, P, CT * T), "dt": (B, P, CT * T), "dtu": (B, P, CT * T),
           "bc": (B, 2 * NS, T), "y": (B, P, CT * T), "wT": (NE, T)}


def kernel(**inputs):
    import numpy as np
    import concourse.bacc as bacc
    from concourse.bass_utils import run_bass_kernel_spmd as run

    nc = bacc.Bacc("TRN2", target_bir_lowering=False, num_devices=1)
    arrays, d = {}, {}
    for name, a in lay_out(inputs).items():
        a = np.ascontiguousarray(a)
        arrays[f"in_{name}"] = a
        d[name] = nc.dram_tensor(f"in_{name}", a.shape, mybir.dt.from_np(a.dtype), kind="ExternalInput").ap()
    for name, shape in SCRATCH.items():
        d[name] = nc.dram_tensor(f"scratch_{name}", shape, F32, kind="Internal").ap()
    d["out"] = nc.dram_tensor("out", (B * T, HID), F32, kind="ExternalOutput").ap()
    layer(nc, d)
    r = run(nc, [arrays], core_ids=[0])
    return r.results[0]["out"].reshape(B, T, HID)
```
